# Optimizing a Trainium2 kernel written in Bass

```python
import numpy as np
import jax
import jax.numpy as jnp

def _softmax(x, axis=-1):
    return jax.nn.softmax(x, axis=axis)

def _gelu(x):
    return jax.nn.gelu(x, approximate=True)

def _silu(x):
    return jax.nn.silu(x)

def _sigmoid(x):
    return jax.nn.sigmoid(x)

def _layernorm(x, axis=-1, eps=1e-05):
    m = jnp.mean(x, axis=axis, keepdims=True)
    v = jnp.var(x, axis=axis, keepdims=True)
    return (x - m) / jnp.sqrt(v + eps)

def _scatter_add(tgt, idx, src, axis=0):
    return tgt.at[idx].add(src)

def _segment_sum(src, seg, n):
    return jax.ops.segment_sum(src, seg, n)
kernel_name = 'mk_gnn_resnorm_d4_gnn_r32_e9d445'

def setup_inputs(seed: int=0):
    np.random.seed(seed)
    _w = jnp.asarray

    def _rec_inputs():
        import jax
        import jax.numpy as jnp
        _gk = jax.random.key(seed)
        x = -0.000202 + 1 * jax.random.normal(jax.random.fold_in(_gk, 1), (50000, 128), jnp.float32)
        src = jax.random.randint(jax.random.fold_in(_gk, 2), (25000,), 0, 50000, jnp.int32)
        dst = jnp.minimum((50000 * jax.random.uniform(jax.random.fold_in(_gk, 3), (25000,)) ** 2.0).astype(jnp.int32), 49999)
        _o = jnp.argsort(dst, stable=True)
        src = src[_o]
        dst = dst[_o]
        edge_attr_64 = 0.000167468 + 1.0002 * jax.random.normal(jax.random.fold_in(_gk, 12), (25000, 64), jnp.float32)
        edge_weight = jax.random.uniform(jax.random.fold_in(_gk, 14), (25000,), jnp.float32, 0.0, 1)
        return (x, src, dst, edge_attr_64, edge_weight)
    x, src, dst, edge_attr_64, edge_weight = _rec_inputs()

    def _L0_gnn_setup():
        import jax, jax.numpy as jnp
        import numpy as np
        N = 50000
        DEG = 16
        E = N * DEG
        IN_FEATS = 128
        HEADS = 8
        OUT_FEATS = 16
        key = jax.random.key(seed)
        k1, k2, k3, k4, k5, k6 = jax.random.split(key, 6)
        h = jax.random.normal(k1, (N, IN_FEATS), dtype=jnp.float32)
        edge_weight = jax.random.uniform(k2, (E,), dtype=jnp.float32)
        src = jax.random.randint(k3, (E,), 0, N, dtype=jnp.int32)
        dst = jnp.repeat(jnp.arange(N, dtype=jnp.int32), DEG)
        W_fc = jax.random.normal(k4, (HEADS * OUT_FEATS, IN_FEATS), dtype=jnp.float32) * (1.0 / np.sqrt(IN_FEATS))
        w_attn = jax.random.normal(k5, (OUT_FEATS,), dtype=jnp.float32) * (1.0 / np.sqrt(OUT_FEATS))
        bias = jax.random.normal(k6, (HEADS * OUT_FEATS,), dtype=jnp.float32) * 0.02
        return {'h': h, 'edge_weight': edge_weight, 'src': src, 'dst': dst, 'W_fc': W_fc, 'w_attn': w_attn, 'bias': bias}
    _L0_gnn_all = _L0_gnn_setup()
    _L0_gnn_in = {k: v for k, v in _L0_gnn_all.items() if k in ('W_fc', 'w_attn', 'bias')}
    del _L0_gnn_all

    def _L1_gnn_setup():
        import jax, jax.numpy as jnp
        import numpy as np
        N_NODES = 50000
        N_EDGES = 25000
        IN_DIM = 128
        OUT_DIM = 128
        NUM_HEADS = 8
        HEAD_DIM = OUT_DIM // NUM_HEADS
        LN_EPS = 1e-05
        key = jax.random.key(seed)
        ks = jax.random.split(key, 8)

        def xavier(k, shape, fan_in, fan_out):
            a = float(np.sqrt(6.0 / (fan_in + fan_out)))
            return jax.random.uniform(k, shape, jnp.float32, -a, a)
        x = jax.random.normal(ks[0], (N_NODES, IN_DIM), jnp.float32)
        edge_index = jax.random.randint(ks[1], (2, N_EDGES), 0, N_NODES, jnp.int32)
        W_src = xavier(ks[2], (IN_DIM, OUT_DIM), IN_DIM, OUT_DIM)
        W_dst = xavier(ks[3], (IN_DIM, OUT_DIM), IN_DIM, OUT_DIM)
        attn = xavier(ks[4], (NUM_HEADS, HEAD_DIM), HEAD_DIM, NUM_HEADS)
        W_out = xavier(ks[5], (OUT_DIM, OUT_DIM), OUT_DIM, OUT_DIM)
        b_out = jnp.zeros((OUT_DIM,), jnp.float32)
        gamma = jnp.ones((OUT_DIM,), jnp.float32)
        beta = jnp.zeros((OUT_DIM,), jnp.float32)
        return {'x': x, 'edge_index': edge_index, 'W_src': W_src, 'W_dst': W_dst, 'attn': attn, 'W_out': W_out, 'b_out': b_out, 'gamma': gamma, 'beta': beta}
    _L1_gnn_all = _L1_gnn_setup()
    _L1_gnn_in = {k: v for k, v in _L1_gnn_all.items() if k in ('W_src', 'W_dst', 'attn', 'W_out', 'b_out', 'gamma', 'beta')}
    del _L1_gnn_all

    def _L2_gnn_setup():
        import jax, jax.numpy as jnp
        import numpy as np
        NEG_SLOPE = 0.2
        EPS = 1e-16
        N_NODES = 3125
        N_EDGES = 50000
        CHANNELS = 128
        M_LAYERS = 3

        def _gat_conv(x, src, dst, W, a_src, a_dst, b, n_nodes):
            h = x @ W
            s = h @ a_src
            d = h @ a_dst
            e = s[src] + d[dst]
            e = jnp.where(e > 0, e, NEG_SLOPE * e)
            e_max = jax.ops.segment_max(e, dst, num_segments=n_nodes)
            e_max = jnp.where(jnp.isfinite(e_max), e_max, 0.0)
            w = jnp.exp(e - e_max[dst])
            denom = jax.ops.segment_sum(w, dst, num_segments=n_nodes)
            alpha = w / (denom[dst] + EPS)
            out = jax.ops.segment_sum(alpha[:, None] * h[src], dst, num_segments=n_nodes)
            return out + b
        key = jax.random.key(seed)
        k1, k2, k3, k4, k5 = jax.random.split(key, 5)
        x = jax.random.normal(k1, (N_NODES, CHANNELS), dtype=jnp.float32)
        edge_index = jax.random.randint(k2, (2, N_EDGES), 0, N_NODES, dtype=jnp.int64)
        Ws = jax.random.normal(k3, (M_LAYERS, CHANNELS, CHANNELS), dtype=jnp.float32) / np.sqrt(CHANNELS)
        att_src = jax.random.normal(k4, (M_LAYERS, CHANNELS), dtype=jnp.float32) / np.sqrt(CHANNELS)
        att_dst = jax.random.normal(k5, (M_LAYERS, CHANNELS), dtype=jnp.float32) / np.sqrt(CHANNELS)
        bias = jnp.zeros((M_LAYERS, CHANNELS), dtype=jnp.float32)
        return {'x': x, 'edge_index': edge_index, 'Ws': Ws, 'att_src': att_src, 'att_dst': att_dst, 'bias': bias}
    _L2_gnn_all = _L2_gnn_setup()
    _L2_gnn_in = {k: v for k, v in _L2_gnn_all.items() if k in ('Ws', 'att_src', 'att_dst', 'bias')}
    del _L2_gnn_all

    def _L3_gnn_setup():
        import jax, jax.numpy as jnp
        import numpy as np
        N_NODES = 3125
        NODE_DIM = 128
        EDGE_DIM = 64
        HIDDEN_DIM = 256
        N_EDGES = 20000
        key = jax.random.key(seed)
        k1, k2, k3, k4, k5, k6, k7 = jax.random.split(key, 7)
        x = jax.random.normal(k1, (N_NODES, NODE_DIM), dtype=jnp.float32)
        edge_index = jax.random.randint(k2, (2, N_EDGES), 0, N_NODES, dtype=jnp.int64)
        edge_attr = jax.random.normal(k3, (N_EDGES, EDGE_DIM), dtype=jnp.float32)
        in_dim = 2 * NODE_DIM + EDGE_DIM
        lim1 = 1.0 / np.sqrt(in_dim)
        lim2 = 1.0 / np.sqrt(HIDDEN_DIM)
        W1 = jax.random.uniform(k4, (in_dim, HIDDEN_DIM), minval=-lim1, maxval=lim1, dtype=jnp.float32)
        b1 = jax.random.uniform(k5, (HIDDEN_DIM,), minval=-lim1, maxval=lim1, dtype=jnp.float32)
        W2 = jax.random.uniform(k6, (HIDDEN_DIM, NODE_DIM), minval=-lim2, maxval=lim2, dtype=jnp.float32)
        b2 = jax.random.uniform(k7, (NODE_DIM,), minval=-lim2, maxval=lim2, dtype=jnp.float32)
        return {'x': x, 'edge_index': edge_index, 'edge_attr': edge_attr, 'W1': W1, 'b1': b1, 'W2': W2, 'b2': b2}
    _L3_gnn_all = _L3_gnn_setup()
    _L3_gnn_in = {k: v for k, v in _L3_gnn_all.items() if k in ('W1', 'b1', 'W2', 'b2')}
    del _L3_gnn_all
    return {'x': x, 'src': src, 'dst': dst, 'edge_attr_64': edge_attr_64, 'edge_weight': edge_weight, 'L0_gnn_W_fc': _L0_gnn_in['W_fc'], 'L0_gnn_w_attn': _L0_gnn_in['w_attn'], 'L0_gnn_bias': _L0_gnn_in['bias'], 'L1_gnn_W_src': _L1_gnn_in['W_src'], 'L1_gnn_W_dst': _L1_gnn_in['W_dst'], 'L1_gnn_attn': _L1_gnn_in['attn'], 'L1_gnn_W_out': _L1_gnn_in['W_out'], 'L1_gnn_b_out': _L1_gnn_in['b_out'], 'L1_gnn_gamma': _L1_gnn_in['gamma'], 'L1_gnn_beta': _L1_gnn_in['beta'], 'L2_gnn_Ws': _L2_gnn_in['Ws'], 'L2_gnn_att_src': _L2_gnn_in['att_src'], 'L2_gnn_att_dst': _L2_gnn_in['att_dst'], 'L2_gnn_bias': _L2_gnn_in['bias'], 'L3_gnn_W1': _L3_gnn_in['W1'], 'L3_gnn_b1': _L3_gnn_in['b1'], 'L3_gnn_W2': _L3_gnn_in['W2'], 'L3_gnn_b2': _L3_gnn_in['b2']}

def reference(x, src, dst, edge_attr_64, edge_weight, L0_gnn_W_fc, L0_gnn_w_attn, L0_gnn_bias, L1_gnn_W_src, L1_gnn_W_dst, L1_gnn_attn, L1_gnn_W_out, L1_gnn_b_out, L1_gnn_gamma, L1_gnn_beta, L2_gnn_Ws, L2_gnn_att_src, L2_gnn_att_dst, L2_gnn_bias, L3_gnn_W1, L3_gnn_b1, L3_gnn_W2, L3_gnn_b2):
    import jax
    import jax.numpy as jnp

    def _L0_gnn_ref(h, edge_weight, src, dst, W_fc, w_attn, bias):
        import jax, jax.numpy as jnp
        import numpy as np
        N = 50000
        DEG = 16
        E = N * DEG
        IN_FEATS = 128
        HEADS = 8
        OUT_FEATS = 16
        n = h.shape[0]
        hp = (h @ W_fc.T).reshape(n, HEADS, OUT_FEATS)
        score = jnp.einsum('ehf,f->eh', hp[src] + hp[dst], w_attn)
        e = jax.nn.leaky_relu(score + jnp.log1p(edge_weight)[:, None])
        m = jax.ops.segment_max(e, dst, num_segments=n)
        ex = jnp.exp(e - m[dst])
        denom = jax.ops.segment_sum(ex, dst, num_segments=n)
        alpha = ex / denom[dst]
        out = jax.ops.segment_sum(alpha[..., None] * hp[src], dst, num_segments=n)
        return out.reshape(n, HEADS * OUT_FEATS) + bias

    def _L1_gnn_ref(x, edge_index, W_src, W_dst, attn, W_out, b_out, gamma, beta):
        import jax, jax.numpy as jnp
        import numpy as np
        N_NODES = 50000
        N_EDGES = 25000
        IN_DIM = 128
        OUT_DIM = 128
        NUM_HEADS = 8
        HEAD_DIM = OUT_DIM // NUM_HEADS
        LN_EPS = 1e-05
        N = x.shape[0]
        H, D = attn.shape
        src, dst = (edge_index[0], edge_index[1])
        h_src = (x @ W_src).reshape(N, H, D)
        h_dst = (x @ W_dst).reshape(N, H, D)
        h_src_e = h_src[src]
        e = jax.nn.leaky_relu(h_src_e + h_dst[dst], 0.2)
        s = jnp.einsum('ehd,hd->eh', e, attn)
        m = jax.ops.segment_max(s, dst, num_segments=N)
        exp = jnp.exp(s - m[dst])
        denom = jax.ops.segment_sum(exp, dst, num_segments=N)
        alpha = exp / (denom[dst] + 1e-08)
        msg = (h_src_e * alpha[..., None]).reshape(-1, H * D)
        out = jax.ops.segment_sum(msg, dst, num_segments=N)
        out = out @ W_out + b_out
        out = out + x
        mu = jnp.mean(out, axis=-1, keepdims=True)
        var = jnp.var(out, axis=-1, keepdims=True)
        out = (out - mu) * jax.lax.rsqrt(var + LN_EPS) * gamma + beta
        return out

    def _L2_gnn_ref(x, edge_index, Ws, att_src, att_dst, bias):
        import jax, jax.numpy as jnp
        import numpy as np
        NEG_SLOPE = 0.2
        EPS = 1e-16
        N_NODES = 3125
        N_EDGES = 50000
        CHANNELS = 128
        M_LAYERS = 3

        def _gat_conv(x, src, dst, W, a_src, a_dst, b, n_nodes):
            h = x @ W
            s = h @ a_src
            d = h @ a_dst
            e = s[src] + d[dst]
            e = jnp.where(e > 0, e, NEG_SLOPE * e)
            e_max = jax.ops.segment_max(e, dst, num_segments=n_nodes)
            e_max = jnp.where(jnp.isfinite(e_max), e_max, 0.0)
            w = jnp.exp(e - e_max[dst])
            denom = jax.ops.segment_sum(w, dst, num_segments=n_nodes)
            alpha = w / (denom[dst] + EPS)
            out = jax.ops.segment_sum(alpha[:, None] * h[src], dst, num_segments=n_nodes)
            return out + b
        n = x.shape[0]
        loop = jnp.arange(n, dtype=edge_index.dtype)
        src = jnp.concatenate([edge_index[0], loop])
        dst = jnp.concatenate([edge_index[1], loop])
        for m in range(Ws.shape[0]):
            x = x + jax.nn.sigmoid(_gat_conv(x, src, dst, Ws[m], att_src[m], att_dst[m], bias[m], n))
        return x

    def _L3_gnn_ref(x, edge_index, edge_attr, W1, b1, W2, b2):
        import jax, jax.numpy as jnp
        import numpy as np
        N_NODES = 3125
        NODE_DIM = 128
        EDGE_DIM = 64
        HIDDEN_DIM = 256
        N_EDGES = 20000
        row = edge_index[0]
        col = edge_index[1]
        msg = jnp.concatenate([x[row], x[col], edge_attr], axis=-1)
        h = jax.nn.relu(msg @ W1 + b1)
        msg_out = h @ W2 + b2
        out = jax.ops.segment_sum(msg_out, row, num_segments=x.shape[0])
        return out
    edge_index = jnp.stack([src, dst])
    x = _layernorm(x + _L0_gnn_ref(x, edge_weight, src, dst, L0_gnn_W_fc, L0_gnn_w_attn, L0_gnn_bias), axis=-1)
    x = _layernorm(x + _L1_gnn_ref(x, edge_index, L1_gnn_W_src, L1_gnn_W_dst, L1_gnn_attn, L1_gnn_W_out, L1_gnn_b_out, L1_gnn_gamma, L1_gnn_beta), axis=-1)
    x = _layernorm(x + _L2_gnn_ref(x, edge_index, L2_gnn_Ws, L2_gnn_att_src, L2_gnn_att_dst, L2_gnn_bias), axis=-1)
    x = _layernorm(x + _L3_gnn_ref(x, edge_index, edge_attr_64, L3_gnn_W1, L3_gnn_b1, L3_gnn_W2, L3_gnn_b2), axis=-1)
    return x

_drawn_inputs = setup_inputs


def setup_inputs(seed=0):
    import zlib

    import numpy as np

    out = dict(_drawn_inputs(seed))
    spreads = {'L1_gnn_b_out': (0.0, 0.1),
     'L1_gnn_gamma': (1.0, 0.2),
     'L1_gnn_beta': (0.0, 0.1),
     'L2_gnn_bias': (0.0, 0.437)}
    factors = {'edge_weight': 3.761,
     'L1_gnn_W_dst': 3.457,
     'L2_gnn_att_dst': 23.356,
     'L3_gnn_b1': 5.477,
     'L0_gnn_bias': 2.67}
    for name, (base, spread) in spreads.items():
        noise = np.random.default_rng([zlib.crc32(name.encode()), seed]).standard_normal(out[name].shape)
        drawn = base * np.exp(spread * noise) if base else spread * noise
        out[name] = jnp.asarray(drawn.astype(out[name].dtype))
    for name, factor in factors.items():
        out[name] = (out[name] * factor).astype(out[name].dtype)
    return out
```

```python
import concourse.bass as bass
from concourse import mybir
from contextlib import ExitStack

fp32 = mybir.dt.float32
i32 = mybir.dt.int32
ALU = mybir.AluOpType
ACT = mybir.ActivationFunctionType
AX = mybir.AxisListType

P = 128
N_NODES = 50000
N_EDGES = 25000
D = 128
HEADS = 8
HD = D // HEADS
J = -(-N_EDGES // P)
SLOTS = P * J
ET = 4
EG = J // ET
NT = 8
NGRP = -(-N_NODES // (P * NT))
NPAD = NGRP * P * NT
TAIL = (N_NODES - (NGRP - 1) * P * NT) // NT
EXT = D + 2
ROWS = SLOTS + N_NODES
SKIP = 60000
BIG = 1.0e38
LN_EPS = 1e-5
assert EG == NGRP and EG % 2 == 1
PAIRS = EG // 2


class Chain:

    def __init__(self, eng, sem):
        self.eng, self.sem, self.off, self.n = eng, sem, 0, 0

    def start(self, g, per, shift=0):
        self.off, self.n, self.per = g * per + shift, 0, per

    def finish(self):
        assert self.n == self.per, (self.n, self.per)

    def inc(self, ins):
        self.n += 1
        ins.then_inc(self.sem, 1)

    def sync(self):
        hold(self.eng, self.sem, self.off + self.n)

    def fused(self):
        self.eng.wait_ge(self.sem, self.off + self.n)

    def link(self, ins):
        self.inc(ins)
        self.sync()


def hold(eng, sem, value):
    eng.wait_ge(sem, value)
    if not isinstance(value, int):
        eng.nop(nofuse=True)


def load_store(load, store, eng):
    load(0, 0, 0, True)
    load(1, 1, 0, True)
    for g in range(2):
        store(g, g, 0, True)
        load(g + 2, g, 1, False)
    with eng.Fori(1, PAIRS - 1) as t:
        for b in range(2):
            store(t * 2 + b, b, t, False)
            load(t * 2 + b + 2, b, t + 1, False)
    store(EG - 3, 0, PAIRS - 1, False)
    load(EG - 1, 0, PAIRS, False)
    store(EG - 2, 1, PAIRS - 1, False)
    store(EG - 1, 0, PAIRS, False)


def groups(eng, body):
    body(0, 0, 0, True)
    body(1, 1, 0, True)
    with eng.Fori(1, PAIRS) as t:
        body(t * 2, 0, t, False)
        body(t * 2 + 1, 1, t, False)
    body(EG - 1, 0, PAIRS, False)


def build(nc, x, src, dst, ew, ea, w0t, w_attn, bias0, w_src, w_dst, attn, w_out, b_out, gamma, beta,
          w2, a_src, a_dst, b2, w31, b31, w32, b32, out):
    ctx = ExitStack()
    with ctx:
        def sb(name, shape, dt=fp32):
            return ctx.enter_context(nc.sbuf_tensor(name, shape, dt))

        def sem(name):
            return ctx.enter_context(nc.semaphore(name))

        def two(name):
            return [sem(f"{name}{b}") for b in range(2)]

        def dram(name, shape, dt=fp32):
            return nc.dram_tensor(name, shape, dt, kind="Internal").ap()

        slot_of_node = dram("slot_of_node", (NPAD, 1), i32)
        x0_dst = dram("x0_dst", (SLOTS, D))
        t1 = dram("t1", (ROWS, D))
        x2s = [dram(f"x2s{m}", (SLOTS, D)) for m in range(3)]
        t2 = [dram(f"t2_{m}", (ROWS, EXT)) for m in range(3)]
        t3 = dram("t3", (ROWS, D))
        acc = dram("acc", (N_NODES + P, D))

        ident = sb("ident", [P, P])
        ones_row = sb("ones_row", [1, P])
        eps = sb("eps", [P, 1])
        zero = sb("zero", [P, 1])
        one = sb("one", [P, 1])
        tri = sb("tri", [P, P])
        src_i = sb("src_i", [P, J], i32)
        dst_i = sb("dst_i", [P, J], i32)
        key = sb("key", [P, J])
        src_f = sb("src_f", [P, J])
        lew = sb("lew", [P, J])
        cont = sb("cont", [P, J + 1])
        pen = sb("pen", [P, J + 1])
        firstm = sb("firstm", [P, J])
        firstpen = sb("firstpen", [P, J])
        lastpen = sb("lastpen", [P, J])
        lastm = sb("lastm", [P, J])
        endm = sb("endm", [P, J])
        endpen = sb("endpen", [P, J])
        kfn = sb("kfn", [P, 2], i32)
        kx = sb("kx", [P, 2])
        cols = sb("cols", [P, 6])
        crep = sb("crep", [P, 4, 8])
        rows = sb("rows", [8, 4, P])
        slot_f = sb("slot_f", [P, J])
        slot_i = sb("slot_i", [P, J], i32)
        gsrc = sb("gsrc", [P, J], i32)
        gdst = sb("gdst", [P, J], i32)
        dscat = sb("dscat", [P, J], i32)
        left = sb("left", [P, P])
        right = sb("right", [P, P])
        node_i = sb("node_i", [P, NPAD // P], i32)
        cur = sb("cur", [P, 2, ET], i32)
        cur2 = sb("cur2", [P, 2, ET], i32)
        dstc = sb("dstc", [P, J], i32)

        w0 = sb("w0", [P, D + HEADS])
        wa_bc = sb("wa_bc", [P, HD])
        wsrc = sb("wsrc", [P, D])
        wdst = sb("wdst", [P, D])
        attn_bc = sb("attn_bc", [P, D])
        wout = sb("wout", [P, D])
        bo_row = sb("bo_row", [1, D])
        bias_bc = sb("bias_bc", [P, D])
        bo_bc = sb("bo_bc", [P, D])
        gam_bc = sb("gam_bc", [P, D])
        bet_bc = sb("bet_bc", [P, D])
        wext = sb("wext", [P, 3, EXT])
        b2row = sb("b2row", [1, 3, EXT])
        w31a = sb("w31a", [P, 2 * D])
        w31b = sb("w31b", [P, 2 * D])
        w31c = sb("w31c", [64, 2 * D])
        b31c = sb("b31c", [P, 2])
        w32s = sb("w32s", [P, 2, D])
        b32row = sb("b32row", [1, D])

        H = sb("H", [P, J, EXT])
        S = sb("S", [P, HEADS, J])
        F = sb("F", [P, HEADS, J])
        B = sb("B", [P, HEADS, J])
        colv = sb("colv", [P, HEADS])
        colc = sb("colc", [P, HEADS])
        rowd = sb("rowd", [HEADS, P])
        rowc = sb("rowc", [HEADS, P])
        Cf = sb("Cf", [P, D + HEADS])
        es = sb("es", [P, J])
        dd = sb("dd", [P, J])
        sdt = sb("sdt", [P, J, 2])
        bufa = sb("bufa", [P, 2, NT, D])
        bufb = sb("bufb", [P, 2, NT, D])
        bufc = sb("bufc", [P, NT, D])
        bufd = sb("bufd", [P, NT, D])
        bufT = sb("bufT", [P, 2, NT, D])
        trow = sb("trow", [P, 3, NT, EXT])
        gbuf = sb("gbuf", [P, 2, ET, EXT])
        av = bufb[:, 0, 0:6, :].rearrange("p (m t) f -> p m t f", m=3)
        w0a = bufd[:, 2, :]
        eab = trow[:, 0:2, :, :].rearrange("p b r e -> p b (r e)")[:, :, 0:ET * 64].rearrange(
            "p b (j f) -> p b j f", f=64)
        eaT = trow[0:64, 2, :, :].rearrange("p r e -> p (r e)")[:, 0:ET * P]
        srep = bufd[:, ET:2 * ET, :]
        cnt = sb("cnt", [P, ET])
        idf = sb("idf", [P, ET])
        idx_add = sb("idx_add", [P, 2, ET], i32)
        real = sb("real", [P, J])
        spare = sb("spare", [P, 1])
        spare_i = sb("spare_i", [P, 1], i32)
        spare_pad = sb("spare_pad", [1, D])
        st = sb("st", [P, NT, 6])
        mv = sb("mv", [P, NT, 2])
        rstd = sb("rstd", [P, NT])
        PS = [ctx.enter_context(nc.psum_tensor(f"ps{i}", [P, 512], fp32)) for i in range(8)]

        def bc(ap, n):
            return ap.unsqueeze(1).broadcast_to([P, n, D])

        def rows4(ap, g):
            return ap[0:SLOTS, :].rearrange("(p j) w -> p j w", p=P)[:, bass.ds(g * ET, ET), :]

        def node_rows(ap, g, off=0, parts=P):
            return ap[bass.ds(off + g * (P * NT), parts * NT), :].rearrange("(p r) w -> p r w", r=NT)

        s_ld = sem("s_loads")
        s_pset = sem("s_pool_setup")
        s_vset = sem("s_dve_setup")
        s_eset = sem("s_pe_setup")
        s_aset = sem("s_act_setup")
        s_slots = sem("s_slot_table_set")
        s_scat = two("s_slots_scattered")
        s_scq = sem("s_scatter_idx")
        s_gmap = two("s_rows_looked_up")
        s_mapq = sem("s_lookup_idx")
        K6, K5 = range(6), range(5)
        s_ga = [two(f"s_gathered{k}_") for k in K6]
        s_gi = [sem(f"s_gather_idx{k}") for k in K6]
        s_tr = [sem(f"s_transposed{k}") for k in (0, 1)]
        s_ev = [sem(f"s_evacuated{k}") for k in (0, 1)]
        s_mm = [sem(f"s_projected{k}") for k in (0, 1)]
        s_he = [sem(f"s_h_kept{k}") for k in K5]
        s_sv = [sem(f"s_scored{k}") for k in (0, 1)]
        s_xst = two("s_x0dst_stored")
        s_sm = [sem(f"s_softmax{k}") for k in K5]
        s_smp = [sem(f"s_softmax_moved{k}") for k in K5]
        s_sme = [sem(f"s_softmax_exp{k}") for k in K5]
        s_b = [sem(f"s_scanned{k}") for k in K5]
        s_cl = [two(f"s_slots_loaded{k}_") for k in K5]
        s_cv = [sem(f"s_slot_dve{k}") for k in K5]
        s_ca = [sem(f"s_slot_act{k}") for k in K5]
        s_cp = [sem(f"s_slot_pe{k}") for k in K5]
        s_cs = [two(f"s_slots_stored{k}_") for k in K5]
        s_asc = two("s_acc_rows_scattered")
        s_asq = sem("s_acc_idx")
        s_accp = sem("s_acc_padding")
        s_dl = two("s_nodes_loaded")
        s_dv = sem("s_dense_dve")
        s_da = sem("s_dense_act")
        s_dp = sem("s_dense_pe")
        s_dx1 = two("s_x1_stored")
        s_dx3 = two("s_x3_stored")
        s_dt2 = [sem(f"s_t2_stored{m}") for m in range(3)]
        s_el = two("s_edge_attr_loaded")
        s_ma = sem("s_message_act")
        s_mp = sem("s_message_pe")
        s_mv = sem("s_message_dve")
        s_add = sem("s_messages_added")
        s_fl = two("s_final_loaded")
        s_fs = two("s_final_stored")
        s_fv = sem("s_final_dve")
        s_fa = sem("s_final_act")

        CLD = [16, 16, 32, 32, 48]
        CST = [16, 32, 32, 32, 16]
        CA = [1, 8, 6, 6, 2]
        CP = [0, 4, 2, 2, 0]
        CPER = [20, 35, 10, 10, 24]
        DPER, DA, DP = 109, 28, 6
        MA, MP, MV = 7, 4, 13
        FPER = 25
        mark = {}
        block = ctx.enter_context(nc.Block())
        N_LOADS = 27
        heads = [HEADS, HEADS, 1, 1, 1]

        @block.vector
        def _(dve):
            v = nc.vector
            c = Chain(dve, s_vset)

            for t, val in ((eps, LN_EPS), (zero, 0.0), (one, 1.0)):
                c.inc(v.memset(t[:], val))
            c.inc(v.memset(cont[:], 0.0))
            dve.wait_ge(s_ld, 16 * N_LOADS)
            c.inc(v.tensor_copy(key[:], dst_i[:]))
            c.inc(v.tensor_copy(src_f[:], src_i[:]))
            c.inc(v.tensor_copy(kx[:], kfn[:]))
            dve.wait_ge(s_pset, 5)
            c.inc(v.tensor_copy(slot_f[:], slot_i[:]))
            c.sync()
            kf, kl = key[:, 0:1], key[:, J - 1:J]
            c.inc(v.tensor_tensor(cont[:, 1:J], key[:, 1:J], key[:, 0:J - 1], ALU.is_equal))
            c.inc(v.tensor_scalar(firstm[:], key[:], kf, None, ALU.is_equal))
            c.inc(v.tensor_scalar(lastm[:], key[:], kl, None, ALU.is_equal))
            c.inc(v.tensor_scalar(dstc[:], key[:], float(N_NODES - 1), None, ALU.min))
            c.inc(v.tensor_tensor(cols[:, 0:1], kf, kx[:, 1:2], ALU.is_equal))
            c.inc(v.tensor_tensor(cols[:, 1:2], kf, kl, ALU.is_equal))
            c.inc(v.tensor_tensor(cols[:, 2:3], kl, kx[:, 0:1], ALU.is_equal))
            c.sync()
            c.inc(v.tensor_scalar(pen[:], cont[:], 1.0, BIG, ALU.subtract, ALU.mult))
            c.inc(v.tensor_scalar(firstpen[:], firstm[:], 1.0, BIG, ALU.subtract, ALU.mult))
            c.inc(v.tensor_scalar(lastpen[:], lastm[:], 1.0, BIG, ALU.subtract, ALU.mult))
            c.inc(v.tensor_tensor(cols[:, 3:4], cols[:, 0:1], cols[:, 1:2], ALU.mult))
            c.inc(v.tensor_tensor(cols[:, 4:5], cols[:, 2:3], cols[:, 1:2], ALU.mult))
            c.inc(v.tensor_scalar(endm[:], cont[:, 1:J + 1], -1.0, 1.0, ALU.mult, ALU.add))
            c.sync()
            c.link(v.tensor_scalar(endm[:, J - 1:J], cols[:, 2:3], -1.0, 1.0, ALU.mult, ALU.add))
            c.inc(v.tensor_scalar(endpen[:], endm[:], 1.0, BIG, ALU.subtract, ALU.mult))
            c.inc(v.tensor_scalar(dd[:], key[:], float(SKIP), None, ALU.subtract))
            for n, q in enumerate((3, 0, 4, 2)):
                c.inc(v.tensor_scalar(crep[:, n, :], cols[:, q:q + 1].broadcast_to([P, 8]), 1.0, BIG,
                                      ALU.subtract, ALU.mult))
            c.inc(v.tensor_copy(bufc[:, 0, :], kf.broadcast_to([P, P])))
            c.inc(v.tensor_copy(bufc[:, 1, :], kl.broadcast_to([P, P])))
            c.sync()
            mark["rep"] = c.n
            c.link(v.tensor_tensor(dd[:], dd[:], endm[:], ALU.mult))
            c.inc(v.tensor_scalar(dscat[:], dd[:], float(SKIP), None, ALU.add))
            dve.wait_ge(s_eset, 1)
            c.inc(v.tensor_scalar(left[:], PS[0][:, 0:P], kl, None, ALU.is_equal))
            c.inc(v.tensor_scalar(right[:], PS[0][:, P:2 * P], kf, None, ALU.is_equal))
            c.link(v.tensor_copy(rows[:], PS[1][0:8, :].rearrange("h (n p) -> h n p", n=4)))
            mark["lr"] = c.n
            c.link(v.tensor_tensor(w0a.rearrange("p (h f) -> p h f", f=HD),
                                   w0[:, 0:D].rearrange("p (h f) -> p h f", f=HD),
                                   wa_bc[:].unsqueeze(1).broadcast_to([P, HEADS, HD]), ALU.mult))
            c.inc(v.tensor_reduce(w0[:, D:D + HEADS], w0a.rearrange("p (h f) -> p h f", f=HD), AX.X, ALU.add))
            for m in range(3):
                c.link(v.tensor_tensor(bufd[:, 0:2, :], wext[:, m, 0:D].unsqueeze(1).broadcast_to([P, 2, D]),
                                       av[:, m, :, :], ALU.mult))
                c.link(v.tensor_reduce(wext[:, m, D:EXT], bufd[:, 0:2, :], AX.X, ALU.add))

            def spread(c, to, val, k_moved, sem_moved, name):
                c.link(v.tensor_tensor_scan(dd[:, ::-1], cont[:, J:0:-1], val[:, ::-1], 0.0, ALU.mult, ALU.add))
                mark[name] = c.n
                dve.wait_ge(sem_moved, k_moved)
                c.link(v.tensor_copy(colc[:, 0:1], PS[1][:, 0:1]))
                c.link(v.scalar_tensor_tensor(to, lastm[:], colc[:, 0:1], dd[:], ALU.mult, ALU.add))

            c.inc(v.tensor_scalar(real[:], key[:], float(N_NODES), None, ALU.is_lt))
            dve.wait_ge(s_pset, 12)
            c.link(v.tensor_tensor(es[:], slot_f[:], endm[:], ALU.mult))
            spread(c, S[:, 0, :], es, 2, s_eset, "spread_slots")
            c.link(v.tensor_copy(gdst[:], S[:, 0, :]))
            c.link(v.tensor_copy(spare[:], spare_i[:]))
            mark["setup"] = c.n

            def norm(c, src_of, dst_of, n, act_sem, act_at, name):
                for i in range(n):
                    c.inc(v.bn_stats(st[:, i, :], src_of(i)))
                c.sync()
                for i in range(n):
                    c.inc(v.bn_aggr(mv[:, i, :], st[:, i, :]))
                mark[name] = c.n
                hold(dve, act_sem, act_at)
                c.sync()
                c.link(v.reciprocal(rstd[:, 0:n], rstd[:, 0:n]))
                for i in range(n):
                    c.inc(v.tensor_scalar(dst_of(i), src_of(i), mv[:, i, 0:1], rstd[:, i:i + 1],
                                          ALU.subtract, ALU.mult))

            def softmax(k):
                c = Chain(dve, s_sm[k])
                nh = heads[k]
                hs = range(nh)
                if k == 0:
                    dve.wait_ge(s_sv[0], EG)
                    dve.wait_ge(s_aset, 1)
                    c.link(v.tensor_tensor(S[:], S[:], lew[:].unsqueeze(1).broadcast_to([P, HEADS, J]), ALU.add))
                    c.link(v.scalar_tensor_tensor(F[:], S[:], 0.01, S[:], ALU.mult, ALU.max))
                    c.link(v.tensor_copy(S[:], F[:]))
                elif k == 1:
                    dve.wait_ge(s_sv[1], 3 * EG)
                else:
                    dve.wait_ge(s_he[k], EG)
                    dve.wait_ge(s_ca[k - 1], EG * CA[k - 1])
                    c.inc(v.tensor_tensor(es[:], sdt[:, :, 0], sdt[:, :, 1], ALU.add))
                    c.link(v.tensor_tensor(S[:, 1, :], sdt[:, :, 1], endm[:], ALU.mult))
                    c.link(v.scalar_tensor_tensor(es[:], es[:], 0.2, es[:], ALU.mult, ALU.max))
                    spread(c, S[:, 2, :], S[:, 1, :], 1, s_smp[k], f"spread{k}")
                    c.link(v.tensor_tensor(S[:, 1, :], H[:, :, D], S[:, 2, :], ALU.add))
                    c.link(v.scalar_tensor_tensor(S[:, 0, :], S[:, 1, :], 0.2, S[:, 1, :], ALU.mult, ALU.max))
                base = 1 if k >= 2 else 0
                for h in hs:
                    c.inc(v.tensor_tensor_scan(F[:, h, :], pen[:, 0:J], S[:, h, :], 0.0, ALU.add, ALU.max))
                c.sync()
                c.link(v.tensor_copy(colv[:, 0:nh], F[:, 0:nh, J - 1]))
                mark[f"colf{k}"] = c.n
                dve.wait_ge(s_smp[k], base + 1)
                c.link(v.tensor_tensor_scan(rowd[0:nh, :], rows[0:nh, 0, :], PS[0][0:nh, 0:P], 0.0, ALU.add, ALU.max))
                c.inc(v.memset(rowc[0:nh, 0:1], -BIG))
                c.link(v.tensor_tensor(rowc[0:nh, 1:P], rowd[0:nh, 0:P - 1], rows[0:nh, 1, 1:P], ALU.add))
                mark[f"rowf{k}"] = c.n
                dve.wait_ge(s_smp[k], base + 2)
                c.link(v.tensor_copy(colc[:, 0:nh], PS[1][:, 0:nh]))
                for h in hs:
                    c.inc(v.scalar_tensor_tensor(F[:, h, :], firstpen[:], colc[:, h:h + 1], F[:, h, :], ALU.add, ALU.max))
                c.sync()
                if k >= 2:
                    c.link(v.tensor_tensor(S[:, 1, :], es[:], endpen[:], ALU.add))
                    c.link(v.tensor_tensor(F[:, 0, :], F[:, 0, :], S[:, 1, :], ALU.max))
                for h in hs:
                    c.inc(v.tensor_tensor_scan(B[:, h, ::-1], pen[:, J:0:-1], F[:, h, ::-1], 0.0, ALU.add, ALU.max))
                c.sync()
                c.link(v.tensor_copy(colv[:, 0:nh], B[:, 0:nh, 0]))
                mark[f"colb{k}"] = c.n
                dve.wait_ge(s_smp[k], base + 3)
                c.link(v.tensor_tensor_scan(rowd[0:nh, ::-1], rows[0:nh, 2, ::-1], PS[0][0:nh, P - 1::-1], 0.0,
                                            ALU.add, ALU.max))
                c.inc(v.memset(rowc[0:nh, P - 1:P], -BIG))
                c.link(v.tensor_tensor(rowc[0:nh, 0:P - 1], rowd[0:nh, 1:P], rows[0:nh, 3, 0:P - 1], ALU.add))
                mark[f"rowb{k}"] = c.n
                dve.wait_ge(s_smp[k], base + 4)
                c.link(v.tensor_copy(colc[:, 0:nh], PS[1][:, 0:nh]))
                for h in hs:
                    c.inc(v.scalar_tensor_tensor(B[:, h, :], lastpen[:], colc[:, h:h + 1], B[:, h, :], ALU.add, ALU.max))
                c.sync()
                c.link(v.tensor_tensor(S[:, 0:nh, :], S[:, 0:nh, :], B[:, 0:nh, :], ALU.subtract))
                if k >= 2:
                    c.link(v.tensor_tensor(es[:], es[:], B[:, 0, :], ALU.subtract))
                    c.link(v.tensor_tensor(es[:], es[:], endm[:], ALU.mult))
                mark[f"exp{k}"] = c.n
                dve.wait_ge(s_sme[k], 2 if k >= 2 else 1)
                for h in hs:
                    c.inc(v.tensor_tensor_scan(F[:, h, :], cont[:, 0:J], S[:, h, :], 0.0, ALU.mult, ALU.add))
                c.sync()
                mark[f"sums{k}"] = c.n
                return c

            def scan_messages(k, cs):
                c = Chain(dve, s_b[k])

                def body(g, first):
                    c.start(g, ET + 1, 0 if first else -1)
                    hg = H[:, bass.ds(g * ET, ET), 0:D]
                    if heads[k] == 1:
                        wv = S[:, 0, bass.ds(g * ET, ET)].unsqueeze(2).broadcast_to([P, ET, D])
                        c.inc(v.tensor_tensor(hg, hg, wv, ALU.mult))
                    else:
                        hv = hg.rearrange("p j (h f) -> p j h f", f=HD)
                        wv = S[:, :, bass.ds(g * ET, ET)].rearrange("p h j -> p j h").unsqueeze(3).broadcast_to(
                            [P, ET, HEADS, HD])
                        c.inc(v.tensor_tensor(hv, hv, wv, ALU.mult))
                    for i in range(1 if first else 0, ET):
                        c.fused()
                        c.inc(v.scalar_tensor_tensor(H[:, bass.ds(g * ET + i, 1), 0:D], H[:, bass.ds(g * ET + i - 1, 1), 0:D],
                                                     cont[:, bass.ds(g * ET + i, 1)], H[:, bass.ds(g * ET + i, 1), 0:D],
                                                     ALU.mult, ALU.add))

                if k < 2:
                    dve.wait_ge(s_he[k], EG * (k + 1))
                body(0, True)
                with dve.Fori(1, EG) as g:
                    body(g, False)
                dve.wait_ge(s_b[k], EG * (ET + 1) - 1)
                c = cs
                nh = heads[k]
                dve.wait_ge(s_smp[k], (5 if k < 2 else 6))
                c.link(v.tensor_copy(Cf[:, 0:D + nh], PS[0][:, 0:D + nh]))
                mark[f"cf{k}"] = c.n
                for h in range(nh):
                    c.inc(v.scalar_tensor_tensor(F[:, h, :], firstm[:], Cf[:, D + h:D + h + 1], F[:, h, :], ALU.mult, ALU.add))
                c.sync()
                if k == 0:
                    c.link(v.tensor_scalar(F[:], F[:], 1e-30, None, ALU.max))
                elif k == 1:
                    c.link(v.tensor_scalar(F[:], F[:], 1e-8, None, ALU.add))
                else:
                    c.link(v.tensor_tensor(F[:, 0, :], F[:, 0, :], es[:], ALU.add))
                    c.link(v.tensor_scalar(F[:, 0, :], F[:, 0, :], 1e-16, None, ALU.add))
                c.link(v.reciprocal(B[:, 0:nh, :], F[:, 0:nh, :]))

            def slot_update(k):
                c = Chain(dve, s_cv[k])
                PER = CPER[k]

                def body(g, b, r, first):
                    c.start(g, PER)
                    hold(dve, s_cl[k][b], r * CLD[k] + CLD[k])
                    for i in range(ET):
                        hj = H[:, bass.ds(g * ET + i, 1), 0:D].rearrange("p a f -> p (a f)")
                        c.inc(v.scalar_tensor_tensor(hj, Cf[:, 0:D], firstm[:, bass.ds(g * ET + i, 1)], hj, ALU.mult, ALU.add))
                    c.sync()
                    if k >= 2:
                        for i in range(ET):
                            hj = H[:, bass.ds(g * ET + i, 1), 0:D].rearrange("p a f -> p (a f)")
                            c.inc(v.scalar_tensor_tensor(hj, gbuf[:, b, i, 0:D], es[:, bass.ds(g * ET + i, 1)], hj,
                                                         ALU.mult, ALU.add))
                        c.sync()
                    hg = H[:, bass.ds(g * ET, ET), 0:D]
                    if heads[k] == 1:
                        c.link(v.tensor_tensor(bufc[:, 0:ET, :], hg, B[:, 0, bass.ds(g * ET, ET)].unsqueeze(2).broadcast_to([P, ET, D]), ALU.mult))
                    else:
                        c.link(v.tensor_tensor(bufc[:, 0:ET, :].rearrange("p j (h f) -> p j h f", f=HD),
                                               hg.rearrange("p j (h f) -> p j h f", f=HD),
                                               B[:, :, bass.ds(g * ET, ET)].rearrange("p h j -> p j h").unsqueeze(3).broadcast_to([P, ET, HEADS, HD]),
                                               ALU.mult))
                    mark[f"agg{k}"] = c.n
                    xs = bufa[:, b, 0:ET, :]
                    xo = bufb[:, b, 0:ET, :]
                    if k == 0:
                        c.link(v.tensor_tensor(bufc[:, 0:ET, :], bufc[:, 0:ET, :], xs, ALU.add))
                        c.link(v.tensor_tensor(bufc[:, 0:ET, :], bufc[:, 0:ET, :], bc(bias_bc[:], ET), ALU.add))
                        if not first:
                            hold(dve, s_cs[k][b], r * 16)
                        norm(c, lambda i: bufc[:, i, :], lambda i: bufb[:, b, i, :], ET, s_ca[k], g + 1, "c0_var")
                    elif k == 1:
                        hold(dve, s_cp[k], g * CP[1] + 2)
                        c.link(v.tensor_tensor(bufd[:, 0:ET, :], PS[2][:, :].rearrange("p (j f) -> p j f", f=D), xs, ALU.add))
                        norm(c, lambda i: bufd[:, i, :], lambda i: bufd[:, i, :], ET, s_ca[k], g * CA[1] + 2, "c1_var1")
                        c.inc(v.tensor_tensor(bufd[:, ET:2 * ET, :], xs, bc(bet_bc[:], ET), ALU.add))
                        c.sync()
                        c.link(v.tensor_tensor(bufd[:, 0:ET, :], bufd[:, 0:ET, :], bc(gam_bc[:], ET), ALU.mult))
                        c.link(v.tensor_tensor(bufd[:, 0:ET, :], bufd[:, 0:ET, :], bufd[:, ET:2 * ET, :], ALU.add))
                        c.sync()
                        if not first:
                            hold(dve, s_cs[k][b], r * CST[k])
                        norm(c, lambda i: bufd[:, i, :], lambda i: bufb[:, b, i, :], ET, s_ca[k], g * CA[1] + 3, "c1_var2")
                    else:
                        hold(dve, s_ca[k], g * CA[k] + 1)
                        if not first:
                            hold(dve, s_cs[k][b], r * CST[k])
                        if k < 4:
                            c.inc(v.tensor_tensor(xo, xs, bufd[:, 0:ET, :], ALU.add))
                        else:
                            c.link(v.tensor_tensor(bufd[:, ET:2 * ET, :], xs, bufd[:, 0:ET, :], ALU.add))
                            c.link(v.tensor_tensor(bufd[:, ET:2 * ET, :], bufd[:, ET:2 * ET, :], bufa[:, b, ET:2 * ET, :], ALU.add))
                            if not first:
                                hold(dve, s_asc[b], r * 64)
                            norm(c, lambda i: bufd[:, ET + i, :], lambda i: bufb[:, b, i, :], ET, s_ca[k], g * CA[k] + 2, "c4_var")
                    mark[f"xo{k}"] = c.n
                    c.finish()

                groups(dve, body)
                dve.wait_ge(s_cv[k], EG * PER)

            def score0(g, b, r, first):
                hold(dve, s_mm[0], g + 1)
                v.tensor_copy(S[:, :, bass.ds(g * ET, ET)].rearrange("p h j -> p j h"),
                              PS[6 + b][:, 0:ET * HEADS].rearrange("p (j h) -> p j h", h=HEADS)).then_inc(s_sv[0], 1)

            groups(dve, score0)
            scan_messages(0, softmax(0))
            slot_update(0)

            def dense(g, b, r, first):
                c = Chain(dve, s_dv)
                c.start(g, DPER)
                hold(dve, s_dl[b], r * 16 + 16)
                c.link(v.tensor_tensor(bufc[:], bufa[:, b], bc(bias_bc[:], NT), ALU.add))
                if not first:
                    hold(dve, s_dx1[b], r * 16)
                norm(c, lambda i: bufc[:, i, :], lambda i: bufb[:, b, i, :], NT, s_da, g * DA + 1, "d_var1")
                mark["dx1"] = c.n
                c.sync()
                c.inc(v.tensor_tensor(bufc[:], bufb[:, b], bc(bo_bc[:], NT), ALU.add))
                c.inc(v.tensor_tensor(bufd[:], bufb[:, b], bc(bet_bc[:], NT), ALU.add))
                c.sync()
                norm(c, lambda i: bufc[:, i, :], lambda i: bufc[:, i, :], NT, s_da, g * DA + 2, "d_var2")
                c.sync()
                c.link(v.tensor_tensor(bufc[:], bufc[:], bc(gam_bc[:], NT), ALU.mult))
                c.link(v.tensor_tensor(bufc[:], bufc[:], bufd[:], ALU.add))
                norm(c, lambda i: bufc[:, i, :], lambda i: bufa[:, b, i, :], NT, s_da, g * DA + 3, "d_var3")
                mark["dx2"] = c.n
                c.sync()
                for m in range(3):
                    hold(dve, s_da, g * DA + 8 * m + 8)
                    c.link(v.tensor_tensor(bufc[:], bufa[:, b] if m == 0 else bufc[:], bufd[:], ALU.add))
                    mark[f"dm{m}"] = c.n
                c.link(v.tensor_tensor(bufc[:], bufc[:], bufa[:, b], ALU.add))
                norm(c, lambda i: bufc[:, i, :], lambda i: bufa[:, b, i, :], NT, s_da, g * DA + DA, "d_var4")
                mark["dx3"] = c.n
                c.sync()
                c.finish()

            groups(dve, dense)

            def score1(g, b, r, first):
                c = Chain(dve, s_sv[1])
                c.start(g, 3)
                hold(dve, s_he[1], g * 2 + 2)
                c.link(v.tensor_tensor(bufb[:, b, 0:ET, :], bufb[:, b, 0:ET, :],
                                       PS[6 + b][:, :].rearrange("p (j f) -> p j f", f=D), ALU.max))
                c.link(v.tensor_tensor(bufb[:, b, 0:ET, :], bufb[:, b, 0:ET, :], bc(attn_bc[:], ET), ALU.mult))
                c.inc(v.tensor_reduce(S[:, :, bass.ds(g * ET, ET)].rearrange("p h j -> p j h"),
                                      bufb[:, b, 0:ET, :].rearrange("p j (h f) -> p j h f", f=HD), AX.X, ALU.add))
                c.finish()

            groups(dve, score1)
            scan_messages(1, softmax(1))
            slot_update(1)
            for k in (2, 3, 4):
                scan_messages(k, softmax(k))
                slot_update(k)

            def dedup(g, b, r, first):
                c = Chain(dve, s_mv)
                c.start(g, MV)
                sj = src_f[:, bass.ds(g * ET, ET)]
                c.inc(v.tensor_copy(srep, sj.unsqueeze(2).broadcast_to([P, ET, P])))
                mark["srep"] = c.n
                hold(dve, s_mp, g * MP + 1)
                if not (isinstance(g, int) and g == 0):
                    hold(dve, s_mp, g * MP)
                for i in range(ET):
                    c.inc(v.tensor_scalar(bufc[:, i, :], PS[3][:, i * P:(i + 1) * P], src_f[:, bass.ds(g * ET + i, 1)],
                                          None, ALU.is_equal))
                mark["same"] = c.n
                c.sync()
                c.link(v.tensor_tensor(bufc[:, ET:2 * ET, :], bufc[:, 0:ET, :], bc(tri[:], ET), ALU.mult))
                c.link(v.tensor_reduce(cnt[:], bufc[:, ET:2 * ET, :], AX.X, ALU.add))
                c.link(v.tensor_scalar(cnt[:], cnt[:], 0.0, None, ALU.is_equal))
                c.link(v.tensor_tensor(cnt[:], cnt[:], real[:, bass.ds(g * ET, ET)], ALU.mult))
                c.link(v.tensor_scalar(idf[:], sj, spare[:, 0:1], None, ALU.subtract))
                c.link(v.tensor_tensor(idf[:], idf[:], cnt[:], ALU.mult))
                if not first:
                    hold(dve, s_add, g * 64 - 64)
                c.link(v.tensor_scalar(idx_add[:, b, :], idf[:], spare[:, 0:1], None, ALU.add))
                mark["idx"] = c.n
                c.link(v.tensor_scalar(colv[:, 0:1], spare[:, 0:1], 1.0, None, ALU.mult))
                c.finish()

            groups(dve, dedup)
            dve.wait_ge(s_mv, EG * MV)

            def final(g, b, r, first):
                c = Chain(dve, s_fv)
                c.start(g, FPER)
                hold(dve, s_fl[b], r * 16 + 16)
                if not first:
                    hold(dve, s_fs[b], r * 16)
                norm(c, lambda i: bufa[:, b, i, :], lambda i: bufb[:, b, i, :], NT, s_fa, g + 1, "f_var")
                c.finish()

            groups(dve, final)

        @block.scalar
        def _(act):
            a = nc.scalar

            def move(to, of, sem_):
                a.activation(to, of, ACT.Copy).then_inc(sem_, 1)

            def root(sem_):
                return a.activation

            act.wait_ge(s_ld, 16 * N_LOADS)
            act.wait_ge(s_vset, 4)
            a.activation(lew[:], lew[:], ACT.Ln, bias=one[:, 0:1]).then_inc(s_aset, 1)

            def std(n, sem_):
                a.activation(rstd[:, 0:n], mv[:, 0:n, 1], ACT.Sqrt, bias=eps[:, 0:1]).then_inc(sem_, 1)

            def project(k):
                def body(g, b, r, first):
                    hold(act, s_tr[k], g + 1)
                    if not first:
                        hold(act, s_mm[k], g - 1)
                    move(bufT[:, b, 0:ET, :], PS[b][:, :].rearrange("p (j f) -> p j f", f=P), s_ev[k])
                    move(bufT[:, b, ET:2 * ET, :], PS[2 + b][:, :].rearrange("p (j f) -> p j f", f=P), s_ev[k])
                    hold(act, s_mm[k], g + 1)
                    move(H[:, bass.ds(g * ET, ET), 0:D], PS[4 + b][:, :].rearrange("p (j f) -> p j f", f=D), s_he[k])
                    if k == 1:
                        if not first:
                            hold(act, s_sv[1], g * 3 - 3)
                        a.activation(bufb[:, b, 0:ET, :], PS[6 + b][:, :].rearrange("p (j f) -> p j f", f=D),
                                     ACT.Copy, scale=0.2).then_inc(s_he[1], 1)
                groups(act, body)

            def exps(k):
                nh = heads[k]
                act.wait_ge(s_sm[k], mark[f"exp{k}"])
                a.activation(S[:, 0:nh, :], S[:, 0:nh, :], ACT.Exp).then_inc(s_sme[k], 1)
                if k >= 2:
                    a.activation(es[:], es[:], ACT.Exp).then_inc(s_sme[k], 1)

            def slot_update(k):
                def body(g, b, r, first):
                    if k == 0:
                        hold(act, s_cv[0], g * CPER[0] + mark["c0_var"])
                        std(ET, s_ca[0])
                        return
                    if k == 1:
                        hold(act, s_cp[1], g * CP[1] + 1)
                        move(bufT[:, 0, 0:ET, :], PS[0][:, :].rearrange("p (j f) -> p j f", f=P), s_ca[1])
                        for n in (1, 2):
                            hold(act, s_cv[1], g * CPER[1] + mark[f"c1_var{n}"])
                            std(ET, s_ca[1])
                    else:
                        hold(act, s_cv[k], g * CPER[k] + mark[f"agg{k}"])
                        a.activation(bufd[:, 0:ET, :], bufc[:, 0:ET, :], ACT.Sigmoid).then_inc(s_ca[k], 1)
                        if k == 4:
                            hold(act, s_cv[4], g * CPER[4] + mark["c4_var"])
                            std(ET, s_ca[4])
                            return
                    hold(act, s_cp[k], g * CP[k] + CP[k] - 1)
                    move(bufT[:, 1, 0:ET, :], PS[1][:, :].rearrange("p (j f) -> p j f", f=P), s_ca[k])
                    hold(act, s_cp[k], g * CP[k] + CP[k])
                    if not first:
                        hold(act, s_cs[k][b], r * CST[k])
                    r3 = PS[3][:, 0:3 * EXT].rearrange("p (j e) -> p j e", e=EXT)
                    r4 = PS[4][:, 0:EXT].rearrange("p (j e) -> p j e", e=EXT)
                    move(trow[:, b, 0:3, :], r3, s_ca[k])
                    move(trow[:, b, 3:4, :], r4, s_ca[k])
                    move(sdt[:, bass.ds(g * ET, 3), :], r3[:, :, D:EXT], s_ca[k])
                    move(sdt[:, bass.ds(g * ET + 3, 1), :], r4[:, :, D:EXT], s_ca[k])
                groups(act, body)

            def dense(g, b, r, first):
                for n in (1, 2, 3):
                    hold(act, s_dv, g * DPER + mark[f"d_var{n}"])
                    std(NT, s_da)
                for m in range(3):
                    hold(act, s_dp, g * DP + 2 * m + 1)
                    for q in range(2):
                        move(bufT[:, 0, q * ET:(q + 1) * ET, :], PS[q][:, :].rearrange("p (j f) -> p j f", f=P), s_da)
                    hold(act, s_dp, g * DP + 2 * m + 2)
                    for q, w in enumerate((3, 3, 2)):
                        a.activation(bufd[:, 3 * q:3 * q + w, :],
                                     PS[2 + q][:, 0:w * EXT].rearrange("p (j e) -> p j e", e=EXT)[:, :, 0:D],
                                     ACT.Sigmoid).then_inc(s_da, 1)
                    if not (isinstance(g, int) and g == 0):
                        hold(act, s_dt2[m], g * 16)
                    for q, w in enumerate((3, 3, 2)):
                        move(trow[:, m, 3 * q:3 * q + w, :],
                             PS[2 + q][:, 0:w * EXT].rearrange("p (j e) -> p j e", e=EXT), s_da)
                hold(act, s_dv, g * DPER + mark["d_var4"])
                std(NT, s_da)

            project(0)
            exps(0)
            slot_update(0)
            for q in range(2):
                act.wait_ge(s_cs[0][q], (PAIRS + 1 - q) * CST[0])
            groups(act, dense)
            act.wait_ge(s_cv[0], EG * CPER[0])
            for q in range(2):
                act.wait_ge(s_dx1[q], (PAIRS + 1 - q) * 16)
            for m in range(3):
                act.wait_ge(s_dt2[m], EG * 16)
            project(1)
            exps(1)
            slot_update(1)
            for k in (2, 3, 4):
                act.wait_ge(s_cv[k - 1], EG * CPER[k - 1])
                for q in range(2):
                    act.wait_ge(s_cs[k - 1][q], (PAIRS + 1 - q) * CST[k - 1])

                def keep(g, b, r, first, k=k):
                    hold(act, s_ga[k][b], r * 64 + 64)
                    move(H[:, bass.ds(g * ET, ET), :], gbuf[:, b, :, :], s_he[k])
                groups(act, keep)
                exps(k)
                slot_update(k)
            for q in range(2):
                act.wait_ge(s_cs[4][q], (PAIRS + 1 - q) * CST[4])
                act.wait_ge(s_asc[q], (PAIRS + 1 - q) * 64)

            def message(g, b, r, first):
                hold(act, s_mp, g * MP + 1)
                for q in range(2):
                    move(bufT[:, 0, q * ET:(q + 1) * ET, :], PS[q][:, :].rearrange("p (j f) -> p j f", f=P), s_ma)
                move(eaT, PS[2][0:64, :], s_ma)
                hold(act, s_mp, g * MP + 2)
                for q in range(2):
                    a.activation(bufT[:, 1, q * ET:(q + 1) * ET, :], PS[4 + q][:, :].rearrange("p (j f) -> p j f", f=P),
                                 ACT.Relu, bias=b31c[:, q:q + 1]).then_inc(s_ma, 1)
                hold(act, s_mp, g * MP + 3)
                move(bufd[:, 0:ET, :], PS[6][:, :].rearrange("p (j f) -> p j f", f=D), s_ma)
                hold(act, s_mp, g * MP + 4)
                if not first:
                    hold(act, s_add, g * 64 - 64)
                move(bufb[:, b, 0:ET, :], PS[7][:, :].rearrange("p (j f) -> p j f", f=D), s_ma)
            groups(act, message)

            def final(g, b, r, first):
                hold(act, s_fv, g * FPER + mark["f_var"])
                std(NT, s_fa)
            groups(act, final)

        @block.tensor
        def _(pe):
            t = nc.tensor

            def mm(to, w, m, start=True, stop=True):
                return t.matmul(to, w, m, start=start, stop=stop)

            pe.wait_ge(s_pset, 9)
            pe.wait_ge(s_vset, mark["rep"])
            t.transpose(PS[0][:, 0:P], bufc[:, 0, :], ident[:])
            t.transpose(PS[0][:, P:2 * P], bufc[:, 1, :], ident[:])
            for n in range(4):
                last = t.transpose(PS[1][0:8, n * P:(n + 1) * P], crep[:, n, :], ident[:])
            last.then_inc(s_eset, 1)
            pe.wait_ge(s_vset, mark["spread_slots"])
            pe.wait_ge(s_pset, 11)
            mm(PS[1][:, 0:1], right[:], dd[:, 0:1]).then_inc(s_eset, 1)
            pe.wait_ge(s_vset, mark["setup"])

            def project(k):
                def body(g, b, r, first):
                    hold(pe, s_ga[k][b], r * 128 + 128)
                    for i in range(ET):
                        t.transpose(PS[b][:, i * P:(i + 1) * P], bufa[:, b, i, :], ident[:])
                    for i in range(ET):
                        last = t.transpose(PS[2 + b][:, i * P:(i + 1) * P], bufa[:, b, ET + i, :], ident[:])
                    last.then_inc(s_tr[k], 1)
                    hold(pe, s_ev[k], g * 2 + 2)
                    if not first:
                        hold(pe, s_he[k], (g - 1) * (k + 1))
                        hold(pe, s_sv[k], g - 1 if k == 0 else g * 3 - 5)
                    for i in range(ET):
                        xs, xd = bufT[:, b, i, :], bufT[:, b, ET + i, :]
                        o = PS[4 + b][:, i * D:(i + 1) * D]
                        if k == 0:
                            e = PS[6 + b][:, i * HEADS:(i + 1) * HEADS]
                            mm(o, xs, w0[:, 0:D])
                            mm(e, xs, w0[:, D:D + HEADS], stop=False)
                            last = mm(e, xd, w0[:, D:D + HEADS], start=False)
                        else:
                            e = PS[6 + b][:, i * D:(i + 1) * D]
                            mm(o, xs, wsrc[:])
                            mm(e, xs, wsrc[:], stop=False)
                            last = mm(e, xd, wdst[:], start=False)
                    last.then_inc(s_mm[k], 1)
                groups(pe, body)

            def softmax(k):
                nh = heads[k]
                if k >= 2:
                    pe.wait_ge(s_sm[k], mark[f"spread{k}"])
                    mm(PS[1][:, 0:1], right[:], dd[:, 0:1]).then_inc(s_smp[k], 1)
                for d in "fb":
                    pe.wait_ge(s_sm[k], mark[f"col{d}{k}"])
                    t.transpose(PS[0][0:nh, 0:P], colv[:, 0:nh], ident[:]).then_inc(s_smp[k], 1)
                    pe.wait_ge(s_sm[k], mark[f"row{d}{k}"])
                    t.transpose(PS[1][:, 0:nh], rowc[0:nh, :], ident[0:nh, 0:nh]).then_inc(s_smp[k], 1)
                pe.wait_ge(s_sm[k], mark[f"sums{k}"])
                pe.wait_ge(s_b[k], EG * (ET + 1) - 1)
                mm(PS[0][:, 0:D], left[:], H[:, J - 1, 0:D])
                mm(PS[0][:, D:D + nh], left[:], F[:, 0:nh, J - 1]).then_inc(s_smp[k], 1)

            def ext(m, to, xT, n):
                for i in range(n):
                    o = PS[to + i // 3][:, (i % 3) * EXT:(i % 3 + 1) * EXT]
                    mm(o, xT(i), wext[:, m, :], stop=False)
                    last = mm(o, ones_row[0:1, :], b2row[0:1, m, :], start=False)
                return last

            def slot_update(k):
                if k in (0, 4):
                    return

                def body(g, b, r, first):
                    if k == 1:
                        hold(pe, s_cv[1], g * CPER[1] + mark["agg1"])
                        for i in range(ET):
                            last = t.transpose(PS[0][:, i * P:(i + 1) * P], bufc[:, i, :], ident[:])
                        last.then_inc(s_cp[1], 1)
                        hold(pe, s_ca[1], g * CA[1] + 1)
                        for i in range(ET):
                            o = PS[2][:, i * D:(i + 1) * D]
                            mm(o, bufT[:, 0, i, :], wout[:], stop=False)
                            last = mm(o, ones_row[0:1, :], bo_row[0:1, :], start=False)
                        last.then_inc(s_cp[1], 1)
                    hold(pe, s_cv[k], g * CPER[k] + mark[f"xo{k}"])
                    for i in range(ET):
                        last = t.transpose(PS[1][:, i * P:(i + 1) * P], bufb[:, b, i, :], ident[:])
                    last.then_inc(s_cp[k], 1)
                    hold(pe, s_ca[k], g * CA[k] + (4 if k == 1 else 2))
                    ext(k - 1, 3, lambda i: bufT[:, 1, i, :], ET).then_inc(s_cp[k], 1)
                groups(pe, body)

            def dense(g, b, r, first):
                for m in range(3):
                    hold(pe, s_dv, g * DPER + (mark["dx2"] if m == 0 else mark[f"dm{m - 1}"]))
                    if m or not (isinstance(g, int) and g == 0):
                        hold(pe, s_da, g * DA + 8 * m + 3 if m else g * DA)
                    for i in range(NT):
                        xi = bufa[:, b, i, :] if m == 0 else bufc[:, i, :]
                        last = t.transpose(PS[i // 4][:, (i % 4) * P:(i % 4 + 1) * P], xi, ident[:])
                    last.then_inc(s_dp, 1)
                    hold(pe, s_da, g * DA + 8 * m + 5)
                    ext(m, 2, lambda i: bufT[:, 0, i, :], NT).then_inc(s_dp, 1)

            project(0)
            softmax(0)
            pe.wait_ge(s_sm[0], mark["cf0"])
            groups(pe, dense)
            pe.wait_ge(s_da, EG * DA)
            project(1)
            softmax(1)
            pe.wait_ge(s_sm[1], mark["cf1"])
            slot_update(1)
            for k in (2, 3, 4):
                pe.wait_ge(s_ca[k - 1], EG * CA[k - 1])
                softmax(k)
                pe.wait_ge(s_sm[k], mark[f"cf{k}"])
                slot_update(k)

            def message(g, b, r, first):
                hold(pe, s_ga[5][b], r * 128 + 128)
                hold(pe, s_el[b], r * 16 + 16)
                hold(pe, s_mv, g * MV + mark["srep"])
                for i in range(ET):
                    at = slice(i * P, (i + 1) * P)
                    t.transpose(PS[0][:, at], bufa[:, b, i, :], ident[:])
                    t.transpose(PS[1][:, at], bufa[:, b, ET + i, :], ident[:])
                    t.transpose(PS[2][0:64, at], eab[:, b, i, :], ident[:])
                    last = t.transpose(PS[3][:, at], srep[:, i, :], ident[:])
                last.then_inc(s_mp, 1)
                hold(pe, s_ma, g * MA + 3)
                for q in range(2):
                    o = PS[4 + q][:, :]
                    at = slice(q * P, (q + 1) * P)
                    mm(o, w31a[:, at], bufT[:, 0, 0:ET, :].rearrange("p j f -> p (j f)"), stop=False)
                    mm(o, w31b[:, at], bufT[:, 0, ET:2 * ET, :].rearrange("p j f -> p (j f)"), start=False, stop=False)
                    last = mm(o, w31c[:, at], eaT, start=False)
                last.then_inc(s_mp, 1)
                hold(pe, s_ma, g * MA + 5)
                for i in range(ET):
                    o = PS[6][:, i * D:(i + 1) * D]
                    mm(o, bufT[:, 1, i, :], w32s[:, 0, :], stop=False)
                    mm(o, bufT[:, 1, ET + i, :], w32s[:, 1, :], start=False, stop=False)
                    last = mm(o, ones_row[0:1, :], b32row[0:1, :], start=False)
                last.then_inc(s_mp, 1)
                hold(pe, s_ma, g * MA + 6)
                hold(pe, s_mv, g * MV + mark["same"])
                for i in range(ET):
                    last = mm(PS[7][:, i * D:(i + 1) * D], bufc[:, i, :], bufd[:, i, :])
                last.then_inc(s_mp, 1)
            groups(pe, message)

        @block.gpsimd
        def _(pool):
            q = nc.gpsimd
            c = Chain(pool, s_pset)
            c.link(q.memset(ident[:], 0.0))
            c.inc(q.affine_select(out=ident[:], in_=ident[:], compare_op=ALU.not_equal, fill=1.0, base=0,
                                  pattern=[[-1, P]], channel_multiplier=1))
            c.link(q.memset(tri[:], 1.0))
            c.inc(q.affine_select(out=tri[:], in_=tri[:], compare_op=ALU.is_gt, fill=0.0, base=0,
                                  pattern=[[-1, P]], channel_multiplier=1))
            c.inc(q.iota(slot_i[:], pattern=[[1, J]], base=0, channel_multiplier=J))
            c.inc(q.iota(node_i[:], pattern=[[1, NPAD // P]], base=SLOTS, channel_multiplier=NPAD // P))
            c.inc(q.memset(kfn[:], -1))
            c.inc(q.memset(b2row[:], 0.0))
            c.inc(q.memset(ones_row[:], 1.0))
            c.sync()
            pool.wait_ge(s_vset, mark["lr"])
            c.inc(q.affine_select(out=left[:], in_=left[:], compare_op=ALU.is_gt, fill=0.0, base=0,
                                  pattern=[[1, P]], channel_multiplier=-1))
            c.inc(q.affine_select(out=right[:], in_=right[:], compare_op=ALU.is_gt, fill=0.0, base=0,
                                  pattern=[[-1, P]], channel_multiplier=1))
            c.link(q.iota(spare_i[:], pattern=[[0, 1]], base=N_NODES, channel_multiplier=1))
            pool.wait_ge(s_vset, mark["setup"])

            def fetch(table, idx, to, cur_, b, sem_):
                for i in range(ET):
                    q.indirect_dma_start(out=to(i), out_offset=None, in_=table,
                                         in_offset=bass.IndirectOffsetOnAxis(ap=cur_[:, b, i:i + 1], axis=0)
                                         ).then_inc(sem_, 16)

            def gather2(k, table, isrc, idst, free):
                def body(g, b, r, first):
                    c = Chain(pool, s_gi[k])
                    c.start(g, 2)
                    if not first:
                        hold(pool, s_ga[k][b], r * 128)
                        free(g, b, r)
                    c.inc(q.tensor_copy(cur[:, b, :], isrc[:, bass.ds(g * ET, ET)]))
                    c.inc(q.tensor_copy(cur2[:, b, :], idst[:, bass.ds(g * ET, ET)]))
                    c.sync()
                    fetch(table, None, lambda i: bufa[:, b, i, :], cur, b, s_ga[k][b])
                    fetch(table, None, lambda i: bufa[:, b, ET + i, :], cur2, b, s_ga[k][b])
                return body

            def free0(g, b, r):
                hold(pool, s_tr[0], g - 1)
                hold(pool, s_xst[b], r * 16)
            groups(pool, gather2(0, x[:, :], src_i, dstc, free0))

            pool.wait_ge(s_slots, 16)
            for b in range(2):
                pool.wait_ge(s_ga[0][b], (PAIRS + 1 - b) * 128)

            def scatter_slots(g, b, r, first):
                c = Chain(pool, s_scq)
                c.start(g, 2)
                if not first:
                    hold(pool, s_scat[b], r * 64)
                c.inc(q.tensor_copy(cur[:, b, :], dscat[:, bass.ds(g * ET, ET)]))
                c.inc(q.tensor_copy(cur2[:, b, :], slot_i[:, bass.ds(g * ET, ET)]))
                c.sync()
                for i in range(ET):
                    q.indirect_dma_start(out=slot_of_node[:, :], out_offset=bass.IndirectOffsetOnAxis(ap=cur[:, b, i:i + 1], axis=0),
                                         in_=cur2[:, b, i:i + 1], in_offset=None, bounds_check=N_NODES - 1,
                                         oob_is_err=False).then_inc(s_scat[b], 16)
            groups(pool, scatter_slots)
            for b in range(2):
                pool.wait_ge(s_scat[b], (PAIRS + 1 - b) * 64)

            def look_up(g, b, r, first):
                c = Chain(pool, s_mapq)
                c.start(g, 2, -g if first else -2)
                if not first:
                    hold(pool, s_gmap[b], r * 64)
                    c.inc(q.tensor_copy(gsrc[:, bass.ds(g * ET - 2 * ET, ET)], cur2[:, b, :]))
                c.inc(q.tensor_copy(cur[:, b, :], src_i[:, bass.ds(g * ET, ET)]))
                c.sync()
                fetch(slot_of_node[:, :], None, lambda i: cur2[:, b, i:i + 1], cur, b, s_gmap[b])
            groups(pool, look_up)
            for g in (EG - 2, EG - 1):
                b = g % 2
                pool.wait_ge(s_gmap[b], (PAIRS + 1 - b) * 64)
                q.tensor_copy(gsrc[:, g * ET:(g + 1) * ET], cur2[:, b, :]).then_inc(s_mapq, 1)
            pool.wait_ge(s_mapq, 2 * EG)

            def stored(k):
                for b in range(2):
                    pool.wait_ge(s_cs[k][b], (PAIRS + 1 - b) * CST[k])

            stored(0)
            for b in range(2):
                pool.wait_ge(s_dx1[b], (PAIRS + 1 - b) * 16)
                pool.wait_ge(s_dx3[b], (PAIRS + 1 - b) * 32)
            for m in range(3):
                pool.wait_ge(s_dt2[m], EG * 16)
            groups(pool, gather2(1, t1[:, :], gsrc, gdst, lambda g, b, r: hold(pool, s_tr[1], g - 1)))
            for b in range(2):
                pool.wait_ge(s_ga[1][b], (PAIRS + 1 - b) * 128)
            for k in (2, 3, 4):
                stored(k - 1)

                def gather1(g, b, r, first, k=k):
                    c = Chain(pool, s_gi[k])
                    c.start(g, 1)
                    if not first:
                        hold(pool, s_ga[k][b], r * 64)
                        hold(pool, s_he[k], g - 1)
                    c.link(q.tensor_copy(cur[:, b, :], gsrc[:, bass.ds(g * ET, ET)]))
                    fetch(t2[k - 2][:, :], None, lambda i: gbuf[:, b, i, :], cur, b, s_ga[k][b])
                groups(pool, gather1)
                for b in range(2):
                    pool.wait_ge(s_ga[k][b], (PAIRS + 1 - b) * 64)

            pool.wait_ge(s_accp, 16)

            def scatter_acc(g, b, r, first):
                c = Chain(pool, s_asq)
                c.start(g, 1)
                if not first:
                    hold(pool, s_asc[b], r * 64)
                c.link(q.tensor_copy(cur[:, b, :], dscat[:, bass.ds(g * ET, ET)]))
                hold(pool, s_cv[4], g * CPER[4] + mark["xo4"])
                for i in range(ET):
                    q.indirect_dma_start(out=acc[:, :], out_offset=bass.IndirectOffsetOnAxis(ap=cur[:, b, i:i + 1], axis=0),
                                         in_=bufb[:, b, i, :], in_offset=None, bounds_check=N_NODES - 1,
                                         oob_is_err=False).then_inc(s_asc[b], 16)
            groups(pool, scatter_acc)
            for b in range(2):
                pool.wait_ge(s_asc[b], (PAIRS + 1 - b) * 64)
            stored(4)

            g2 = gather2(5, t3[:, :], gsrc, gdst, lambda g, b, r: hold(pool, s_mp, g * MP - 2 * MP + 1))

            def add(g, b, r, first):
                hold(pool, s_ma, g * MA + MA)
                hold(pool, s_mv, g * MV + mark["idx"])
                for i in range(ET):
                    q.indirect_dma_start(out=acc[:, :], out_offset=bass.IndirectOffsetOnAxis(ap=idx_add[:, b, i:i + 1], axis=0),
                                         in_=bufb[:, b, i, :], in_offset=None, compute_op=ALU.add).then_inc(s_add, 16)
                    hold(pool, s_add, g * 64 + i * 16 + 16)
            load_store(g2, add, pool)

        @block.sync
        def _(sp):
            n_loads = [0]

            def load(to, of, slow=False):
                n_loads[0] += 1
                sp.dma_start(to, of, allow_slow_non_contiguous=slow).then_inc(s_ld, 16)
            load(src_i[:], src)
            load(dst_i[:], dst)
            load(lew[:], ew)
            load(w0[:, 0:D], w0t)
            load(wa_bc[:], w_attn.unsqueeze(0).broadcast_to([P, HD]))
            load(bias_bc[:], bias0.unsqueeze(0).broadcast_to([P, D]))
            load(wsrc[:], w_src)
            load(wdst[:], w_dst)
            load(attn_bc[:], attn.unsqueeze(0).broadcast_to([P, D]))
            load(wout[:], w_out)
            load(bo_row[:], b_out.unsqueeze(0))
            load(bo_bc[:], b_out.unsqueeze(0).broadcast_to([P, D]))
            load(gam_bc[:], gamma.unsqueeze(0).broadcast_to([P, D]))
            load(bet_bc[:], beta.unsqueeze(0).broadcast_to([P, D]))
            load(wext[:, :, 0:D], w2.rearrange("m k n -> k m n"))
            load(av[:, :, 0, :], a_src.unsqueeze(0).broadcast_to([P, 3, D]))
            load(av[:, :, 1, :], a_dst.unsqueeze(0).broadcast_to([P, 3, D]))
            load(w31a[:], w31[0:D, :])
            load(w31b[:], w31[D:2 * D, :])
            load(w31c[:], w31[2 * D:2 * D + 64, :])
            load(b31c[:], b31)
            load(w32s[:], w32.rearrange("(t p) n -> p t n", p=P))
            load(b32row[:], b32.unsqueeze(0))
            sp.wait_ge(s_pset, 9)
            load(b2row[:, :, 0:D], b2.unsqueeze(0))
            load(kfn[0:P - 1, 0:1], dst[1:P, 0:1], slow=True)
            load(kfn[1:P, 1:2], dst[0:P - 1, J - 1:J], slow=True)
            load(spare_pad[:], b_out.unsqueeze(0))
            assert n_loads[0] == N_LOADS
            sp.dma_start(slot_of_node.rearrange("(p c) w -> p (c w)", p=P), node_i[:]).then_inc(s_slots, 16)
            sp.dma_start(acc[N_NODES:N_NODES + P, :], ident[:]).then_inc(s_accp, 16)

            def keep_dst(g, b, r, first):
                hold(sp, s_ga[0][b], r * 128 + 128)
                sp.dma_start(rows4(x0_dst, g), bufa[:, b, ET:2 * ET, :]).then_inc(s_xst[b], 16)
            groups(sp, keep_dst)

            def all_of(pair, per):
                for b in range(2):
                    sp.wait_ge(pair[b], (PAIRS + 1 - b) * per)

            def slots(k):
                def load_(g, b, r, first):
                    if not first:
                        hold(sp, s_cv[k], g * CPER[k] - CPER[k])
                    def get(to, of):
                        sp.dma_start(to, rows4(of, g)).then_inc(s_cl[k][b], 16)
                    get(bufa[:, b, 0:ET, :], [x0_dst, t1, x2s[0], x2s[1], x2s[2]][k])
                    if k >= 2:
                        get(gbuf[:, b, :, :], t2[k - 2])
                    if k == 4:
                        get(bufa[:, b, ET:2 * ET, :], x2s[0])

                def store(g, b, r, first):
                    hold(sp, s_cv[k], g * CPER[k] + mark[f"xo{k}"])
                    sp.dma_start(rows4([t1, x2s[0], x2s[1], x2s[2], t3][k], g), bufb[:, b, 0:ET, :]).then_inc(s_cs[k][b], 16)
                    if k in (1, 2, 3):
                        hold(sp, s_ca[k], g * CA[k] + CA[k])
                        sp.dma_start(rows4(t2[k - 1], g), trow[:, b, 0:ET, :]).then_inc(s_cs[k][b], 16)
                load_store(load_, store, sp)

            sp.wait_ge(s_tr[0], EG)
            all_of(s_xst, 16)
            slots(0)
            all_of(s_cs[0], CST[0])
            sp.wait_ge(s_cv[0], EG * CPER[0])

            def dense_load(g, b, r, first):
                parts = TAIL if isinstance(g, int) and g == EG - 1 else P
                if not first:
                    hold(sp, s_dx3[b], r * 32)
                sp.dma_start(bufa[0:parts, b, :, :], node_rows(x, g, 0, parts)).then_inc(s_dl[b], 16)

            def dense_store(g, b, r, first):
                parts = TAIL if isinstance(g, int) and g == EG - 1 else P
                hold(sp, s_dv, g * DPER + mark["dx1"])
                sp.dma_start(node_rows(t1, g, SLOTS, parts), bufb[0:parts, b, :, :]).then_inc(s_dx1[b], 16)
                for m in range(3):
                    hold(sp, s_da, g * DA + 8 * m + 11)
                    sp.dma_start(node_rows(t2[m], g, SLOTS, parts), trow[0:parts, m, :, :]).then_inc(s_dt2[m], 16)
                hold(sp, s_dv, g * DPER + mark["dx3"])
                sp.dma_start(node_rows(t3, g, SLOTS, parts), bufa[0:parts, b, :, :]).then_inc(s_dx3[b], 16)
                sp.dma_start(node_rows(acc, g, 0, parts), bufa[0:parts, b, :, :]).then_inc(s_dx3[b], 16)
            load_store(dense_load, dense_store, sp)

            sp.wait_ge(s_tr[1], EG)
            slots(1)
            for k in (2, 3, 4):
                all_of(s_cs[k - 1], CST[k - 1])
                sp.wait_ge(s_cv[k - 1], EG * CPER[k - 1])
                sp.wait_ge(s_he[k], EG)
                slots(k)

            def edge_attr(g, b, r, first):
                if not first:
                    hold(sp, s_mp, g * MP - 2 * MP + 1)
                sp.dma_start(eab[:, b, :, :], rows4(ea, g)).then_inc(s_el[b], 16)
            groups(sp, edge_attr)

            sp.wait_ge(s_add, EG * 64)
            sp.wait_ge(s_mp, EG * MP)

            def final_load(g, b, r, first):
                parts = TAIL if isinstance(g, int) and g == EG - 1 else P
                if not first:
                    hold(sp, s_fv, g * FPER - FPER)
                sp.dma_start(bufa[0:parts, b, :, :], node_rows(acc, g, 0, parts)).then_inc(s_fl[b], 16)

            def final_store(g, b, r, first):
                parts = TAIL if isinstance(g, int) and g == EG - 1 else P
                hold(sp, s_fv, g * FPER + FPER)
                sp.dma_start(node_rows(out, g, 0, parts), bufb[0:parts, b, :, :]).then_inc(s_fs[b], 16)
            load_store(final_load, final_store, sp)
            all_of(s_fs, 16)
            all_of(s_el, 16)


def kernel(**inputs):
    import numpy as np
    import concourse.bacc as bacc
    from concourse.bass_utils import run_bass_kernel_spmd

    def slots(name, fill):
        a = np.asarray(inputs[name])
        pad = np.full((SLOTS - N_EDGES,) + a.shape[1:], fill, a.dtype)
        return np.concatenate([a, pad])

    arrays = {
        "x": inputs["x"],
        "src": slots("src", 0).reshape(P, J),
        "dst": slots("dst", N_NODES).reshape(P, J),
        "ew": slots("edge_weight", 0).reshape(P, J),
        "ea": slots("edge_attr_64", 0),
        "w0t": np.asarray(inputs["L0_gnn_W_fc"]).T,
        "w_attn": inputs["L0_gnn_w_attn"],
        "bias0": inputs["L0_gnn_bias"],
        "w_src": inputs["L1_gnn_W_src"],
        "w_dst": inputs["L1_gnn_W_dst"],
        "attn": np.asarray(inputs["L1_gnn_attn"]).reshape(-1),
        "w_out": inputs["L1_gnn_W_out"],
        "b_out": inputs["L1_gnn_b_out"],
        "gamma": inputs["L1_gnn_gamma"],
        "beta": inputs["L1_gnn_beta"],
        "w2": inputs["L2_gnn_Ws"],
        "a_src": inputs["L2_gnn_att_src"],
        "a_dst": inputs["L2_gnn_att_dst"],
        "b2": inputs["L2_gnn_bias"],
        "w31": inputs["L3_gnn_W1"],
        "b31": np.asarray(inputs["L3_gnn_b1"]).reshape(2, P).T,
        "w32": inputs["L3_gnn_W2"],
        "b32": inputs["L3_gnn_b2"],
    }
    nc = bacc.Bacc("TRN2", target_bir_lowering=False, num_devices=1)
    fed, aps = {}, {}
    for name, a in arrays.items():
        a = np.ascontiguousarray(a)
        fed[f"in_{name}"] = a
        aps[name] = nc.dram_tensor(f"in_{name}", a.shape, mybir.dt.from_np(a.dtype), kind="ExternalInput").ap()
    aps["out"] = nc.dram_tensor("out_0", (N_NODES, D), fp32, kind="ExternalOutput").ap()
    build(nc, **aps)
    r = run_bass_kernel_spmd(nc, [fed], core_ids=[0])
    return r.results[0]["out_0"]
```

```python
import concourse.bass as bass
from concourse import mybir
from contextlib import ExitStack

fp32 = mybir.dt.float32
i32 = mybir.dt.int32
bf16 = mybir.dt.bfloat16
ALU = mybir.AluOpType
ACT = mybir.ActivationFunctionType
AX = mybir.AxisListType

P = 128
N_NODES = 50000
N_EDGES = 25000
D = 128
HEADS = 8
HD = D // HEADS
J = -(-N_EDGES // P)
SLOTS = P * J
ET = 4
EG = J // ET
NT = 8
NGRP = -(-N_NODES // (P * NT))
NPAD = NGRP * P * NT
TAIL = (N_NODES - (NGRP - 1) * P * NT) // NT
EXT = D + 2
ROWS = SLOTS + N_NODES
SKIP = 60000
BIG = 1.0e38
LN_EPS = 1e-5
assert EG == NGRP and EG % 2 == 1
PAIRS = EG // 2


class Chain:

    def __init__(self, eng, sem):
        self.base = sem.base if isinstance(sem, From) else 0
        self.sem = sem.sem if isinstance(sem, From) else sem
        self.eng, self.off, self.n = eng, self.base, 0

    def start(self, g, per, shift=0):
        self.off, self.n, self.per = g * per + (shift + self.base), 0, per

    def finish(self):
        assert self.n == self.per, (self.n, self.per)

    def inc(self, ins):
        self.n += 1
        ins.then_inc(self.sem, 1)

    def sync(self):
        hold(self.eng, self.sem, self.off + self.n)

    def fused(self):
        self.eng.wait_ge(self.sem, self.off + self.n)

    def link(self, ins):
        self.inc(ins)
        self.sync()


class From:

    def __init__(self, sem, base):
        self.sem, self.base = sem, base


def hold(eng, sem, value):
    if isinstance(sem, From):
        sem, value = sem.sem, value + sem.base
    eng.wait_ge(sem, value)
    if not isinstance(value, int):
        eng.nop(nofuse=True)


def load_store(load, store, eng):
    load(0, 0, 0, True)
    load(1, 1, 0, True)
    for g in range(2):
        store(g, g, 0, True)
        load(g + 2, g, 1, False)
    with eng.Fori(1, PAIRS - 1) as t:
        for b in range(2):
            store(t * 2 + b, b, t, False)
            load(t * 2 + b + 2, b, t + 1, False)
    store(EG - 3, 0, PAIRS - 1, False)
    load(EG - 1, 0, PAIRS, False)
    store(EG - 2, 1, PAIRS - 1, False)
    store(EG - 1, 0, PAIRS, False)


def skewed(eng, parts):
    top = max(lag for _, lag in parts)
    start = (top + 3) // 2 * 2

    def one(s):
        for part, lag in parts:
            g = s - lag
            if 0 <= g < EG:
                part(g, g % 2, g // 2, g < 2)
    for s in range(start):
        one(s)
    with eng.Fori(start // 2, PAIRS) as t:
        for q in range(2):
            for part, lag in parts:
                b = (q - lag) % 2
                part(t * 2 + (q - lag), b, t + (q - lag - b) // 2, False)
    for s in range(EG - 1, EG + top):
        one(s)


def groups(eng, body):
    body(0, 0, 0, True)
    body(1, 1, 0, True)
    with eng.Fori(1, PAIRS) as t:
        body(t * 2, 0, t, False)
        body(t * 2 + 1, 1, t, False)
    body(EG - 1, 0, PAIRS, False)


def build(nc, x, src, dst, ew, ea, w0t, w_attn, bias0, w_src, w_dst, attn, w_out, b_out, gamma, beta,
          w2, a_src, a_dst, b2, w31, b31, w32, b32, out):
    ctx = ExitStack()
    with ctx:
        def sb(name, shape, dt=fp32):
            return ctx.enter_context(nc.sbuf_tensor(name, shape, dt))

        def sem(name):
            return ctx.enter_context(nc.semaphore(name))

        def two(name):
            return [sem(f"{name}{b}") for b in range(2)]

        def dram(name, shape, dt=fp32):
            return nc.dram_tensor(name, shape, dt, kind="Internal").ap()

        slot_of_node = dram("slot_of_node", (NPAD, 1), i32)
        x0_dst = dram("x0_dst", (SLOTS, D))
        t1 = dram("t1", (ROWS, D))
        x2s = [dram(f"x2s{m}", (SLOTS, D)) for m in range(3)]
        t2 = [dram(f"t2_{m}", (ROWS, EXT)) for m in range(3)]
        t3 = dram("t3", (ROWS, D))
        acc = dram("acc", (N_NODES + P, D))

        ident = sb("ident", [P, P])
        ones3 = sb("ones3", [3, P], bf16)
        zero = sb("zero", [P, 1])
        one = sb("one", [P, 1])
        tri = sb("tri", [P, P])
        src_i = sb("src_i", [P, J], i32)
        dst_i = sb("dst_i", [P, J], i32)
        key = sb("key", [P, J])
        src_f = sb("src_f", [P, J])
        lew = sb("lew", [P, J])
        cont = sb("cont", [P, J + 1])
        pen = sb("pen", [P, J + 1])
        firstm = sb("firstm", [P, J])
        firstpen = sb("firstpen", [P, J])
        lastpen = sb("lastpen", [P, J])
        lastm = sb("lastm", [P, J])
        endm = sb("endm", [P, J])
        endpen = sb("endpen", [P, J])
        kfn = sb("kfn", [P, 2], i32)
        kx = sb("kx", [P, 2])
        cols = sb("cols", [P, 6])
        crep = sb("crep", [P, 4, 8])
        rows = sb("rows", [8, 4, P])
        slot_i = sb("slot_i", [P, J], i32)
        gsrc = sb("gsrc", [P, J], i32)
        gdst = sb("gdst", [P, J], i32)
        dscat = sb("dscat", [P, J], i32)
        left = sb("left", [P, P])
        right = sb("right", [P, P])
        node_i = sb("node_i", [P, NPAD // P], i32)
        cur = sb("cur", [P, 2, ET], i32)
        cur2 = sb("cur2", [P, 2, ET], i32)
        dstc = sb("dstc", [P, J], i32)

        w0 = sb("w0", [P, D + HEADS])
        wa_bc = sb("wa_bc", [P, HD])
        wsrc = sb("wsrc", [P, D])
        wdst = sb("wdst", [P, D])
        attn_bc = sb("attn_bc", [P, D])
        wout = sb("wout", [P, D])
        bias_bc = sb("bias_bc", [P, D])
        bo_bc = sb("bo_bc", [P, D])
        gam_bc = sb("gam_bc", [P, D])
        bet_bc = sb("bet_bc", [P, D])
        wext = sb("wext", [P, 3, EXT])
        brow = sb("brow", [3, 5, EXT])
        b3 = sb("b3", [3, 5, EXT], bf16)
        w31a = sb("w31a", [P, 2 * D])
        w31b = sb("w31b", [P, 2 * D])
        w31c = sb("w31c", [64, 2 * D])
        b31c = sb("b31c", [P, 2])
        w32s = sb("w32s", [P, 2, D])

        H = sb("H", [P, J, EXT])
        S = sb("S", [P, HEADS, J])
        F = sb("F", [P, HEADS, J])
        B = sb("B", [P, HEADS, J])
        colv = sb("colv", [P, HEADS])
        colc = sb("colc", [P, HEADS])
        rowd = sb("rowd", [HEADS, P])
        rowc = sb("rowc", [HEADS, P])
        Cf = sb("Cf", [P, D + HEADS])
        es = sb("es", [P, J])
        dd = sb("dd", [P, J])
        sdt = sb("sdt", [P, J, 2])
        slot_f = sdt[:, 0:J // 2, :].rearrange("p j c -> p (j c)")
        bufa = sb("bufa", [P, 2, NT, D])
        bufb = sb("bufb", [P, 2, NT, D])
        bufc = sb("bufc", [P, NT, D])
        bufd = sb("bufd", [P, NT, D])
        bufT = sb("bufT", [P, 2, NT, D])
        trow = sb("trow", [P, 3, NT, EXT])
        gbuf = sb("gbuf", [P, 2, ET, EXT])
        av = bufb[:, 0, 0:6, :].rearrange("p (m t) f -> p m t f", m=3)
        w0a = bufd[:, 2, :]
        eab = trow[:, 0:2, :, :].rearrange("p b r e -> p b (r e)")[:, :, 0:ET * 64].rearrange(
            "p b (j f) -> p b j f", f=64)
        eaT = trow[0:64, 2, :, :].rearrange("p r e -> p (r e)")[:, 0:ET * P]
        srep = bufd[:, ET:2 * ET, :]
        cnt = sb("cnt", [P, ET])
        idf = sb("idf", [P, ET])
        idx_add = sb("idx_add", [P, 2, ET], i32)
        real = sb("real", [P, J])
        spare = sb("spare", [P, 1])
        spare_i = sb("spare_i", [P, 1], i32)
        st = sb("st", [P, 4, NT, 6])
        mvs = sb("mvs", [P, 4, 2, NT, 2])
        rs = sb("rs", [P, 4, 2, NT])
        nmr = sb("nmr", [P, 2, NT])
        half = sb("half", [P, NT])
        Hflat = H[:, :, :].rearrange("p j e -> p (j e)")
        n_dense = [0]

        def dense_buf(n):
            at = n_dense[0]
            n_dense[0] += n * NT * D
            return Hflat[:, at:at + n * NT * D].rearrange("p (b r f) -> p b r f", b=n, f=D)
        dx, da, dx1, dy, dt_, dx2, dxm, dx3 = (dense_buf(n) for n in (2, 2, 2, 1, 2, 2, 2, 2))
        dsig, dT = dense_buf(3), dense_buf(3)
        PS = [ctx.enter_context(nc.psum_tensor(f"ps{i}", [P, 512], fp32)) for i in range(8)]

        def bc(ap, n):
            return ap.unsqueeze(1).broadcast_to([P, n, D])

        def rows4(ap, g):
            return ap[0:SLOTS, :].rearrange("(p j) w -> p j w", p=P)[:, bass.ds(g * ET, ET), :]

        def node_rows(ap, g, off=0, parts=P):
            return ap[bass.ds(off + g * (P * NT), parts * NT), :].rearrange("(p r) w -> p r w", r=NT)

        s_ld = sem("s_loads")
        s_pset = sem("s_pool_setup")
        s_vset = sem("s_dve_setup")
        s_eset = sem("s_pe_setup")
        s_aset = sem("s_act_setup")
        s_slots = sem("s_slot_table_set")
        s_scat = two("s_slots_scattered")
        s_gmap = two("s_rows_looked_up")
        K6, K5 = range(6), range(5)
        s_ga = [two(f"s_gathered{k}_") for k in K6]
        s_idx = sem("s_indices_copied")
        at = [0]

        def idx(n):
            at[0] += n * EG
            return From(s_idx, at[0] - n * EG)
        gi0, s_scq, s_mapq, gi1, gi2, gi3, gi4, s_asq, gi5 = (idx(n) for n in (2, 2, 2, 2, 1, 1, 1, 1, 2))
        s_gi = [gi0, gi1, gi2, gi3, gi4, gi5]
        s_tr = [sem(f"s_transposed{k}") for k in (0, 1)]
        s_ev = [sem(f"s_evacuated{k}") for k in (0, 1)]
        s_mm = [sem(f"s_projected{k}") for k in (0, 1)]
        s_he = [sem(f"s_h_kept{k}") for k in K5]
        s_sv = [sem(f"s_scored{k}") for k in (0, 1)]
        s_xst = two("s_x0dst_stored")
        s_sm = [sem(f"s_softmax{k}") for k in K5]
        s_moved, s_exp, s_scan = sem("s_softmax_moved"), sem("s_softmax_exp"), sem("s_scanned")
        s_smp = [From(s_moved, n) for n in (0, 5, 10, 16, 22)]
        s_sme = [From(s_exp, n) for n in (0, 1, 2, 4, 6)]
        s_b = [From(s_scan, k * (EG * (ET + 1) - 1)) for k in K5]
        s_cl = [two(f"s_slots_loaded{k}_") for k in K5]
        s_agg = [sem(f"s_aggregated{k}") for k in K5]
        s_y = {k: sem(f"s_slot_y{k}") for k in (1, 4)}
        s_z = sem("s_slot_z")
        s_xo = [sem(f"s_slot_out{k}") for k in K5]
        s_sg = {k: sem(f"s_slot_sigmoid{k}") for k in (2, 3, 4)}
        s_ct = {k: sem(f"s_slot_turned{k}") for k in (1, 2, 3)}
        s_ce = {k: sem(f"s_slot_T_kept{k}") for k in (1, 2, 3)}
        s_cm = {k: sem(f"s_slot_rows{k}") for k in (1, 2, 3)}
        s_cr = {k: sem(f"s_slot_rows_kept{k}") for k in (1, 2, 3)}
        s_wt, s_we, s_wm = sem("s_agg_turned"), sem("s_agg_T_kept"), sem("s_wout_product")
        s_rc = {k: sem(f"s_slot_rstd{k}") for k in (0, 1, 4)}
        s_rc2 = sem("s_slot_rstd_second")
        s_cs = [two(f"s_slots_stored{k}_") for k in K5]
        s_asc = two("s_acc_rows_scattered")
        s_accp = sem("s_acc_padding")
        s_dl = two("s_nodes_loaded")
        s_da_ = sem("s_dense_a")
        s_dtt = sem("s_dense_t")
        s_A = [sem(f"s_dense_A{n}") for n in range(5)]
        s_Bm = [sem(f"s_dense_B{m}") for m in range(3)]
        s_rd = [sem(f"s_dense_rstd{n}") for n in range(4)]
        s_dT = [sem(f"s_dense_turned{m}") for m in range(3)]
        s_dE = [sem(f"s_dense_T_kept{m}") for m in range(3)]
        s_dM = [sem(f"s_dense_product{m}") for m in range(3)]
        s_dS = [sem(f"s_dense_sigmoid{m}") for m in range(3)]
        s_dR = [sem(f"s_dense_rows_kept{m}") for m in range(3)]
        s_dN = sem("s_dense_x3")
        s_dx1 = two("s_x1_stored")
        s_dx3 = two("s_x3_stored")
        s_dt2 = [sem(f"s_t2_stored{m}") for m in range(3)]
        s_el = two("s_edge_attr_loaded")
        s_ma = sem("s_message_act")
        s_mp = sem("s_message_pe")
        s_mv = sem("s_message_dve")
        s_add = sem("s_messages_added")
        s_fl = two("s_final_loaded")
        s_fs = two("s_final_stored")
        s_fv = sem("s_final_dve")
        s_fv2 = sem("s_final_out")
        s_fr = sem("s_final_rstd")

        CLD = [16, 16, 32, 32, 48]
        CST = [16, 32, 32, 32, 16]
        MA, MP, MV = 7, 4, 13
        AGG = [4 + 1 + 2 + 2 * ET, 5, 9, 9, 9]
        XO = [ET, ET, 1, 1, ET]
        Z1 = 1 + ET + 2 + 2 * ET
        DA1, DA2, DA3, DA4 = 2 * NT, 1 + NT + 2 * NT, NT + 2 + 2 * NT, NT
        DB = [1, 1, 2 + 2 * NT]
        mark = {}
        block = ctx.enter_context(nc.Block())
        N_LOADS = 26
        heads = [HEADS, HEADS, 1, 1, 1]

        @block.vector
        def _(dve):
            v = nc.vector
            c = Chain(dve, s_vset)

            for t, val in ((half, -0.5), (zero, 0.0), (one, 1.0)):
                c.inc(v.memset(t[:], val))
            c.inc(v.memset(cont[:], 0.0))
            dve.wait_ge(s_ld, 16 * N_LOADS)
            c.inc(v.tensor_copy(key[:], dst_i[:]))
            c.inc(v.tensor_copy(src_f[:], src_i[:]))
            c.inc(v.tensor_copy(kx[:], kfn[:]))
            dve.wait_ge(s_pset, 5)
            c.inc(v.tensor_copy(slot_f[:], slot_i[:]))
            c.sync()
            kf, kl = key[:, 0:1], key[:, J - 1:J]
            c.inc(v.tensor_tensor(cont[:, 1:J], key[:, 1:J], key[:, 0:J - 1], ALU.is_equal))
            c.inc(v.tensor_scalar(firstm[:], key[:], kf, None, ALU.is_equal))
            c.inc(v.tensor_scalar(lastm[:], key[:], kl, None, ALU.is_equal))
            c.inc(v.tensor_scalar(dstc[:], key[:], float(N_NODES - 1), None, ALU.min))
            c.inc(v.tensor_tensor(cols[:, 0:1], kf, kx[:, 1:2], ALU.is_equal))
            c.inc(v.tensor_tensor(cols[:, 1:2], kf, kl, ALU.is_equal))
            c.inc(v.tensor_tensor(cols[:, 2:3], kl, kx[:, 0:1], ALU.is_equal))
            c.sync()
            c.inc(v.tensor_scalar(pen[:], cont[:], 1.0, BIG, ALU.subtract, ALU.mult))
            c.inc(v.tensor_scalar(firstpen[:], firstm[:], 1.0, BIG, ALU.subtract, ALU.mult))
            c.inc(v.tensor_scalar(lastpen[:], lastm[:], 1.0, BIG, ALU.subtract, ALU.mult))
            c.inc(v.tensor_tensor(cols[:, 3:4], cols[:, 0:1], cols[:, 1:2], ALU.mult))
            c.inc(v.tensor_tensor(cols[:, 4:5], cols[:, 2:3], cols[:, 1:2], ALU.mult))
            c.inc(v.tensor_scalar(endm[:], cont[:, 1:J + 1], -1.0, 1.0, ALU.mult, ALU.add))
            c.sync()
            c.link(v.tensor_scalar(endm[:, J - 1:J], cols[:, 2:3], -1.0, 1.0, ALU.mult, ALU.add))
            c.inc(v.tensor_scalar(endpen[:], endm[:], 1.0, BIG, ALU.subtract, ALU.mult))
            c.inc(v.tensor_scalar(dd[:], key[:], float(SKIP), None, ALU.subtract))
            for n, q in enumerate((3, 0, 4, 2)):
                c.inc(v.tensor_scalar(crep[:, n, :], cols[:, q:q + 1].broadcast_to([P, 8]), 1.0, BIG,
                                      ALU.subtract, ALU.mult))
            c.inc(v.tensor_copy(bufc[:, 0, :], kf.broadcast_to([P, P])))
            c.inc(v.tensor_copy(bufc[:, 1, :], kl.broadcast_to([P, P])))
            c.sync()
            mark["rep"] = c.n
            c.link(v.tensor_tensor(dd[:], dd[:], endm[:], ALU.mult))
            c.inc(v.tensor_scalar(dscat[:], dd[:], float(SKIP), None, ALU.add))
            dve.wait_ge(s_eset, 1)
            c.inc(v.tensor_scalar(left[:], PS[0][:, 0:P], kl, None, ALU.is_equal))
            c.inc(v.tensor_scalar(right[:], PS[0][:, P:2 * P], kf, None, ALU.is_equal))
            c.link(v.tensor_copy(rows[:], PS[1][0:8, :].rearrange("h (n p) -> h n p", n=4)))
            mark["lr"] = c.n
            c.link(v.tensor_tensor(w0a.rearrange("p (h f) -> p h f", f=HD),
                                   w0[:, 0:D].rearrange("p (h f) -> p h f", f=HD),
                                   wa_bc[:].unsqueeze(1).broadcast_to([P, HEADS, HD]), ALU.mult))
            c.inc(v.tensor_reduce(w0[:, D:D + HEADS], w0a.rearrange("p (h f) -> p h f", f=HD), AX.X, ALU.add))
            for m in range(3):
                c.link(v.tensor_tensor(bufd[:, 0:2, :], wext[:, m, 0:D].unsqueeze(1).broadcast_to([P, 2, D]),
                                       av[:, m, :, :], ALU.mult))
                c.link(v.tensor_reduce(wext[:, m, D:EXT], bufd[:, 0:2, :], AX.X, ALU.add))

            t0, t1_, hi = (Hflat[0:3, n * 5 * EXT:(n + 1) * 5 * EXT].rearrange("p (n e) -> p n e", e=EXT)
                           for n in range(3))
            c.link(v.tensor_copy(b3[:], brow[:]))
            c.inc(v.tensor_copy(hi, b3[:]))
            c.sync()
            c.link(v.tensor_tensor(t0, brow[:], hi, ALU.subtract))
            c.link(v.tensor_scalar(brow[:], hi, ident[0:3, 0:1], None, ALU.mult))
            c.link(v.tensor_copy(b3[:], t0))
            c.link(v.tensor_copy(hi, b3[:]))
            c.link(v.tensor_tensor(t1_, t0, hi, ALU.subtract))
            c.link(v.scalar_tensor_tensor(brow[:], hi, ident[0:3, 1:2], brow[:], ALU.mult, ALU.add))
            c.link(v.scalar_tensor_tensor(brow[:], t1_, ident[0:3, 2:3], brow[:], ALU.mult, ALU.add))
            c.link(v.tensor_copy(b3[:], brow[:]))

            def spread(c, to, val, k_moved, sem_moved, name):
                c.link(v.tensor_tensor_scan(dd[:, ::-1], cont[:, J:0:-1], val[:, ::-1], 0.0, ALU.mult, ALU.add))
                mark[name] = c.n
                hold(dve, sem_moved, k_moved)
                c.link(v.tensor_copy(colc[:, 0:1], PS[1][:, 0:1]))
                c.link(v.scalar_tensor_tensor(to, lastm[:], colc[:, 0:1], dd[:], ALU.mult, ALU.add))

            c.inc(v.tensor_scalar(real[:], key[:], float(N_NODES), None, ALU.is_lt))
            dve.wait_ge(s_pset, 12)
            c.link(v.tensor_tensor(es[:], slot_f[:], endm[:], ALU.mult))
            spread(c, S[:, 0, :], es, 2, s_eset, "spread_slots")
            c.link(v.tensor_copy(gdst[:], S[:, 0, :]))
            c.link(v.tensor_copy(spare[:], spare_i[:]))
            mark["setup"] = c.n

            def stats(c, src_of, n, which, b):
                c.sync()
                for i in range(n):
                    c.inc(v.bn_stats(st[:, which, i, :], src_of(i)))
                c.sync()
                for i in range(n):
                    c.inc(v.bn_aggr(mvs[:, which, b, i, :], st[:, which, i, :]))

            def scale(c, src_of, dst_of, n, which, b):
                for i in range(n):
                    c.inc(v.tensor_scalar(dst_of(i), src_of(i), mvs[:, which, b, i, 0:1], rs[:, which, b, i:i + 1],
                                          ALU.subtract, ALU.mult))

            def softmax(k):
                c = Chain(dve, s_sm[k])
                nh = heads[k]
                hs = range(nh)
                if k == 0:
                    dve.wait_ge(s_sv[0], EG)
                    dve.wait_ge(s_aset, 1)
                    c.link(v.tensor_tensor(S[:], S[:], lew[:].unsqueeze(1).broadcast_to([P, HEADS, J]), ALU.add))
                    c.link(v.scalar_tensor_tensor(F[:], S[:], 0.01, S[:], ALU.mult, ALU.max))
                    c.link(v.tensor_copy(S[:], F[:]))
                elif k == 1:
                    dve.wait_ge(s_sv[1], 3 * EG)
                else:
                    dve.wait_ge(s_he[k], EG)
                    dve.wait_ge(s_cr[k - 1], EG * 4)
                    c.inc(v.tensor_tensor(es[:], sdt[:, :, 0], sdt[:, :, 1], ALU.add))
                    c.link(v.tensor_tensor(S[:, 1, :], sdt[:, :, 1], endm[:], ALU.mult))
                    c.link(v.scalar_tensor_tensor(es[:], es[:], 0.2, es[:], ALU.mult, ALU.max))
                    spread(c, S[:, 2, :], S[:, 1, :], 1, s_smp[k], f"spread{k}")
                    c.link(v.tensor_tensor(S[:, 1, :], H[:, :, D], S[:, 2, :], ALU.add))
                    c.link(v.scalar_tensor_tensor(S[:, 0, :], S[:, 1, :], 0.2, S[:, 1, :], ALU.mult, ALU.max))
                base = 1 if k >= 2 else 0
                for h in hs:
                    c.inc(v.tensor_tensor_scan(F[:, h, :], pen[:, 0:J], S[:, h, :], 0.0, ALU.add, ALU.max))
                c.sync()
                c.link(v.tensor_copy(colv[:, 0:nh], F[:, 0:nh, J - 1]))
                mark[f"colf{k}"] = c.n
                hold(dve, s_smp[k], base + 1)
                c.link(v.tensor_tensor_scan(rowd[0:nh, :], rows[0:nh, 0, :], PS[0][0:nh, 0:P], 0.0, ALU.add, ALU.max))
                c.inc(v.memset(rowc[0:nh, 0:1], -BIG))
                c.link(v.tensor_tensor(rowc[0:nh, 1:P], rowd[0:nh, 0:P - 1], rows[0:nh, 1, 1:P], ALU.add))
                mark[f"rowf{k}"] = c.n
                hold(dve, s_smp[k], base + 2)
                c.link(v.tensor_copy(colc[:, 0:nh], PS[1][:, 0:nh]))
                for h in hs:
                    c.inc(v.scalar_tensor_tensor(F[:, h, :], firstpen[:], colc[:, h:h + 1], F[:, h, :], ALU.add, ALU.max))
                c.sync()
                if k >= 2:
                    c.link(v.tensor_tensor(S[:, 1, :], es[:], endpen[:], ALU.add))
                    c.link(v.tensor_tensor(F[:, 0, :], F[:, 0, :], S[:, 1, :], ALU.max))
                for h in hs:
                    c.inc(v.tensor_tensor_scan(B[:, h, ::-1], pen[:, J:0:-1], F[:, h, ::-1], 0.0, ALU.add, ALU.max))
                c.sync()
                c.link(v.tensor_copy(colv[:, 0:nh], B[:, 0:nh, 0]))
                mark[f"colb{k}"] = c.n
                hold(dve, s_smp[k], base + 3)
                c.link(v.tensor_tensor_scan(rowd[0:nh, ::-1], rows[0:nh, 2, ::-1], PS[0][0:nh, P - 1::-1], 0.0,
                                            ALU.add, ALU.max))
                c.inc(v.memset(rowc[0:nh, P - 1:P], -BIG))
                c.link(v.tensor_tensor(rowc[0:nh, 0:P - 1], rowd[0:nh, 1:P], rows[0:nh, 3, 0:P - 1], ALU.add))
                mark[f"rowb{k}"] = c.n
                hold(dve, s_smp[k], base + 4)
                c.link(v.tensor_copy(colc[:, 0:nh], PS[1][:, 0:nh]))
                for h in hs:
                    c.inc(v.scalar_tensor_tensor(B[:, h, :], lastpen[:], colc[:, h:h + 1], B[:, h, :], ALU.add, ALU.max))
                c.sync()
                c.link(v.tensor_tensor(S[:, 0:nh, :], S[:, 0:nh, :], B[:, 0:nh, :], ALU.subtract))
                if k >= 2:
                    c.link(v.tensor_tensor(es[:], es[:], B[:, 0, :], ALU.subtract))
                    c.link(v.tensor_tensor(es[:], es[:], endm[:], ALU.mult))
                mark[f"exp{k}"] = c.n
                hold(dve, s_sme[k], 2 if k >= 2 else 1)
                for h in hs:
                    c.inc(v.tensor_tensor_scan(F[:, h, :], cont[:, 0:J], S[:, h, :], 0.0, ALU.mult, ALU.add))
                c.sync()
                mark[f"sums{k}"] = c.n
                return c

            def scan_messages(k, cs):
                c = Chain(dve, s_b[k])

                def body(g, first):
                    c.start(g, ET + 1, 0 if first else -1)
                    hg = H[:, bass.ds(g * ET, ET), 0:D]
                    if heads[k] == 1:
                        wv = S[:, 0, bass.ds(g * ET, ET)].unsqueeze(2).broadcast_to([P, ET, D])
                        c.inc(v.tensor_tensor(hg, hg, wv, ALU.mult))
                    else:
                        hv = hg.rearrange("p j (h f) -> p j h f", f=HD)
                        wv = S[:, :, bass.ds(g * ET, ET)].rearrange("p h j -> p j h").unsqueeze(3).broadcast_to(
                            [P, ET, HEADS, HD])
                        c.inc(v.tensor_tensor(hv, hv, wv, ALU.mult))
                    for i in range(1 if first else 0, ET):
                        c.fused()
                        c.inc(v.scalar_tensor_tensor(H[:, bass.ds(g * ET + i, 1), 0:D], H[:, bass.ds(g * ET + i - 1, 1), 0:D],
                                                     cont[:, bass.ds(g * ET + i, 1)], H[:, bass.ds(g * ET + i, 1), 0:D],
                                                     ALU.mult, ALU.add))

                if k < 2:
                    dve.wait_ge(s_he[k], EG * (k + 1))
                body(0, True)
                with dve.Fori(1, EG) as g:
                    body(g, False)
                hold(dve, s_b[k], EG * (ET + 1) - 1)
                c = cs
                nh = heads[k]
                hold(dve, s_smp[k], (5 if k < 2 else 6))
                c.link(v.tensor_copy(Cf[:, 0:D + nh], PS[0][:, 0:D + nh]))
                mark[f"cf{k}"] = c.n
                for h in range(nh):
                    c.inc(v.scalar_tensor_tensor(F[:, h, :], firstm[:], Cf[:, D + h:D + h + 1], F[:, h, :], ALU.mult, ALU.add))
                c.sync()
                if k == 0:
                    c.link(v.tensor_scalar(F[:], F[:], 1e-30, None, ALU.max))
                elif k == 1:
                    c.link(v.tensor_scalar(F[:], F[:], 1e-8, None, ALU.add))
                else:
                    c.link(v.tensor_tensor(F[:, 0, :], F[:, 0, :], es[:], ALU.add))
                    c.link(v.tensor_scalar(F[:, 0, :], F[:, 0, :], 1e-16, None, ALU.add))
                c.link(v.reciprocal(B[:, 0:nh, :], F[:, 0:nh, :]))

            def slot_update(k):
                def quad(t, b):
                    return t[:, b * ET:(b + 1) * ET, :]

                def aggregate(g, b, r, first):
                    c = Chain(dve, s_agg[k])
                    c.start(g, AGG[k])
                    hold(dve, s_cl[k][b], r * CLD[k] + CLD[k])
                    for i in range(ET):
                        hj = H[:, bass.ds(g * ET + i, 1), 0:D].rearrange("p a f -> p (a f)")
                        c.inc(v.scalar_tensor_tensor(hj, Cf[:, 0:D], firstm[:, bass.ds(g * ET + i, 1)], hj, ALU.mult, ALU.add))
                    c.sync()
                    if k >= 2:
                        for i in range(ET):
                            hj = H[:, bass.ds(g * ET + i, 1), 0:D].rearrange("p a f -> p (a f)")
                            c.inc(v.scalar_tensor_tensor(hj, gbuf[:, b, i, 0:D], es[:, bass.ds(g * ET + i, 1)], hj,
                                                         ALU.mult, ALU.add))
                        c.sync()
                    if not first and k >= 1:
                        if k == 1:
                            hold(dve, s_wt, g - 1)
                        else:
                            hold(dve, s_sg[k], g - 1)
                    hg = H[:, bass.ds(g * ET, ET), 0:D]
                    to = quad(bufc, b)
                    if heads[k] == 1:
                        c.inc(v.tensor_tensor(to, hg, B[:, 0, bass.ds(g * ET, ET)].unsqueeze(2).broadcast_to([P, ET, D]), ALU.mult))
                    else:
                        c.inc(v.tensor_tensor(to.rearrange("p j (h f) -> p j h f", f=HD),
                                              hg.rearrange("p j (h f) -> p j h f", f=HD),
                                              B[:, :, bass.ds(g * ET, ET)].rearrange("p h j -> p j h").unsqueeze(3).broadcast_to([P, ET, HEADS, HD]),
                                              ALU.mult))
                    if k == 0:
                        c.sync()
                        c.link(v.tensor_tensor(to, to, bufa[:, b, 0:ET, :], ALU.add))
                        c.inc(v.tensor_tensor(to, to, bc(bias_bc[:], ET), ALU.add))
                        stats(c, lambda i: bufc[:, b * ET + i, :], ET, 0, b)
                    c.finish()

                def stored_before(g, b, r, first):
                    if not first:
                        hold(dve, s_cs[k][b], r * CST[k])
                        if k == 4:
                            hold(dve, s_asc[b], r * 64)

                def out0(g, b, r, first):
                    c = Chain(dve, s_xo[k])
                    c.start(g, ET)
                    hold(dve, s_rc[0], g * 2 + 2)
                    hold(dve, s_agg[0], g * AGG[0] + AGG[0])
                    stored_before(g, b, r, first)
                    scale(c, lambda i: bufc[:, b * ET + i, :], lambda i: bufb[:, b, i, :], ET, 0, b)
                    c.finish()

                def y1(g, b, r, first):
                    c = Chain(dve, s_y[1])
                    c.start(g, 1 + 2 * ET)
                    hold(dve, s_wm, g + 1)
                    if not first:
                        hold(dve, s_z, g * Z1 - Z1)
                    c.inc(v.tensor_tensor(quad(bufd, b), PS[2][:, :].rearrange("p (j f) -> p j f", f=D),
                                          bufa[:, b, 0:ET, :], ALU.add))
                    stats(c, lambda i: bufd[:, b * ET + i, :], ET, 0, b)
                    c.finish()

                def z1(g, b, r, first):
                    c = Chain(dve, s_z)
                    c.start(g, Z1)
                    c.inc(v.tensor_tensor(bufa[:, b, ET:2 * ET, :], bufa[:, b, 0:ET, :], bc(bet_bc[:], ET), ALU.add))
                    hold(dve, s_rc[1], g * 2 + 2)
                    hold(dve, s_y[1], g * (1 + 2 * ET) + 1 + 2 * ET)
                    scale(c, lambda i: bufd[:, b * ET + i, :], lambda i: bufd[:, b * ET + i, :], ET, 0, b)
                    c.sync()
                    c.link(v.tensor_tensor(quad(bufd, b), quad(bufd, b), bc(gam_bc[:], ET), ALU.mult))
                    if not first:
                        hold(dve, s_xo[1], g * ET - ET)
                    c.inc(v.tensor_tensor(bufb[:, b, ET:2 * ET, :], quad(bufd, b), bufa[:, b, ET:2 * ET, :], ALU.add))
                    stats(c, lambda i: bufb[:, b, ET + i, :], ET, 1, b)
                    c.finish()

                def out1(g, b, r, first):
                    c = Chain(dve, s_xo[1])
                    c.start(g, ET)
                    hold(dve, s_rc2, g * 2 + 2)
                    hold(dve, s_z, g * Z1 + Z1)
                    stored_before(g, b, r, first)
                    if not first:
                        hold(dve, s_ct[1], g - 1)
                    scale(c, lambda i: bufb[:, b, ET + i, :], lambda i: bufb[:, b, i, :], ET, 1, b)
                    c.finish()

                def out2(g, b, r, first):
                    c = Chain(dve, s_xo[k])
                    c.start(g, 1)
                    hold(dve, s_sg[k], g + 1)
                    stored_before(g, b, r, first)
                    if not first:
                        hold(dve, s_ct[k], g - 1)
                    c.inc(v.tensor_tensor(bufb[:, b, 0:ET, :], bufa[:, b, 0:ET, :], quad(bufd, b), ALU.add))
                    c.finish()

                def y4(g, b, r, first):
                    c = Chain(dve, s_y[4])
                    c.start(g, 2 + 2 * ET)
                    hold(dve, s_sg[4], g + 1)
                    if not first:
                        hold(dve, s_xo[4], g * ET - ET)
                    t = bufb[:, b, ET:2 * ET, :]
                    c.link(v.tensor_tensor(t, bufa[:, b, 0:ET, :], quad(bufd, b), ALU.add))
                    c.inc(v.tensor_tensor(t, t, bufa[:, b, ET:2 * ET, :], ALU.add))
                    stats(c, lambda i: bufb[:, b, ET + i, :], ET, 0, b)
                    c.finish()

                def out4(g, b, r, first):
                    c = Chain(dve, s_xo[4])
                    c.start(g, ET)
                    hold(dve, s_rc[4], g * 2 + 2)
                    hold(dve, s_y[4], g * (2 + 2 * ET) + 2 + 2 * ET)
                    stored_before(g, b, r, first)
                    scale(c, lambda i: bufb[:, b, ET + i, :], lambda i: bufb[:, b, i, :], ET, 0, b)
                    c.finish()

                skewed(dve, {0: [(aggregate, 0), (out0, 1)],
                             1: [(y1, 1), (out1, 2), (aggregate, 0), (z1, 1)],
                             2: [(aggregate, 0), (out2, 1)],
                             3: [(aggregate, 0), (out2, 1)],
                             4: [(aggregate, 0), (out4, 2), (y4, 1)]}[k])
                dve.wait_ge(s_agg[k], EG * AGG[k])
                dve.wait_ge(s_xo[k], EG * XO[k])

            def score0(g, b, r, first):
                hold(dve, s_mm[0], g + 1)
                v.tensor_copy(S[:, :, bass.ds(g * ET, ET)].rearrange("p h j -> p j h"),
                              PS[6 + b][:, 0:ET * HEADS].rearrange("p (j h) -> p j h", h=HEADS)).then_inc(s_sv[0], 1)

            groups(dve, score0)
            scan_messages(0, softmax(0))
            slot_update(0)

            def dense_a1(g, b, r, first):
                c = Chain(dve, s_A[0])
                c.start(g, DA1)
                hold(dve, s_da_, g + 1)
                stats(c, lambda i: da[:, b, i, :], NT, 0, b)
                c.finish()

            def dense_a2(g, b, r, first):
                c = Chain(dve, s_A[1])
                c.start(g, DA2)
                hold(dve, s_rd[0], g * 2 + 2)
                hold(dve, s_A[0], g * DA1 + DA1)
                if not first:
                    hold(dve, s_dx1[b], r * 16)
                    hold(dve, s_dtt, g - 1)
                scale(c, lambda i: da[:, b, i, :], lambda i: dx1[:, b, i, :], NT, 0, b)
                c.sync()
                if not (isinstance(g, int) and g == 0):
                    hold(dve, s_A[3], g * DA4)
                c.inc(v.tensor_tensor(dy[:, 0], dx1[:, b], bc(bo_bc[:], NT), ALU.add))
                stats(c, lambda i: dy[:, 0, i, :], NT, 1, b)
                c.finish()

            def dense_a3(g, b, r, first):
                c = Chain(dve, s_A[2])
                c.start(g, DA3)
                hold(dve, s_rd[1], g * 2 + 2)
                hold(dve, s_A[1], g * DA2 + DA2)
                scale(c, lambda i: dy[:, 0, i, :], lambda i: dy[:, 0, i, :], NT, 1, b)
                c.sync()
                c.link(v.tensor_tensor(dy[:, 0], dy[:, 0], bc(gam_bc[:], NT), ALU.mult))
                hold(dve, s_dtt, g + 1)
                c.inc(v.tensor_tensor(dy[:, 0], dy[:, 0], dt_[:, b], ALU.add))
                stats(c, lambda i: dy[:, 0, i, :], NT, 2, b)
                c.finish()

            def dense_a4(g, b, r, first):
                c = Chain(dve, s_A[3])
                c.start(g, DA4)
                hold(dve, s_rd[2], g * 2 + 2)
                hold(dve, s_A[2], g * DA3 + DA3)
                if not first:
                    hold(dve, s_Bm[2], g * DB[2] - DB[2])
                    hold(dve, s_dT[0], g * 2 - 2)
                scale(c, lambda i: dy[:, 0, i, :], lambda i: dx2[:, b, i, :], NT, 2, b)
                c.finish()

            def dense_b(m):
                def body(g, b, r, first):
                    c = Chain(dve, s_Bm[m])
                    c.start(g, DB[m])
                    hold(dve, s_dS[m], g * 3 + 3)
                    if m == 0:
                        hold(dve, s_A[3], g * DA4 + DA4)
                        if not first:
                            hold(dve, s_dN, g * NT - NT)
                    else:
                        hold(dve, s_Bm[m - 1], g * DB[m - 1] + DB[m - 1])
                    c.inc(v.tensor_tensor(dxm[:, b], dx2[:, b] if m == 0 else dxm[:, b], dsig[:, m], ALU.add))
                    if m == 2:
                        c.sync()
                        c.inc(v.tensor_tensor(dxm[:, b], dxm[:, b], dx2[:, b], ALU.add))
                        stats(c, lambda i: dxm[:, b, i, :], NT, 3, b)
                    c.finish()
                return body

            skewed(dve, [(dense_a2, 1), (dense_b(2), 3), (dense_b(0), 2), (dense_a3, 1), (dense_b(1), 2),
                         (dense_a1, 0), (dense_a4, 1)])

            def score1(g, b, r, first):
                c = Chain(dve, s_sv[1])
                c.start(g, 3)
                hold(dve, s_he[1], g * 2 + 2)
                c.link(v.tensor_tensor(bufb[:, b, 0:ET, :], bufb[:, b, 0:ET, :],
                                       PS[6 + b][:, :].rearrange("p (j f) -> p j f", f=D), ALU.max))
                c.link(v.tensor_tensor(bufb[:, b, 0:ET, :], bufb[:, b, 0:ET, :], bc(attn_bc[:], ET), ALU.mult))
                c.inc(v.tensor_reduce(S[:, :, bass.ds(g * ET, ET)].rearrange("p h j -> p j h"),
                                      bufb[:, b, 0:ET, :].rearrange("p j (h f) -> p j h f", f=HD), AX.X, ALU.add))
                c.finish()

            groups(dve, score1)
            scan_messages(1, softmax(1))
            slot_update(1)
            for k in (2, 3, 4):
                scan_messages(k, softmax(k))
                slot_update(k)

            def dedup(g, b, r, first):
                c = Chain(dve, s_mv)
                c.start(g, MV)
                sj = src_f[:, bass.ds(g * ET, ET)]
                c.inc(v.tensor_copy(srep, sj.unsqueeze(2).broadcast_to([P, ET, P])))
                mark["srep"] = c.n
                hold(dve, s_mp, g * MP + 1)
                if not (isinstance(g, int) and g == 0):
                    hold(dve, s_mp, g * MP)
                for i in range(ET):
                    c.inc(v.tensor_scalar(bufc[:, i, :], PS[3][:, i * P:(i + 1) * P], src_f[:, bass.ds(g * ET + i, 1)],
                                          None, ALU.is_equal))
                mark["same"] = c.n
                c.sync()
                c.link(v.tensor_tensor(bufc[:, ET:2 * ET, :], bufc[:, 0:ET, :], bc(tri[:], ET), ALU.mult))
                c.link(v.tensor_reduce(cnt[:], bufc[:, ET:2 * ET, :], AX.X, ALU.add))
                c.link(v.tensor_scalar(cnt[:], cnt[:], 0.0, None, ALU.is_equal))
                c.link(v.tensor_tensor(cnt[:], cnt[:], real[:, bass.ds(g * ET, ET)], ALU.mult))
                c.link(v.tensor_scalar(idf[:], sj, spare[:, 0:1], None, ALU.subtract))
                c.link(v.tensor_tensor(idf[:], idf[:], cnt[:], ALU.mult))
                if not first:
                    hold(dve, s_add, g * 64 - 64)
                c.link(v.tensor_scalar(idx_add[:, b, :], idf[:], spare[:, 0:1], None, ALU.add))
                mark["idx"] = c.n
                c.link(v.tensor_scalar(colv[:, 0:1], spare[:, 0:1], 1.0, None, ALU.mult))
                c.finish()

            groups(dve, dedup)
            dve.wait_ge(s_mv, EG * MV)

            def final_stats(g, b, r, first):
                c = Chain(dve, s_fv)
                c.start(g, 2 * NT)
                hold(dve, s_fl[b], r * 16 + 16)
                stats(c, lambda i: bufa[:, b, i, :], NT, 0, b)
                c.finish()

            def final_scale(g, b, r, first):
                c = Chain(dve, s_fv2)
                c.start(g, NT)
                hold(dve, s_fr, g * 2 + 2)
                hold(dve, s_fv, g * 2 * NT + 2 * NT)
                if not first:
                    hold(dve, s_fs[b], r * 16)
                scale(c, lambda i: bufa[:, b, i, :], lambda i: bufb[:, b, i, :], NT, 0, b)
                c.finish()

            skewed(dve, [(final_stats, 0), (final_scale, 1)])

        @block.scalar
        def _(act):
            a = nc.scalar

            def move(to, of, sem_):
                a.activation(to, of, ACT.Copy).then_inc(sem_, 1)

            act.wait_ge(s_ld, 16 * N_LOADS)
            act.wait_ge(s_vset, 4)
            a.activation(lew[:], lew[:], ACT.Ln, bias=one[:, 0:1]).then_inc(s_aset, 1)

            def project(k):
                def body(g, b, r, first):
                    hold(act, s_tr[k], g + 1)
                    if not first:
                        hold(act, s_mm[k], g - 1)
                    move(bufT[:, b, 0:ET, :], PS[b][:, :].rearrange("p (j f) -> p j f", f=P), s_ev[k])
                    move(bufT[:, b, ET:2 * ET, :], PS[2 + b][:, :].rearrange("p (j f) -> p j f", f=P), s_ev[k])
                    hold(act, s_mm[k], g + 1)
                    move(H[:, bass.ds(g * ET, ET), 0:D], PS[4 + b][:, :].rearrange("p (j f) -> p j f", f=D), s_he[k])
                    if k == 1:
                        if not first:
                            hold(act, s_sv[1], g * 3 - 3)
                        a.activation(bufb[:, b, 0:ET, :], PS[6 + b][:, :].rearrange("p (j f) -> p j f", f=D),
                                     ACT.Copy, scale=0.2).then_inc(s_he[1], 1)
                groups(act, body)

            def exps(k):
                nh = heads[k]
                act.wait_ge(s_sm[k], mark[f"exp{k}"])
                a.activation(S[:, 0:nh, :], S[:, 0:nh, :], ACT.Exp).then_inc(s_exp, 1)
                if k >= 2:
                    a.activation(es[:], es[:], ACT.Exp).then_inc(s_exp, 1)

            def slot_update(k):
                if k == 0:
                    return
                def turn_agg(g, b, r, first):
                    hold(act, s_wt, g + 1)
                    if not first:
                        hold(act, s_wm, g)
                    move(bufT[:, 0, 0:ET, :], PS[0][:, :].rearrange("p (j f) -> p j f", f=P), s_we)

                def sigmoid(g, b, r, first):
                    hold(act, s_agg[k], g * AGG[k] + AGG[k])
                    if not first:
                        hold(act, s_y[4] if k == 4 else s_xo[k], (g - 1) * ((2 + 2 * ET) if k == 4 else 1))
                    a.activation(bufd[:, b * ET:(b + 1) * ET, :], bufc[:, b * ET:(b + 1) * ET, :],
                                 ACT.Sigmoid).then_inc(s_sg[k], 1)

                def keep_rows(g, b, r, first):
                    hold(act, s_ct[k], g + 1)
                    if not first:
                        hold(act, s_cm[k], g)
                    move(bufT[:, 1, 0:ET, :], PS[1][:, :].rearrange("p (j f) -> p j f", f=P), s_ce[k])
                    hold(act, s_cm[k], g + 1)
                    if not first:
                        hold(act, s_cs[k][b], r * CST[k])
                    r3 = PS[3][:, 0:3 * EXT].rearrange("p (j e) -> p j e", e=EXT)
                    r4 = PS[4][:, 0:EXT].rearrange("p (j e) -> p j e", e=EXT)
                    move(trow[:, b, 0:3, :], r3, s_cr[k])
                    move(trow[:, b, 3:4, :], r4, s_cr[k])
                    move(sdt[:, bass.ds(g * ET, 3), :], r3[:, :, D:EXT], s_cr[k])
                    move(sdt[:, bass.ds(g * ET + 3, 1), :], r4[:, :, D:EXT], s_cr[k])

                skewed(act, {1: [(turn_agg, 0), (keep_rows, 3)],
                             2: [(sigmoid, 0), (keep_rows, 2)],
                             3: [(sigmoid, 0), (keep_rows, 2)],
                             4: [(sigmoid, 0)]}[k])

            def dense_m(m):
                banks = 5 if m == 0 else 2

                def body(g, b, r, first):
                    for q in range(2):
                        hold(act, s_dT[m], g * 2 + q + 1)
                        if q == 0 and not (isinstance(g, int) and g == 0):
                            hold(act, s_dM[m], g * 3)
                        move(dT[:, m, q * ET:(q + 1) * ET, :], PS[q][:, :].rearrange("p (j f) -> p j f", f=P), s_dE[m])
                    if not (isinstance(g, int) and g == 0):
                        hold(act, s_Bm[m], g * DB[m])
                        hold(act, s_dt2[m], g * 16)
                    for q, w in enumerate((3, 3, 2)):
                        hold(act, s_dM[m], g * 3 + q + 1)
                        a.activation(dsig[:, m, 3 * q:3 * q + w, :],
                                     PS[banks + q][:, 0:w * EXT].rearrange("p (j e) -> p j e", e=EXT)[:, :, 0:D],
                                     ACT.Sigmoid).then_inc(s_dS[m], 1)
                    for q, w in enumerate((3, 3, 2)):
                        move(trow[:, m, 3 * q:3 * q + w, :],
                             PS[banks + q][:, 0:w * EXT].rearrange("p (j e) -> p j e", e=EXT), s_dR[m])
                return body

            def dense_scale(g, b, r, first):
                hold(act, s_rd[3], g * 4 + 4)
                if not first:
                    hold(act, s_dx3[b], r * 32)
                for i in range(NT):
                    a.activation(dx3[:, b, i, :], dxm[:, b, i, :], ACT.Identity, scale=rs[:, 3, b, i:i + 1],
                                 bias=nmr[:, b, i:i + 1]).then_inc(s_dN, 1)

            project(0)
            exps(0)
            act.wait_ge(s_agg[0], EG * AGG[0])
            skewed(act, [(dense_m(2), 3), (dense_m(0), 2), (dense_scale, 3), (dense_m(1), 2)])
            for q in range(2):
                act.wait_ge(s_cs[0][q], (PAIRS + 1 - q) * CST[0])
                act.wait_ge(s_dx1[q], (PAIRS + 1 - q) * 16)
                act.wait_ge(s_dx3[q], (PAIRS + 1 - q) * 32)
            for m in range(3):
                act.wait_ge(s_dt2[m], EG * 16)
                act.wait_ge(s_Bm[m], EG * DB[m])
                act.wait_ge(s_dM[m], EG * 3)
            project(1)
            exps(1)
            slot_update(1)
            for k in (2, 3, 4):
                act.wait_ge(s_agg[k - 1], EG * AGG[k - 1])
                act.wait_ge(s_xo[k - 1], EG * XO[k - 1])

                def keep(g, b, r, first, k=k):
                    hold(act, s_ga[k][b], r * 64 + 64)
                    move(H[:, bass.ds(g * ET, ET), :], gbuf[:, b, :, :], s_he[k])
                groups(act, keep)
                exps(k)
                for q in range(2):
                    act.wait_ge(s_cs[k - 1][q], (PAIRS + 1 - q) * CST[k - 1])
                slot_update(k)
            for q in range(2):
                act.wait_ge(s_cs[4][q], (PAIRS + 1 - q) * CST[4])
                act.wait_ge(s_asc[q], (PAIRS + 1 - q) * 64)

            def message(g, b, r, first):
                hold(act, s_mp, g * MP + 1)
                for q in range(2):
                    move(bufT[:, 0, q * ET:(q + 1) * ET, :], PS[q][:, :].rearrange("p (j f) -> p j f", f=P), s_ma)
                move(eaT, PS[2][0:64, :], s_ma)
                hold(act, s_mp, g * MP + 2)
                for q in range(2):
                    a.activation(bufT[:, 1, q * ET:(q + 1) * ET, :], PS[4 + q][:, :].rearrange("p (j f) -> p j f", f=P),
                                 ACT.Relu, bias=b31c[:, q:q + 1]).then_inc(s_ma, 1)
                hold(act, s_mp, g * MP + 3)
                move(bufd[:, 0:ET, :], PS[6][:, :].rearrange("p (j f) -> p j f", f=D), s_ma)
                hold(act, s_mp, g * MP + 4)
                if not first:
                    hold(act, s_add, g * 64 - 64)
                move(bufb[:, b, 0:ET, :], PS[7][:, :].rearrange("p (j f) -> p j f", f=D), s_ma)
            groups(act, message)

        @block.tensor
        def _(pe):
            t = nc.tensor

            def mm(to, w, m, start=True, stop=True):
                return t.matmul(to, w, m, start=start, stop=stop)

            pe.wait_ge(s_pset, 9)
            pe.wait_ge(s_vset, mark["rep"])
            t.transpose(PS[0][:, 0:P], bufc[:, 0, :], ident[:])
            t.transpose(PS[0][:, P:2 * P], bufc[:, 1, :], ident[:])
            for n in range(4):
                last = t.transpose(PS[1][0:8, n * P:(n + 1) * P], crep[:, n, :], ident[:])
            last.then_inc(s_eset, 1)
            pe.wait_ge(s_vset, mark["spread_slots"])
            pe.wait_ge(s_pset, 11)
            mm(PS[1][:, 0:1], right[:], dd[:, 0:1]).then_inc(s_eset, 1)
            pe.wait_ge(s_vset, mark["setup"])

            def project(k):
                def body(g, b, r, first):
                    hold(pe, s_ga[k][b], r * 128 + 128)
                    for i in range(ET):
                        t.transpose(PS[b][:, i * P:(i + 1) * P], bufa[:, b, i, :], ident[:])
                    for i in range(ET):
                        last = t.transpose(PS[2 + b][:, i * P:(i + 1) * P], bufa[:, b, ET + i, :], ident[:])
                    last.then_inc(s_tr[k], 1)
                    hold(pe, s_ev[k], g * 2 + 2)
                    if not first:
                        hold(pe, s_he[k], (g - 1) * (k + 1))
                        hold(pe, s_sv[k], g - 1 if k == 0 else g * 3 - 5)
                    for i in range(ET):
                        xs, xd = bufT[:, b, i, :], bufT[:, b, ET + i, :]
                        o = PS[4 + b][:, i * D:(i + 1) * D]
                        if k == 0:
                            e = PS[6 + b][:, i * HEADS:(i + 1) * HEADS]
                            mm(o, xs, w0[:, 0:D])
                            mm(e, xs, w0[:, D:D + HEADS], stop=False)
                            last = mm(e, xd, w0[:, D:D + HEADS], start=False)
                        else:
                            e = PS[6 + b][:, i * D:(i + 1) * D]
                            mm(o, xs, wsrc[:])
                            mm(e, xs, wsrc[:], stop=False)
                            last = mm(e, xd, wdst[:], start=False)
                    last.then_inc(s_mm[k], 1)
                groups(pe, body)

            def softmax(k):
                nh = heads[k]
                if k >= 2:
                    pe.wait_ge(s_sm[k], mark[f"spread{k}"])
                    mm(PS[1][:, 0:1], right[:], dd[:, 0:1]).then_inc(s_moved, 1)
                for d in "fb":
                    pe.wait_ge(s_sm[k], mark[f"col{d}{k}"])
                    t.transpose(PS[0][0:nh, 0:P], colv[:, 0:nh], ident[:]).then_inc(s_moved, 1)
                    pe.wait_ge(s_sm[k], mark[f"row{d}{k}"])
                    t.transpose(PS[1][:, 0:nh], rowc[0:nh, :], ident[0:nh, 0:nh]).then_inc(s_moved, 1)
                pe.wait_ge(s_sm[k], mark[f"sums{k}"])
                hold(pe, s_b[k], EG * (ET + 1) - 1)
                mm(PS[0][:, 0:D], left[:], H[:, J - 1, 0:D])
                mm(PS[0][:, D:D + nh], left[:], F[:, 0:nh, J - 1]).then_inc(s_moved, 1)

            def ext(m, to, xT, n):
                for i in range(n):
                    o = PS[to + i // 3][:, (i % 3) * EXT:(i % 3 + 1) * EXT]
                    mm(o, xT(i), wext[:, m, :], stop=False)
                    last = mm(o, ones3[:], b3[:, m, :], start=False)
                return last

            def slot_update(k):
                if k in (0, 4):
                    return

                def turn_agg(g, b, r, first):
                    hold(pe, s_agg[1], g * AGG[1] + AGG[1])
                    if not (isinstance(g, int) and g == 0):
                        hold(pe, s_we, g)
                    for i in range(ET):
                        last = t.transpose(PS[0][:, i * P:(i + 1) * P], bufc[:, b * ET + i, :], ident[:])
                    last.then_inc(s_wt, 1)

                def times_wout(g, b, r, first):
                    hold(pe, s_we, g + 1)
                    if not (isinstance(g, int) and g == 0):
                        hold(pe, s_y[1], g * (1 + 2 * ET))
                    for i in range(ET):
                        o = PS[2][:, i * D:(i + 1) * D]
                        mm(o, bufT[:, 0, i, :], wout[:], stop=False)
                        last = mm(o, ones3[:], b3[:, 3, 0:D], start=False)
                    last.then_inc(s_wm, 1)

                def turn_out(g, b, r, first):
                    hold(pe, s_xo[k], g * XO[k] + XO[k])
                    if not (isinstance(g, int) and g == 0):
                        hold(pe, s_ce[k], g)
                    for i in range(ET):
                        last = t.transpose(PS[1][:, i * P:(i + 1) * P], bufb[:, b, i, :], ident[:])
                    last.then_inc(s_ct[k], 1)

                def to_rows(g, b, r, first):
                    hold(pe, s_ce[k], g + 1)
                    if not (isinstance(g, int) and g == 0):
                        hold(pe, s_cr[k], g * 4)
                    ext(k - 1, 3, lambda i: bufT[:, 1, i, :], ET).then_inc(s_cm[k], 1)

                if k == 1:
                    skewed(pe, [(turn_agg, 0), (turn_out, 3), (times_wout, 0), (to_rows, 3)])
                else:
                    skewed(pe, [(turn_out, 0), (to_rows, 0)])

            def dense_m(m):
                banks = 5 if m == 0 else 2

                def body(g, b, r, first):
                    hold(pe, s_A[3] if m == 0 else s_Bm[m - 1], g * (DA4 if m == 0 else 1) + (DA4 if m == 0 else 1))
                    before = {0: (2, 1), 1: (0, 0), 2: (1, 0)}[m]
                    for q in range(2):
                        if m == 0:
                            if not (isinstance(g, int) and g == 0):
                                hold(pe, s_dE[2], g * 2 - 2 + q + 1)
                        elif m == 1:
                            hold(pe, s_dE[0], g * 2 + q + 1)
                        else:
                            if isinstance(g, int) and g == EG - 1:
                                hold(pe, s_dE[1], g * 2 + q + 1)
                            else:
                                hold(pe, s_dE[1], g * 2 + q + 1)
                        for i in range(ET):
                            xi = (dx2 if m == 0 else dxm)[:, b, q * ET + i, :]
                            last = t.transpose(PS[q][:, i * P:(i + 1) * P], xi, ident[:])
                        last.then_inc(s_dT[m], 1)
                    if m == 0:
                        if not (isinstance(g, int) and g == 0):
                            hold(pe, s_dR[0], g * 3)
                    elif m == 1:
                        if not (isinstance(g, int) and g == 0):
                            hold(pe, s_dR[2], g * 3)
                    else:
                        hold(pe, s_dR[1], g * 3 + 3)
                    for i in range(NT):
                        if i % ET == 0:
                            hold(pe, s_dE[m], g * 2 + i // ET + 1)
                        o = PS[banks + i // 3][:, (i % 3) * EXT:(i % 3 + 1) * EXT]
                        mm(o, dT[:, m, i, :], wext[:, m, :], stop=False)
                        last = mm(o, ones3[:], b3[:, m, :], start=False)
                        if i in (2, 5, 7):
                            last.then_inc(s_dM[m], 1)
                return body

            project(0)
            softmax(0)
            pe.wait_ge(s_sm[0], mark["cf0"])
            skewed(pe, [(dense_m(2), 1), (dense_m(0), 0), (dense_m(1), 0)])
            for m in range(3):
                pe.wait_ge(s_dR[m], EG * 3)
            project(1)
            softmax(1)
            pe.wait_ge(s_sm[1], mark["cf1"])
            slot_update(1)
            for k in (2, 3, 4):
                pe.wait_ge(s_cr[k - 1], EG * 4)
                softmax(k)
                pe.wait_ge(s_sm[k], mark[f"cf{k}"])
                slot_update(k)

            def message(g, b, r, first):
                hold(pe, s_ga[5][b], r * 128 + 128)
                hold(pe, s_el[b], r * 16 + 16)
                hold(pe, s_mv, g * MV + mark["srep"])
                for i in range(ET):
                    at = slice(i * P, (i + 1) * P)
                    t.transpose(PS[0][:, at], bufa[:, b, i, :], ident[:])
                    t.transpose(PS[1][:, at], bufa[:, b, ET + i, :], ident[:])
                    t.transpose(PS[2][0:64, at], eab[:, b, i, :], ident[:])
                    last = t.transpose(PS[3][:, at], srep[:, i, :], ident[:])
                last.then_inc(s_mp, 1)
                hold(pe, s_ma, g * MA + 3)
                for q in range(2):
                    o = PS[4 + q][:, :]
                    at = slice(q * P, (q + 1) * P)
                    mm(o, w31a[:, at], bufT[:, 0, 0:ET, :].rearrange("p j f -> p (j f)"), stop=False)
                    mm(o, w31b[:, at], bufT[:, 0, ET:2 * ET, :].rearrange("p j f -> p (j f)"), start=False, stop=False)
                    last = mm(o, w31c[:, at], eaT, start=False)
                last.then_inc(s_mp, 1)
                hold(pe, s_ma, g * MA + 5)
                for i in range(ET):
                    o = PS[6][:, i * D:(i + 1) * D]
                    mm(o, bufT[:, 1, i, :], w32s[:, 0, :], stop=False)
                    mm(o, bufT[:, 1, ET + i, :], w32s[:, 1, :], start=False, stop=False)
                    last = mm(o, ones3[:], b3[:, 4, 0:D], start=False)
                last.then_inc(s_mp, 1)
                hold(pe, s_ma, g * MA + 6)
                hold(pe, s_mv, g * MV + mark["same"])
                for i in range(ET):
                    last = mm(PS[7][:, i * D:(i + 1) * D], bufc[:, i, :], bufd[:, i, :])
                last.then_inc(s_mp, 1)
            groups(pe, message)

        @block.gpsimd
        def _(pool):
            q = nc.gpsimd
            c = Chain(pool, s_pset)
            c.link(q.memset(ident[:], 0.0))
            c.inc(q.affine_select(out=ident[:], in_=ident[:], compare_op=ALU.not_equal, fill=1.0, base=0,
                                  pattern=[[-1, P]], channel_multiplier=1))
            c.link(q.memset(tri[:], 1.0))
            c.inc(q.affine_select(out=tri[:], in_=tri[:], compare_op=ALU.is_gt, fill=0.0, base=0,
                                  pattern=[[-1, P]], channel_multiplier=1))
            c.inc(q.iota(slot_i[:], pattern=[[1, J]], base=0, channel_multiplier=J))
            c.inc(q.iota(node_i[:], pattern=[[1, NPAD // P]], base=SLOTS, channel_multiplier=NPAD // P))
            c.inc(q.memset(kfn[:], -1))
            c.inc(q.memset(brow[:], 0.0))
            c.inc(q.memset(ones3[:], 1.0))
            c.sync()
            pool.wait_ge(s_vset, mark["lr"])
            c.inc(q.affine_select(out=left[:], in_=left[:], compare_op=ALU.is_gt, fill=0.0, base=0,
                                  pattern=[[1, P]], channel_multiplier=-1))
            c.inc(q.affine_select(out=right[:], in_=right[:], compare_op=ALU.is_gt, fill=0.0, base=0,
                                  pattern=[[-1, P]], channel_multiplier=1))
            c.link(q.iota(spare_i[:], pattern=[[0, 1]], base=N_NODES, channel_multiplier=1))
            pool.wait_ge(s_vset, mark["setup"])

            def fetch(table, idx, to, cur_, b, sem_):
                for i in range(ET):
                    q.indirect_dma_start(out=to(i), out_offset=None, in_=table,
                                         in_offset=bass.IndirectOffsetOnAxis(ap=cur_[:, b, i:i + 1], axis=0)
                                         ).then_inc(sem_, 16)

            def gather2(k, table, isrc, idst, free):
                def body(g, b, r, first):
                    c = Chain(pool, s_gi[k])
                    c.start(g, 2)
                    if not first:
                        hold(pool, s_ga[k][b], r * 128)
                        free(g, b, r)
                    c.inc(q.tensor_copy(cur[:, b, :], isrc[:, bass.ds(g * ET, ET)]))
                    c.inc(q.tensor_copy(cur2[:, b, :], idst[:, bass.ds(g * ET, ET)]))
                    c.sync()
                    fetch(table, None, lambda i: bufa[:, b, i, :], cur, b, s_ga[k][b])
                    fetch(table, None, lambda i: bufa[:, b, ET + i, :], cur2, b, s_ga[k][b])
                return body

            def free0(g, b, r):
                hold(pool, s_tr[0], g - 1)
                hold(pool, s_xst[b], r * 16)
            groups(pool, gather2(0, x[:, :], src_i, dstc, free0))

            pool.wait_ge(s_slots, 16)
            for b in range(2):
                pool.wait_ge(s_ga[0][b], (PAIRS + 1 - b) * 128)

            def scatter_slots(g, b, r, first):
                c = Chain(pool, s_scq)
                c.start(g, 2)
                if not first:
                    hold(pool, s_scat[b], r * 64)
                c.inc(q.tensor_copy(cur[:, b, :], dscat[:, bass.ds(g * ET, ET)]))
                c.inc(q.tensor_copy(cur2[:, b, :], slot_i[:, bass.ds(g * ET, ET)]))
                c.sync()
                for i in range(ET):
                    q.indirect_dma_start(out=slot_of_node[:, :], out_offset=bass.IndirectOffsetOnAxis(ap=cur[:, b, i:i + 1], axis=0),
                                         in_=cur2[:, b, i:i + 1], in_offset=None, bounds_check=N_NODES - 1,
                                         oob_is_err=False).then_inc(s_scat[b], 16)
            groups(pool, scatter_slots)
            for b in range(2):
                pool.wait_ge(s_scat[b], (PAIRS + 1 - b) * 64)

            def look_up(g, b, r, first):
                c = Chain(pool, s_mapq)
                c.start(g, 2, -g if first else -2)
                if not first:
                    hold(pool, s_gmap[b], r * 64)
                    c.inc(q.tensor_copy(gsrc[:, bass.ds(g * ET - 2 * ET, ET)], cur2[:, b, :]))
                c.inc(q.tensor_copy(cur[:, b, :], src_i[:, bass.ds(g * ET, ET)]))
                c.sync()
                fetch(slot_of_node[:, :], None, lambda i: cur2[:, b, i:i + 1], cur, b, s_gmap[b])
            groups(pool, look_up)
            for g in (EG - 2, EG - 1):
                b = g % 2
                pool.wait_ge(s_gmap[b], (PAIRS + 1 - b) * 64)
                q.tensor_copy(gsrc[:, g * ET:(g + 1) * ET], cur2[:, b, :]).then_inc(s_idx, 1)
            hold(pool, s_mapq, 2 * EG)

            def root(ready, count, out_sem, which, n, with_mean=False):
                per = 4 if with_mean else 2

                def body(g, b, r, first):
                    c = Chain(pool, out_sem)
                    c.start(g, per)
                    hold(pool, ready, g * count + count)
                    c.link(q.tensor_scalar(rs[:, which, b, 0:n], mvs[:, which, b, 0:n, 1], LN_EPS, None, ALU.add))
                    c.inc(q.tensor_tensor(rs[:, which, b, 0:n], rs[:, which, b, 0:n], half[:, 0:n], ALU.pow))
                    if with_mean:
                        c.inc(q.tensor_scalar(nmr[:, b, 0:n], mvs[:, which, b, 0:n, 0], -1.0, None, ALU.mult))
                        c.sync()
                        c.inc(q.tensor_tensor(nmr[:, b, 0:n], nmr[:, b, 0:n], rs[:, which, b, 0:n], ALU.mult))
                    c.finish()
                return body

            groups(pool, root(s_agg[0], AGG[0], s_rc[0], 0, ET))

            def dense_a(g, b, r, first):
                hold(pool, s_dl[b], r * 16 + 16)
                if not first:
                    hold(pool, s_A[1], g * DA2 - DA2)
                q.tensor_tensor(da[:, b], dx[:, b], bc(bias_bc[:], NT), ALU.add).then_inc(s_da_, 1)

            def dense_t(g, b, r, first):
                hold(pool, s_A[1], g * DA2 + DA2)
                if not first:
                    hold(pool, s_A[2], g * DA3 - DA3)
                q.tensor_tensor(dt_[:, b], dx1[:, b], bc(bet_bc[:], NT), ALU.add).then_inc(s_dtt, 1)

            pool.wait_ge(s_agg[0], EG * AGG[0])
            skewed(pool, [(root(s_A[1], DA2, s_rd[1], 1, NT), 2), (root(s_Bm[2], DB[2], s_rd[3], 3, NT, True), 4),
                          (dense_t, 2), (root(s_A[2], DA3, s_rd[2], 2, NT), 2),
                          (root(s_A[0], DA1, s_rd[0], 0, NT), 1), (dense_a, 0)])

            def stored(k):
                for b in range(2):
                    pool.wait_ge(s_cs[k][b], (PAIRS + 1 - b) * CST[k])

            stored(0)
            for b in range(2):
                pool.wait_ge(s_dx1[b], (PAIRS + 1 - b) * 16)
                pool.wait_ge(s_dx3[b], (PAIRS + 1 - b) * 32)
            for m in range(3):
                pool.wait_ge(s_dt2[m], EG * 16)
            groups(pool, gather2(1, t1[:, :], gsrc, gdst, lambda g, b, r: hold(pool, s_tr[1], g - 1)))
            for b in range(2):
                pool.wait_ge(s_ga[1][b], (PAIRS + 1 - b) * 128)
            skewed(pool, [(root(s_y[1], 1 + 2 * ET, s_rc[1], 0, ET), 0), (root(s_z, Z1, s_rc2, 1, ET), 0)])
            for k in (2, 3, 4):
                stored(k - 1)

                def gather1(g, b, r, first, k=k):
                    c = Chain(pool, s_gi[k])
                    c.start(g, 1)
                    if not first:
                        hold(pool, s_ga[k][b], r * 64)
                        hold(pool, s_he[k], g - 1)
                    c.link(q.tensor_copy(cur[:, b, :], gsrc[:, bass.ds(g * ET, ET)]))
                    fetch(t2[k - 2][:, :], None, lambda i: gbuf[:, b, i, :], cur, b, s_ga[k][b])
                groups(pool, gather1)
                for b in range(2):
                    pool.wait_ge(s_ga[k][b], (PAIRS + 1 - b) * 64)
                if k == 4:
                    break

            pool.wait_ge(s_accp, 16)

            def scatter_acc(g, b, r, first):
                c = Chain(pool, s_asq)
                c.start(g, 1)
                if not first:
                    hold(pool, s_asc[b], r * 64)
                c.link(q.tensor_copy(cur[:, b, :], dscat[:, bass.ds(g * ET, ET)]))
                hold(pool, s_xo[4], g * ET + ET)
                for i in range(ET):
                    q.indirect_dma_start(out=acc[:, :], out_offset=bass.IndirectOffsetOnAxis(ap=cur[:, b, i:i + 1], axis=0),
                                         in_=bufb[:, b, i, :], in_offset=None, bounds_check=N_NODES - 1,
                                         oob_is_err=False).then_inc(s_asc[b], 16)
            skewed(pool, [(root(s_y[4], 2 + 2 * ET, s_rc[4], 0, ET), 0), (scatter_acc, 1)])
            for b in range(2):
                pool.wait_ge(s_asc[b], (PAIRS + 1 - b) * 64)
            stored(4)

            g2 = gather2(5, t3[:, :], gsrc, gdst, lambda g, b, r: hold(pool, s_mp, g * MP - 2 * MP + 1))

            def add(g, b, r, first):
                hold(pool, s_ma, g * MA + MA)
                hold(pool, s_mv, g * MV + mark["idx"])
                for i in range(ET):
                    q.indirect_dma_start(out=acc[:, :], out_offset=bass.IndirectOffsetOnAxis(ap=idx_add[:, b, i:i + 1], axis=0),
                                         in_=bufb[:, b, i, :], in_offset=None, compute_op=ALU.add).then_inc(s_add, 16)
                    hold(pool, s_add, g * 64 + i * 16 + 16)
            load_store(g2, add, pool)
            groups(pool, root(s_fv, 2 * NT, s_fr, 0, NT))

        @block.sync
        def _(sp):
            n_loads = [0]

            def load(to, of, slow=False):
                n_loads[0] += 1
                sp.dma_start(to, of, allow_slow_non_contiguous=slow).then_inc(s_ld, 16)
            load(src_i[:], src)
            load(dst_i[:], dst)
            load(lew[:], ew)
            load(w0[:, 0:D], w0t)
            load(wa_bc[:], w_attn.unsqueeze(0).broadcast_to([P, HD]))
            load(bias_bc[:], bias0.unsqueeze(0).broadcast_to([P, D]))
            load(wsrc[:], w_src)
            load(wdst[:], w_dst)
            load(attn_bc[:], attn.unsqueeze(0).broadcast_to([P, D]))
            load(wout[:], w_out)
            load(bo_bc[:], b_out.unsqueeze(0).broadcast_to([P, D]))
            load(gam_bc[:], gamma.unsqueeze(0).broadcast_to([P, D]))
            load(bet_bc[:], beta.unsqueeze(0).broadcast_to([P, D]))
            load(wext[:, :, 0:D], w2.rearrange("m k n -> k m n"))
            load(av[:, :, 0, :], a_src.unsqueeze(0).broadcast_to([P, 3, D]))
            load(av[:, :, 1, :], a_dst.unsqueeze(0).broadcast_to([P, 3, D]))
            load(w31a[:], w31[0:D, :])
            load(w31b[:], w31[D:2 * D, :])
            load(w31c[:], w31[2 * D:2 * D + 64, :])
            load(b31c[:], b31)
            load(w32s[:], w32.rearrange("(t p) n -> p t n", p=P))
            sp.wait_ge(s_pset, 9)
            load(brow[:, 0:3, 0:D], b2.unsqueeze(0).broadcast_to([3, 3, D]))
            load(brow[:, 3, 0:D], b_out.unsqueeze(0).broadcast_to([3, D]))
            load(brow[:, 4, 0:D], b32.unsqueeze(0).broadcast_to([3, D]))
            load(kfn[0:P - 1, 0:1], dst[1:P, 0:1], slow=True)
            load(kfn[1:P, 1:2], dst[0:P - 1, J - 1:J], slow=True)
            assert n_loads[0] == N_LOADS
            sp.dma_start(slot_of_node.rearrange("(p c) w -> p (c w)", p=P), node_i[:]).then_inc(s_slots, 16)
            sp.dma_start(acc[N_NODES:N_NODES + P, :], ident[:]).then_inc(s_accp, 16)

            def keep_dst(g, b, r, first):
                hold(sp, s_ga[0][b], r * 128 + 128)
                sp.dma_start(rows4(x0_dst, g), bufa[:, b, ET:2 * ET, :]).then_inc(s_xst[b], 16)
            groups(sp, keep_dst)

            def all_of(pair, per):
                for b in range(2):
                    sp.wait_ge(pair[b], (PAIRS + 1 - b) * per)

            def slots(k):
                def load_(g, b, r, first):
                    if not first:
                        hold(sp, *[(s_agg[0], (g - 1) * AGG[0]), (s_z, (g - 1) * Z1), (s_xo[2], g - 1), (s_xo[3], g - 1),
                                   (s_y[4], (g - 1) * (2 + 2 * ET))][k])
                    def get(to, of):
                        sp.dma_start(to, rows4(of, g)).then_inc(s_cl[k][b], 16)
                    get(bufa[:, b, 0:ET, :], [x0_dst, t1, x2s[0], x2s[1], x2s[2]][k])
                    if k >= 2:
                        get(gbuf[:, b, :, :], t2[k - 2])
                    if k == 4:
                        get(bufa[:, b, ET:2 * ET, :], x2s[0])

                def store(g, b, r, first):
                    hold(sp, s_xo[k], g * XO[k] + XO[k])
                    sp.dma_start(rows4([t1, x2s[0], x2s[1], x2s[2], t3][k], g), bufb[:, b, 0:ET, :]).then_inc(s_cs[k][b], 16)
                    if k in (1, 2, 3):
                        hold(sp, s_cr[k], g * 4 + 4)
                        sp.dma_start(rows4(t2[k - 1], g), trow[:, b, 0:ET, :]).then_inc(s_cs[k][b], 16)
                skewed(sp, [(load_, 0), (store, [2, 4, 3, 3, 3][k])])

            sp.wait_ge(s_tr[0], EG)
            all_of(s_xst, 16)
            slots(0)
            all_of(s_cs[0], CST[0])
            sp.wait_ge(s_agg[0], EG * AGG[0])

            def dense_load(g, b, r, first):
                parts = TAIL if isinstance(g, int) and g == EG - 1 else P
                if not first:
                    hold(sp, s_da_, g - 1)
                sp.dma_start(dx[0:parts, b, :, :], node_rows(x, g, 0, parts)).then_inc(s_dl[b], 16)

            def parts_of(g):
                return TAIL if isinstance(g, int) and g == EG - 1 else P

            def store_x1(g, b, r, first):
                n = parts_of(g)
                hold(sp, s_A[1], g * DA2 + DA2)
                sp.dma_start(node_rows(t1, g, SLOTS, n), dx1[0:n, b, :, :]).then_inc(s_dx1[b], 16)

            def store_rows(m):
                def body(g, b, r, first):
                    n = parts_of(g)
                    hold(sp, s_dR[m], g * 3 + 3)
                    sp.dma_start(node_rows(t2[m], g, SLOTS, n), trow[0:n, m, :, :]).then_inc(s_dt2[m], 16)
                return body

            def store_x3(g, b, r, first):
                n = parts_of(g)
                hold(sp, s_dN, g * NT + NT)
                sp.dma_start(node_rows(t3, g, SLOTS, n), dx3[0:n, b, :, :]).then_inc(s_dx3[b], 16)
                sp.dma_start(node_rows(acc, g, 0, n), dx3[0:n, b, :, :]).then_inc(s_dx3[b], 16)

            skewed(sp, [(dense_load, 0), (store_x1, 2), (store_rows(2), 4), (store_rows(0), 3), (store_x3, 4),
                        (store_rows(1), 3)])

            sp.wait_ge(s_tr[1], EG)
            slots(1)
            for k in (2, 3, 4):
                all_of(s_cs[k - 1], CST[k - 1])
                sp.wait_ge(s_xo[k - 1], EG * XO[k - 1])
                sp.wait_ge(s_he[k], EG)
                slots(k)

            def edge_attr(g, b, r, first):
                if not first:
                    hold(sp, s_mp, g * MP - 2 * MP + 1)
                sp.dma_start(eab[:, b, :, :], rows4(ea, g)).then_inc(s_el[b], 16)
            groups(sp, edge_attr)

            sp.wait_ge(s_add, EG * 64)
            sp.wait_ge(s_mp, EG * MP)

            def final_load(g, b, r, first):
                parts = TAIL if isinstance(g, int) and g == EG - 1 else P
                if not first:
                    hold(sp, s_fv2, g * NT - NT)
                sp.dma_start(bufa[0:parts, b, :, :], node_rows(acc, g, 0, parts)).then_inc(s_fl[b], 16)

            def final_store(g, b, r, first):
                parts = TAIL if isinstance(g, int) and g == EG - 1 else P
                hold(sp, s_fv2, g * NT + NT)
                sp.dma_start(node_rows(out, g, 0, parts), bufb[0:parts, b, :, :]).then_inc(s_fs[b], 16)
            load_store(final_load, final_store, sp)
            all_of(s_fs, 16)
            all_of(s_el, 16)


def kernel(**inputs):
    import numpy as np
    import concourse.bacc as bacc
    from concourse.bass_utils import run_bass_kernel_spmd

    def slots(name, fill):
        a = np.asarray(inputs[name])
        pad = np.full((SLOTS - N_EDGES,) + a.shape[1:], fill, a.dtype)
        return np.concatenate([a, pad])

    arrays = {
        "x": inputs["x"],
        "src": slots("src", 0).reshape(P, J),
        "dst": slots("dst", N_NODES).reshape(P, J),
        "ew": slots("edge_weight", 0).reshape(P, J),
        "ea": slots("edge_attr_64", 0),
        "w0t": np.asarray(inputs["L0_gnn_W_fc"]).T,
        "w_attn": inputs["L0_gnn_w_attn"],
        "bias0": inputs["L0_gnn_bias"],
        "w_src": inputs["L1_gnn_W_src"],
        "w_dst": inputs["L1_gnn_W_dst"],
        "attn": np.asarray(inputs["L1_gnn_attn"]).reshape(-1),
        "w_out": inputs["L1_gnn_W_out"],
        "b_out": inputs["L1_gnn_b_out"],
        "gamma": inputs["L1_gnn_gamma"],
        "beta": inputs["L1_gnn_beta"],
        "w2": inputs["L2_gnn_Ws"],
        "a_src": inputs["L2_gnn_att_src"],
        "a_dst": inputs["L2_gnn_att_dst"],
        "b2": inputs["L2_gnn_bias"],
        "w31": inputs["L3_gnn_W1"],
        "b31": np.asarray(inputs["L3_gnn_b1"]).reshape(2, P).T,
        "w32": inputs["L3_gnn_W2"],
        "b32": inputs["L3_gnn_b2"],
    }
    nc = bacc.Bacc("TRN2", target_bir_lowering=False, num_devices=1)
    fed, aps = {}, {}
    for name, a in arrays.items():
        a = np.ascontiguousarray(a)
        fed[f"in_{name}"] = a
        aps[name] = nc.dram_tensor(f"in_{name}", a.shape, mybir.dt.from_np(a.dtype), kind="ExternalInput").ap()
    aps["out"] = nc.dram_tensor("out_0", (N_NODES, D), fp32, kind="ExternalOutput").ap()
    build(nc, **aps)
    r = run_bass_kernel_spmd(nc, [fed], core_ids=[0])
    return r.results[0]["out_0"]
```

```python
import concourse.bass as bass
from concourse import mybir
from contextlib import ExitStack

fp32 = mybir.dt.float32
i32 = mybir.dt.int32
bf16 = mybir.dt.bfloat16
ALU = mybir.AluOpType
ACT = mybir.ActivationFunctionType
AX = mybir.AxisListType

P = 128
N_NODES = 50000
N_EDGES = 25000
D = 128
HEADS = 8
HD = D // HEADS
J = -(-N_EDGES // P)
SLOTS = P * J
ET = 4
EG = J // ET
NT = 8
NGRP = -(-N_NODES // (P * NT))
NPAD = NGRP * P * NT
TAIL = (N_NODES - (NGRP - 1) * P * NT) // NT
EXT = D + 2
ROWS = SLOTS + N_NODES
SKIP = 60000
BIG = 1.0e38
LN_EPS = 1e-5
SCAN = HEADS + D
SPREAD = EG * (ET + 1) - 1
assert EG == NGRP and EG % 2 == 1
PAIRS = EG // 2


class Chain:

    def __init__(self, eng, sem):
        self.base = sem.base if isinstance(sem, From) else 0
        self.sem = sem.sem if isinstance(sem, From) else sem
        self.eng, self.off, self.n = eng, self.base, 0

    def start(self, g, per, shift=0):
        self.off, self.n, self.per = g * per + (shift + self.base), 0, per

    def finish(self):
        assert self.n == self.per, (self.n, self.per)

    def inc(self, ins):
        self.n += 1
        ins.then_inc(self.sem, 1)

    def sync(self):
        hold(self.eng, self.sem, self.off + self.n)

    def fused(self):
        self.eng.wait_ge(self.sem, self.off + self.n)

    def link(self, ins):
        self.inc(ins)
        self.sync()


class From:

    def __init__(self, sem, base):
        self.sem, self.base = sem, base


def hold(eng, sem, value):
    if isinstance(sem, From):
        sem, value = sem.sem, value + sem.base
    eng.wait_ge(sem, value)
    if not isinstance(value, int):
        eng.nop(nofuse=True)


def back(g):
    return g * -1 + (EG - 1)


def skewed(eng, parts, n=2):
    top = max(lag for _, lag in parts)
    start = -(-(top + n) // n) * n
    assert EG % n == 1

    def one(s):
        for part, lag in parts:
            g = s - lag
            if 0 <= g < EG:
                part(g, g % n, g // n, g < n)
    for s in range(start):
        one(s)
    with eng.Fori(start // n, EG // n) as t:
        for q in range(n):
            for part, lag in parts:
                b = (q - lag) % n
                part(t * n + (q - lag), b, t + (q - lag - b) // n, False)
    for s in range(EG - 1, EG + top):
        one(s)


def groups(eng, body):
    body(0, 0, 0, True)
    body(1, 1, 0, True)
    with eng.Fori(1, PAIRS) as t:
        body(t * 2, 0, t, False)
        body(t * 2 + 1, 1, t, False)
    body(EG - 1, 0, PAIRS, False)


def build(nc, x, src, dst, ew, ea, w0t, w_attn, bias0, w_src, w_dst, attn, w_out, b_out, gamma, beta,
          w2, a_src, a_dst, b2, w31, b31, w32, b32, out):
    ctx = ExitStack()
    with ctx:
        def sb(name, shape, dt=fp32):
            return ctx.enter_context(nc.sbuf_tensor(name, shape, dt))

        def sem(name):
            return ctx.enter_context(nc.semaphore(name))

        def two(name):
            return [sem(f"{name}{b}") for b in range(2)]

        def dram(name, shape, dt=fp32):
            return nc.dram_tensor(name, shape, dt, kind="Internal").ap()

        slot_of_node = dram("slot_of_node", (NPAD, 1), i32)
        x0_dst = dram("x0_dst", (SLOTS, D))
        t1 = dram("t1", (ROWS, D))
        x2s = [dram(f"x2s{m}", (SLOTS, D)) for m in range(3)]
        t2 = [dram(f"t2_{m}", (ROWS, EXT)) for m in range(3)]
        t3 = dram("t3", (ROWS, D))
        acc = dram("acc", (N_NODES + P, D))

        ident = sb("ident", [P, P])
        ones3 = sb("ones3", [3, P], bf16)
        zero = sb("zero", [P, 1])
        one = sb("one", [P, 1])
        tri = sb("tri", [P, P])
        src_i = sb("src_i", [P, J], i32)
        dst_i = sb("dst_i", [P, J], i32)
        key = sb("key", [P, J])
        src_f = sb("src_f", [P, J])
        lew = sb("lew", [P, J])
        cont = sb("cont", [P, J + 1])
        pen = sb("pen", [P, J + 1])
        firstm = sb("firstm", [P, J])
        firstpen = sb("firstpen", [P, J])
        lastpen = sb("lastpen", [P, J])
        lastm = sb("lastm", [P, J])
        endm = sb("endm", [P, J])
        endpen = sb("endpen", [P, J])
        kfn = sb("kfn", [P, 2], i32)
        kx = sb("kx", [P, 2])
        cols = sb("cols", [P, 6])
        crep = sb("crep", [P, 4, 8])
        rows = sb("rows", [8, 4, P])
        slot_i = sb("slot_i", [P, J], i32)
        gsrc = sb("gsrc", [P, J], i32)
        gdst = sb("gdst", [P, J], i32)
        dscat = sb("dscat", [P, J], i32)
        left = sb("left", [P, P])
        right = sb("right", [P, P])
        node_i = sb("node_i", [P, NPAD // P], i32)
        cur = sb("cur", [P, 2, ET], i32)
        cur2 = sb("cur2", [P, 2, ET], i32)
        dstc = sb("dstc", [P, J], i32)

        w0 = sb("w0", [P, D + HEADS])
        wa_bc = sb("wa_bc", [P, HD])
        wsrc = sb("wsrc", [P, D])
        wdst = sb("wdst", [P, D])
        attn_bc = sb("attn_bc", [P, D])
        wout = sb("wout", [P, D])
        bias_bc = sb("bias_bc", [P, D])
        bo_bc = sb("bo_bc", [P, D])
        gam_bc = sb("gam_bc", [P, D])
        bet_bc = sb("bet_bc", [P, D])
        wext = sb("wext", [P, 3, EXT])
        brow = sb("brow", [3, 5, EXT])
        b3 = sb("b3", [3, 5, EXT], bf16)
        w31a = sb("w31a", [P, 2 * D])
        w31b = sb("w31b", [P, 2 * D])
        w31c = sb("w31c", [64, 2 * D])
        b31c = sb("b31c", [P, 2])
        w32s = sb("w32s", [P, 2, D])

        H = sb("H", [P, J, EXT])
        S = sb("S", [P, HEADS, J])
        F = sb("F", [P, HEADS, J])
        B = sb("B", [P, HEADS, J])
        colv = sb("colv", [P, HEADS])
        colc = sb("colc", [P, HEADS])
        rowd = sb("rowd", [HEADS, P])
        rowc = sb("rowc", [HEADS, P])
        Cf = sb("Cf", [P, D + HEADS])
        es = sb("es", [P, J])
        dd = sb("dd", [P, J])
        sdt = sb("sdt", [P, J, 2])
        slot_f = sdt[:, 0:J // 2, :].rearrange("p j c -> p (j c)")
        bufa = sb("bufa", [P, 2, NT, D])
        bufb = sb("bufb", [P, 2, NT, D])
        bufc = sb("bufc", [P, NT, D])
        bufd = sb("bufd", [P, NT, D])
        bufT = sb("bufT", [P, 2, NT, D])
        trow = sb("trow", [P, 3, NT, EXT])
        gbuf = sb("gbuf", [P, 2, ET, EXT])
        av = bufb[:, 0, 0:6, :].rearrange("p (m t) f -> p m t f", m=3)
        w0a = bufd[:, 2, :]
        eab = trow[:, 0:2, :, :].rearrange("p b r e -> p b (r e)")[:, :, 0:ET * 64].rearrange(
            "p b (j f) -> p b j f", f=64)
        eaT = trow[0:64, 2, :, :].rearrange("p r e -> p (r e)")[:, 0:ET * P]
        srep = bufd[:, ET:2 * ET, :]
        cnt = sb("cnt", [P, ET])
        idf = sb("idf", [P, ET])
        idx_add = sb("idx_add", [P, 2, ET], i32)
        real = sb("real", [P, J])
        spare = sb("spare", [P, 1])
        spare_i = sb("spare_i", [P, 1], i32)
        st = sb("st", [P, 4, NT, 6])
        mvs = sb("mvs", [P, 4, 2, NT, 2])
        rs = sb("rs", [P, 4, 2, NT])
        nmr = sb("nmr", [P, 4, NT])
        half = sb("half", [P, NT])
        Hflat = H[:, :, :].rearrange("p j e -> p (j e)")
        n_dense = [0]

        def dense_buf(n):
            at = n_dense[0]
            n_dense[0] += n * NT * D
            return Hflat[:, at:at + n * NT * D].rearrange("p (b r f) -> p b r f", b=n, f=D)
        fx, fy = (Hflat[:, n * 4 * NT * D:(n + 1) * 4 * NT * D].rearrange("p (b r f) -> p b r f", b=4, f=D)
                  for n in range(2))
        at3 = 2 * 4 * NT * D
        same = Hflat[:, at3:at3 + 2 * ET * P].rearrange("p (b i q) -> p b i q", b=2, i=ET)
        dx, da, dx1, dy, dt_, dx2, dxm, dx3 = (dense_buf(n) for n in (2, 2, 2, 2, 2, 2, 2, 2))
        dsig, dT, du = dense_buf(3), dense_buf(3), dense_buf(2)
        PS = [ctx.enter_context(nc.psum_tensor(f"ps{i}", [P, 512], fp32)) for i in range(8)]

        def bc(ap, n):
            return ap.unsqueeze(1).broadcast_to([P, n, D])

        def rows4(ap, g):
            return ap[0:SLOTS, :].rearrange("(p j) w -> p j w", p=P)[:, bass.ds(g * ET, ET), :]

        def node_rows(ap, g, off=0, parts=P):
            return ap[bass.ds(off + g * (P * NT), parts * NT), :].rearrange("(p r) w -> p r w", r=NT)

        s_ld = sem("s_loads")
        s_pset = sem("s_pool_setup")
        s_vset = sem("s_dve_setup")
        s_eset = sem("s_pe_setup")
        s_aset = sem("s_act_setup")
        s_slots = sem("s_slot_table_set")
        s_scat = two("s_slots_scattered")
        s_gmap = two("s_rows_looked_up")
        K6, K5 = range(6), range(5)
        s_ga = [two(f"s_gathered{k}_") for k in K6]
        s_idx = sem("s_indices_copied")
        at = [0]

        def idx(n):
            at[0] += n * EG
            return From(s_idx, at[0] - n * EG)
        gi0, s_scq, s_mapq, gi1, gi2, gi3, gi4, s_asq, gi5 = (idx(n) for n in (2, 2, 2, 1, 1, 1, 1, 1, 1))
        s_gi = [gi0, gi1, gi2, gi3, gi4, gi5]
        s_tr = [sem(f"s_transposed{k}") for k in (0, 1)]
        s_ev = [sem(f"s_evacuated{k}") for k in (0, 1)]
        s_mm = [sem(f"s_projected{k}") for k in (0, 1)]
        s_he = [sem(f"s_h_kept{k}") for k in K5]
        s_sv = [sem(f"s_scored{k}") for k in (0, 1)]
        s_xst = two("s_x0dst_stored")
        s_sm = [sem(f"s_softmax{k}") for k in K5]
        s_moved, s_exp, s_scan = sem("s_softmax_moved"), sem("s_softmax_exp"), sem("s_scanned")
        s_smp = [From(s_moved, n) for n in (0, 5, 10, 16, 22)]
        s_sme = [From(s_exp, n) for n in (0, 1, 2, 4, 6)]
        s_b = [From(s_scan, k * SCAN + (SPREAD if k else 0)) for k in K5]
        s_sp = {1: From(s_scan, SCAN), 5: From(s_scan, 5 * SCAN + SPREAD)}
        CLD = [16, 16, 16, 16, 16]
        s_states_in = two("s_states_loaded")
        CSD = {2: 16, 3: 16, 4: 32}
        s_cx = {k: [From(s_states_in[b], (PAIRS + 1 - b) * 16 * (k - 2)) for b in range(2)] for k in CSD}
        s_slots_in = two("s_slots_loaded")
        s_cl = [[From(s_slots_in[b], (PAIRS + 1 - b) * 16 * (k + (k > 0))) for b in range(2)] for k in K5]
        s_raw = {k: [From(s_slots_in[b], (PAIRS + 1 - b) * 16 * (k + (k > 1))) for b in range(2)] for k in (1, 5)}
        s_agg = [sem(f"s_aggregated{k}") for k in K5]
        s_y = {k: sem(f"s_slot_y{k}") for k in (1, 4)}
        s_z = sem("s_slot_z")
        s_xo = [sem(f"s_slot_out{k}") for k in K5]
        s_sg = {k: sem(f"s_slot_sigmoid{k}") for k in (2, 3, 4)}
        s_ct = {k: sem(f"s_slot_turned{k}") for k in (1, 2, 3)}
        s_ce = {k: sem(f"s_slot_T_kept{k}") for k in (1, 2, 3)}
        s_cm = {k: sem(f"s_slot_rows{k}") for k in (1, 2, 3)}
        s_cr = {k: sem(f"s_slot_rows_kept{k}") for k in (1, 2, 3)}
        s_wt, s_we, s_wm = sem("s_agg_turned"), sem("s_agg_T_kept"), sem("s_wout_product")
        s_rc = {k: sem(f"s_slot_rstd{k}") for k in (0, 1, 4)}
        s_rc2 = sem("s_slot_rstd_second")
        s_ys = sem("s_slot_y_scaled")
        s_xb = sem("s_slot_x_beta")
        s_slots_out, s_rows_out = two("s_slots_stored"), two("s_rows_stored")
        s_cs = [[From(s_slots_out[b], (PAIRS + 1 - b) * 16 * k) for b in range(2)] for k in K5]
        s_ts = {k: [From(s_rows_out[b], (PAIRS + 1 - b) * 16 * (k - 1)) for b in range(2)] for k in (1, 2, 3)}
        s_asc = two("s_acc_rows_scattered")
        s_accp = sem("s_acc_padding")
        s_dl = two("s_nodes_loaded")
        s_da_ = sem("s_dense_a")
        s_dtt = sem("s_dense_t")
        s_A = [sem(f"s_dense_A{n}") for n in range(5)]
        s_Bm = [sem(f"s_dense_B{m}") for m in range(3)]
        s_rd = [sem(f"s_dense_rstd{n}") for n in range(4)]
        s_dT = [sem(f"s_dense_turned{m}") for m in range(3)]
        s_dE = [sem(f"s_dense_T_kept{m}") for m in range(3)]
        s_dM = [sem(f"s_dense_product{m}") for m in range(3)]
        s_dS = [sem(f"s_dense_sigmoid{m}") for m in range(3)]
        s_dR = [sem(f"s_dense_rows_kept{m}") for m in range(3)]
        s_du = sem("s_dense_x2_added")
        s_dN = sem("s_dense_x3")
        s_dx1 = two("s_x1_stored")
        s_dx3 = two("s_x3_stored")
        s_dt2 = [sem(f"s_t2_stored{m}") for m in range(3)]
        s_el = two("s_edge_attr_loaded")
        s_ma = sem("s_message_act")
        s_mp = sem("s_message_pe")
        s_mv = sem("s_message_dve")
        s_m1, s_m2, s_m3 = (From(s_ct[k], EG) for k in (1, 2, 3))
        s_a1, s_a2, s_a3 = (From(s_ce[k], EG) for k in (1, 2, 3))
        s_add = sem("s_messages_added")
        s_fl = [sem(f"s_final_loaded{b}") for b in range(4)]
        s_fs = [sem(f"s_final_stored{b}") for b in range(4)]
        s_fv = sem("s_final_dve")
        s_fv2 = sem("s_final_out")
        s_fr = sem("s_final_rstd")

        MV = 1 + ET + 7
        AGG = [4 + 1 + 2 + 2 * ET, ET + 1, 2 * ET, 2 * ET, 2 * ET]
        XO = [ET, 1, 1, 1, ET]
        Z1 = 2 + 2 * ET
        DA1, DA2, DA3 = 2 * NT, 1 + NT + 2 * NT, NT + 2 + 2 * NT
        DB = [1, 1, 1 + 2 * NT]
        mark = {}
        block = ctx.enter_context(nc.Block())
        N_LOADS = 26
        heads = [HEADS, HEADS, 1, 1, 1]

        @block.vector
        def _(dve):
            v = nc.vector
            c = Chain(dve, s_vset)

            for t, val in ((half, -0.5), (zero, 0.0), (one, 1.0)):
                c.inc(v.memset(t[:], val))
            c.inc(v.memset(cont[:], 0.0))
            dve.wait_ge(s_ld, 16 * N_LOADS)
            c.inc(v.tensor_copy(key[:], dst_i[:]))
            c.inc(v.tensor_copy(src_f[:], src_i[:]))
            c.inc(v.tensor_copy(kx[:], kfn[:]))
            dve.wait_ge(s_pset, 5)
            c.inc(v.tensor_copy(slot_f[:], slot_i[:]))
            c.sync()
            kf, kl = key[:, 0:1], key[:, J - 1:J]
            c.inc(v.tensor_tensor(cont[:, 1:J], key[:, 1:J], key[:, 0:J - 1], ALU.is_equal))
            c.inc(v.tensor_scalar(firstm[:], key[:], kf, None, ALU.is_equal))
            c.inc(v.tensor_scalar(lastm[:], key[:], kl, None, ALU.is_equal))
            c.inc(v.tensor_scalar(dstc[:], key[:], float(N_NODES - 1), None, ALU.min))
            c.inc(v.tensor_tensor(cols[:, 0:1], kf, kx[:, 1:2], ALU.is_equal))
            c.inc(v.tensor_tensor(cols[:, 1:2], kf, kl, ALU.is_equal))
            c.inc(v.tensor_tensor(cols[:, 2:3], kl, kx[:, 0:1], ALU.is_equal))
            c.sync()
            c.inc(v.tensor_scalar(pen[:], cont[:], 1.0, BIG, ALU.subtract, ALU.mult))
            c.inc(v.tensor_scalar(firstpen[:], firstm[:], 1.0, BIG, ALU.subtract, ALU.mult))
            c.inc(v.tensor_scalar(lastpen[:], lastm[:], 1.0, BIG, ALU.subtract, ALU.mult))
            c.inc(v.tensor_tensor(cols[:, 3:4], cols[:, 0:1], cols[:, 1:2], ALU.mult))
            c.inc(v.tensor_tensor(cols[:, 4:5], cols[:, 2:3], cols[:, 1:2], ALU.mult))
            c.inc(v.tensor_scalar(endm[:], cont[:, 1:J + 1], -1.0, 1.0, ALU.mult, ALU.add))
            c.sync()
            c.link(v.tensor_scalar(endm[:, J - 1:J], cols[:, 2:3], -1.0, 1.0, ALU.mult, ALU.add))
            c.inc(v.tensor_scalar(endpen[:], endm[:], 1.0, BIG, ALU.subtract, ALU.mult))
            c.inc(v.tensor_scalar(dd[:], key[:], float(SKIP), None, ALU.subtract))
            for n, q in enumerate((3, 0, 4, 2)):
                c.inc(v.tensor_scalar(crep[:, n, :], cols[:, q:q + 1].broadcast_to([P, 8]), 1.0, BIG,
                                      ALU.subtract, ALU.mult))
            c.inc(v.tensor_copy(bufc[:, 0, :], kf.broadcast_to([P, P])))
            c.inc(v.tensor_copy(bufc[:, 1, :], kl.broadcast_to([P, P])))
            c.sync()
            mark["rep"] = c.n
            c.link(v.tensor_tensor(dd[:], dd[:], endm[:], ALU.mult))
            c.inc(v.tensor_scalar(dscat[:], dd[:], float(SKIP), None, ALU.add))
            dve.wait_ge(s_eset, 1)
            c.inc(v.tensor_scalar(left[:], PS[0][:, 0:P], kl, None, ALU.is_equal))
            c.inc(v.tensor_scalar(right[:], PS[0][:, P:2 * P], kf, None, ALU.is_equal))
            c.link(v.tensor_copy(rows[:], PS[1][0:8, :].rearrange("h (n p) -> h n p", n=4)))
            mark["lr"] = c.n
            c.link(v.tensor_tensor(w0a.rearrange("p (h f) -> p h f", f=HD),
                                   w0[:, 0:D].rearrange("p (h f) -> p h f", f=HD),
                                   wa_bc[:].unsqueeze(1).broadcast_to([P, HEADS, HD]), ALU.mult))
            c.inc(v.tensor_reduce(w0[:, D:D + HEADS], w0a.rearrange("p (h f) -> p h f", f=HD), AX.X, ALU.add))
            for m in range(3):
                c.link(v.tensor_tensor(bufd[:, 0:2, :], wext[:, m, 0:D].unsqueeze(1).broadcast_to([P, 2, D]),
                                       av[:, m, :, :], ALU.mult))
                c.link(v.tensor_reduce(wext[:, m, D:EXT], bufd[:, 0:2, :], AX.X, ALU.add))

            t0, t1_, hi = (Hflat[0:3, n * 5 * EXT:(n + 1) * 5 * EXT].rearrange("p (n e) -> p n e", e=EXT)
                           for n in range(3))
            c.link(v.tensor_copy(b3[:], brow[:]))
            c.inc(v.tensor_copy(hi, b3[:]))
            c.sync()
            c.link(v.tensor_tensor(t0, brow[:], hi, ALU.subtract))
            c.link(v.tensor_scalar(brow[:], hi, ident[0:3, 0:1], None, ALU.mult))
            c.link(v.tensor_copy(b3[:], t0))
            c.link(v.tensor_copy(hi, b3[:]))
            c.link(v.tensor_tensor(t1_, t0, hi, ALU.subtract))
            c.link(v.scalar_tensor_tensor(brow[:], hi, ident[0:3, 1:2], brow[:], ALU.mult, ALU.add))
            c.link(v.scalar_tensor_tensor(brow[:], t1_, ident[0:3, 2:3], brow[:], ALU.mult, ALU.add))
            c.link(v.tensor_copy(b3[:], brow[:]))

            def spread(c, to, val, k_moved, sem_moved, name):
                c.link(v.tensor_tensor_scan(dd[:, ::-1], cont[:, J:0:-1], val[:, ::-1], 0.0, ALU.mult, ALU.add))
                mark[name] = c.n
                hold(dve, sem_moved, k_moved)
                c.link(v.tensor_copy(colc[:, 0:1], PS[1][:, 0:1]))
                c.link(v.scalar_tensor_tensor(to, lastm[:], colc[:, 0:1], dd[:], ALU.mult, ALU.add))

            c.inc(v.tensor_scalar(real[:], key[:], float(N_NODES), None, ALU.is_lt))
            dve.wait_ge(s_pset, 12)
            c.link(v.tensor_tensor(es[:], slot_f[:], endm[:], ALU.mult))
            spread(c, S[:, 0, :], es, 2, s_eset, "spread_slots")
            c.link(v.tensor_copy(gdst[:], S[:, 0, :]))
            c.link(v.tensor_copy(spare[:], spare_i[:]))
            mark["setup"] = c.n

            def stats(c, src_of, n, which, b):
                c.sync()
                for i in range(n):
                    c.inc(v.bn_stats(st[:, which, i, :], src_of(i)))
                c.sync()
                for i in range(n):
                    c.inc(v.bn_aggr(mvs[:, which, b, i, :], st[:, which, i, :]))

            def scale(c, src_of, dst_of, n, which, b):
                for i in range(n):
                    c.inc(v.tensor_scalar(dst_of(i), src_of(i), mvs[:, which, b, i, 0:1], rs[:, which, b, i:i + 1],
                                          ALU.subtract, ALU.mult))

            def softmax(k):
                c = Chain(dve, s_sm[k])
                nh = heads[k]
                hs = range(nh)
                if k == 0:
                    dve.wait_ge(s_sv[0], EG)
                    dve.wait_ge(s_aset, 1)
                    c.link(v.tensor_tensor(S[:], S[:], lew[:].unsqueeze(1).broadcast_to([P, HEADS, J]), ALU.add))
                    c.link(v.scalar_tensor_tensor(F[:], S[:], 0.01, S[:], ALU.mult, ALU.max))
                    c.link(v.tensor_copy(S[:], F[:]))
                elif k == 1:
                    dve.wait_ge(s_sv[1], 3 * EG)
                else:
                    dve.wait_ge(s_he[k], EG)
                    dve.wait_ge(s_cr[k - 1], EG * 4)
                    c.inc(v.tensor_tensor(es[:], sdt[:, :, 0], sdt[:, :, 1], ALU.add))
                    c.link(v.tensor_tensor(S[:, 1, :], sdt[:, :, 1], endm[:], ALU.mult))
                    c.link(v.scalar_tensor_tensor(es[:], es[:], 0.2, es[:], ALU.mult, ALU.max))
                    spread(c, S[:, 2, :], S[:, 1, :], 1, s_smp[k], f"spread{k}")
                    c.link(v.tensor_tensor(S[:, 1, :], H[:, :, D], S[:, 2, :], ALU.add))
                    c.link(v.scalar_tensor_tensor(S[:, 0, :], S[:, 1, :], 0.2, S[:, 1, :], ALU.mult, ALU.max))
                base = 1 if k >= 2 else 0
                for h in hs:
                    c.inc(v.tensor_tensor_scan(F[:, h, :], pen[:, 0:J], S[:, h, :], 0.0, ALU.add, ALU.max))
                c.sync()
                c.link(v.tensor_copy(colv[:, 0:nh], F[:, 0:nh, J - 1]))
                mark[f"colf{k}"] = c.n
                hold(dve, s_smp[k], base + 1)
                c.link(v.tensor_tensor_scan(rowd[0:nh, :], rows[0:nh, 0, :], PS[0][0:nh, 0:P], 0.0, ALU.add, ALU.max))
                c.inc(v.memset(rowc[0:nh, 0:1], -BIG))
                c.link(v.tensor_tensor(rowc[0:nh, 1:P], rowd[0:nh, 0:P - 1], rows[0:nh, 1, 1:P], ALU.add))
                mark[f"rowf{k}"] = c.n
                hold(dve, s_smp[k], base + 2)
                c.link(v.tensor_copy(colc[:, 0:nh], PS[1][:, 0:nh]))
                for h in hs:
                    c.inc(v.scalar_tensor_tensor(F[:, h, :], firstpen[:], colc[:, h:h + 1], F[:, h, :], ALU.add, ALU.max))
                c.sync()
                if k >= 2:
                    c.link(v.tensor_tensor(S[:, 1, :], es[:], endpen[:], ALU.add))
                    c.link(v.tensor_tensor(F[:, 0, :], F[:, 0, :], S[:, 1, :], ALU.max))
                for h in hs:
                    c.inc(v.tensor_tensor_scan(B[:, h, ::-1], pen[:, J:0:-1], F[:, h, ::-1], 0.0, ALU.add, ALU.max))
                c.sync()
                c.link(v.tensor_copy(colv[:, 0:nh], B[:, 0:nh, 0]))
                mark[f"colb{k}"] = c.n
                hold(dve, s_smp[k], base + 3)
                c.link(v.tensor_tensor_scan(rowd[0:nh, ::-1], rows[0:nh, 2, ::-1], PS[0][0:nh, P - 1::-1], 0.0,
                                            ALU.add, ALU.max))
                c.inc(v.memset(rowc[0:nh, P - 1:P], -BIG))
                c.link(v.tensor_tensor(rowc[0:nh, 0:P - 1], rowd[0:nh, 1:P], rows[0:nh, 3, 0:P - 1], ALU.add))
                mark[f"rowb{k}"] = c.n
                hold(dve, s_smp[k], base + 4)
                c.link(v.tensor_copy(colc[:, 0:nh], PS[1][:, 0:nh]))
                for h in hs:
                    c.inc(v.scalar_tensor_tensor(B[:, h, :], lastpen[:], colc[:, h:h + 1], B[:, h, :], ALU.add, ALU.max))
                c.sync()
                c.link(v.tensor_tensor(S[:, 0:nh, :], S[:, 0:nh, :], B[:, 0:nh, :], ALU.subtract))
                if k >= 2:
                    c.link(v.tensor_tensor(es[:], es[:], B[:, 0, :], ALU.subtract))
                    c.link(v.tensor_tensor(es[:], es[:], endm[:], ALU.mult))
                mark[f"exp{k}"] = c.n
                hold(dve, s_sme[k], 2 if k >= 2 else 1)
                for h in hs:
                    c.inc(v.tensor_tensor_scan(F[:, h, :], cont[:, 0:J], S[:, h, :], 0.0, ALU.mult, ALU.add))
                c.sync()
                mark[f"sums{k}"] = c.n
                return c

            def scan_messages(k, cs):
                c = Chain(dve, s_b[k])
                if k < 2:
                    dve.wait_ge(s_he[k], EG * (k + 1))
                cols_of = [H[:, :, h * HD:(h + 1) * HD] for h in range(HEADS)]
                for h, hv in enumerate(cols_of):
                    w = S[:, h % heads[k], :].unsqueeze(2).broadcast_to([P, J, HD])
                    c.inc(v.tensor_tensor(hv, hv, w, ALU.mult))
                c.sync()
                with dve.Fori(0, HD) as f8:
                    for f in range(HEADS):
                        hf = H[:, :, bass.ds(f8 * HEADS + f, 1)].rearrange("p j f -> p (j f)")
                        v.tensor_tensor_scan(hf, cont[:, 0:J], hf, 0.0, ALU.mult, ALU.add).then_inc(s_scan, 1)
                hold(dve, s_b[k], SCAN)
                c = cs
                nh = heads[k]
                hold(dve, s_smp[k], (5 if k < 2 else 6))
                c.link(v.tensor_copy(Cf[:, 0:D + nh], PS[0][:, 0:D + nh]))
                mark[f"cf{k}"] = c.n
                for h in range(nh):
                    c.inc(v.scalar_tensor_tensor(F[:, h, :], firstm[:], Cf[:, D + h:D + h + 1], F[:, h, :], ALU.mult, ALU.add))
                c.sync()
                if k == 0:
                    c.link(v.tensor_scalar(F[:], F[:], 1e-30, None, ALU.max))
                elif k == 1:
                    c.link(v.tensor_scalar(F[:], F[:], 1e-8, None, ALU.add))
                else:
                    c.link(v.tensor_tensor(F[:, 0, :], F[:, 0, :], es[:], ALU.add))
                    c.link(v.tensor_scalar(F[:, 0, :], F[:, 0, :], 1e-16, None, ALU.add))
                c.link(v.reciprocal(B[:, 0:nh, :], F[:, 0:nh, :]))

            def slot_update(k):
                def quad(t, b):
                    return t[:, b * ET:(b + 1) * ET, :]

                def aggregate(g, b, r, first):
                    c = Chain(dve, s_agg[k])
                    c.start(g, AGG[k])
                    hold(dve, s_cl[k][b], r * CLD[k] + CLD[k])
                    for i in range(ET):
                        hj = H[:, bass.ds(g * ET + i, 1), 0:D].rearrange("p a f -> p (a f)")
                        c.inc(v.scalar_tensor_tensor(hj, Cf[:, 0:D], firstm[:, bass.ds(g * ET + i, 1)], hj, ALU.mult, ALU.add))
                    c.sync()
                    if k >= 2:
                        for i in range(ET):
                            hj = H[:, bass.ds(g * ET + i, 1), 0:D].rearrange("p a f -> p (a f)")
                            c.inc(v.scalar_tensor_tensor(hj, gbuf[:, b, i, 0:D], es[:, bass.ds(g * ET + i, 1)], hj,
                                                         ALU.mult, ALU.add))
                        c.finish()
                        return
                    if not first and k == 1:
                        hold(dve, s_wt, g - 1)
                    hg = H[:, bass.ds(g * ET, ET), 0:D]
                    to = quad(bufc, b)
                    if heads[k] == 1:
                        c.inc(v.tensor_tensor(to, hg, B[:, 0, bass.ds(g * ET, ET)].unsqueeze(2).broadcast_to([P, ET, D]), ALU.mult))
                    else:
                        c.inc(v.tensor_tensor(to.rearrange("p j (h f) -> p j h f", f=HD),
                                              hg.rearrange("p j (h f) -> p j h f", f=HD),
                                              B[:, :, bass.ds(g * ET, ET)].rearrange("p h j -> p j h").unsqueeze(3).broadcast_to([P, ET, HEADS, HD]),
                                              ALU.mult))
                    if k == 0:
                        c.sync()
                        c.link(v.tensor_tensor(to, to, bufa[:, b, 0:ET, :], ALU.add))
                        c.inc(v.tensor_tensor(to, to, bc(bias_bc[:], ET), ALU.add))
                        stats(c, lambda i: bufc[:, b * ET + i, :], ET, 0, b)
                    c.finish()

                def stored_before(g, b, r, first):
                    if not first:
                        hold(dve, s_cs[k][b], r * 16)
                        if k == 4:
                            hold(dve, s_asc[b], r * 64)

                def out0(g, b, r, first):
                    c = Chain(dve, s_xo[k])
                    c.start(g, ET)
                    hold(dve, s_rc[0], g * 2 + 2)
                    hold(dve, s_agg[0], g * AGG[0] + AGG[0])
                    stored_before(g, b, r, first)
                    scale(c, lambda i: bufc[:, b * ET + i, :], lambda i: bufb[:, b, i, :], ET, 0, b)
                    c.finish()

                def y1(g, b, r, first):
                    c = Chain(dve, s_y[1])
                    c.start(g, 1 + 2 * ET)
                    hold(dve, s_wm, g + 1)
                    if not first:
                        hold(dve, s_z, g * Z1 - Z1)
                    c.inc(v.tensor_tensor(quad(bufd, b), PS[2][:, :].rearrange("p (j f) -> p j f", f=D),
                                          bufa[:, b, 0:ET, :], ALU.add))
                    stats(c, lambda i: bufd[:, b * ET + i, :], ET, 0, b)
                    c.finish()

                def z1(g, b, r, first):
                    c = Chain(dve, s_z)
                    c.start(g, Z1)
                    hold(dve, s_ys, g + 1)
                    hold(dve, s_xb, g + 1)
                    c.link(v.tensor_tensor(quad(bufd, b), quad(bufd, b), bc(gam_bc[:], ET), ALU.mult))
                    if not first:
                        hold(dve, s_xo[1], g - 1)
                    c.inc(v.tensor_tensor(bufb[:, b, ET:2 * ET, :], quad(bufd, b), bufa[:, b, ET:2 * ET, :], ALU.add))
                    stats(c, lambda i: bufb[:, b, ET + i, :], ET, 1, b)
                    c.finish()

                def out2(g, b, r, first):
                    c = Chain(dve, s_xo[k])
                    c.start(g, 1)
                    hold(dve, s_sg[k], g + 1)
                    hold(dve, s_cx[k][b], r * 16 + 16)
                    stored_before(g, b, r, first)
                    if not first:
                        hold(dve, s_ct[k], g - 1)
                    c.inc(v.tensor_tensor(bufb[:, b, 0:ET, :], bufa[:, b, 0:ET, :], quad(bufd, b), ALU.add))
                    c.finish()

                def y4(g, b, r, first):
                    c = Chain(dve, s_y[4])
                    c.start(g, 2 + 2 * ET)
                    hold(dve, s_sg[4], g + 1)
                    hold(dve, s_cx[4][b], r * 32 + 32)
                    if not first:
                        hold(dve, s_xo[4], g * ET - ET)
                    t = bufb[:, b, ET:2 * ET, :]
                    c.link(v.tensor_tensor(t, bufa[:, b, 0:ET, :], quad(bufd, b), ALU.add))
                    c.inc(v.tensor_tensor(t, t, bufa[:, b, ET:2 * ET, :], ALU.add))
                    stats(c, lambda i: bufb[:, b, ET + i, :], ET, 0, b)
                    c.finish()

                def out4(g, b, r, first):
                    c = Chain(dve, s_xo[4])
                    c.start(g, ET)
                    hold(dve, s_rc[4], g * 2 + 2)
                    hold(dve, s_y[4], g * (2 + 2 * ET) + 2 + 2 * ET)
                    stored_before(g, b, r, first)
                    scale(c, lambda i: bufb[:, b, ET + i, :], lambda i: bufb[:, b, i, :], ET, 0, b)
                    c.finish()

                skewed(dve, {0: [(aggregate, 0), (out0, 1)],
                             1: [(y1, 1), (aggregate, 0), (z1, 2)],
                             2: [(aggregate, 0), (out2, 1)],
                             3: [(aggregate, 0), (out2, 1)],
                             4: [(aggregate, 0), (y4, 1), (out4, 2)]}[k])
                dve.wait_ge(s_agg[k], EG * AGG[k])
                dve.wait_ge(s_xo[k], EG * XO[k])

            def score0(g, b, r, first):
                hold(dve, s_mm[0], g + 1)
                v.tensor_copy(S[:, :, bass.ds(g * ET, ET)].rearrange("p h j -> p j h"),
                              PS[6 + b][:, 0:ET * HEADS].rearrange("p (j h) -> p j h", h=HEADS)).then_inc(s_sv[0], 1)

            groups(dve, score0)
            scan_messages(0, softmax(0))
            slot_update(0)

            def dense_a1(g, b, r, first):
                c = Chain(dve, s_A[0])
                c.start(g, DA1)
                hold(dve, s_da_, g + 1)
                stats(c, lambda i: da[:, b, i, :], NT, 0, b)
                c.finish()

            def dense_a2(g, b, r, first):
                c = Chain(dve, s_A[1])
                c.start(g, DA2)
                hold(dve, s_rd[0], g * 2 + 2)
                hold(dve, s_A[0], g * DA1 + DA1)
                if not first:
                    hold(dve, s_dx1[b], r * 16)
                    hold(dve, s_dtt, g - 1)
                scale(c, lambda i: da[:, b, i, :], lambda i: dx1[:, b, i, :], NT, 0, b)
                c.sync()
                if not first:
                    hold(dve, s_A[3], g - 1)
                c.inc(v.tensor_tensor(dy[:, b], dx1[:, b], bc(bo_bc[:], NT), ALU.add))
                stats(c, lambda i: dy[:, b, i, :], NT, 1, b)
                c.finish()

            def dense_a3(g, b, r, first):
                c = Chain(dve, s_A[2])
                c.start(g, DA3)
                hold(dve, s_rd[1], g * 2 + 2)
                hold(dve, s_A[1], g * DA2 + DA2)
                scale(c, lambda i: dy[:, b, i, :], lambda i: dy[:, b, i, :], NT, 1, b)
                c.sync()
                c.link(v.tensor_tensor(dy[:, b], dy[:, b], bc(gam_bc[:], NT), ALU.mult))
                hold(dve, s_dtt, g + 1)
                c.inc(v.tensor_tensor(dy[:, b], dy[:, b], dt_[:, b], ALU.add))
                stats(c, lambda i: dy[:, b, i, :], NT, 2, b)
                c.finish()

            def dense_b(m):
                def body(g, b, r, first):
                    c = Chain(dve, s_Bm[m])
                    c.start(g, DB[m])
                    hold(dve, s_dS[m], g * 3 + 3)
                    if m == 0:
                        hold(dve, s_A[3], g + 1)
                        if not first:
                            hold(dve, s_dN, g * NT - NT)
                    else:
                        hold(dve, s_Bm[m - 1], g * DB[m - 1] + DB[m - 1])
                    if m == 2:
                        hold(dve, s_du, g + 1)
                    c.inc(v.tensor_tensor(dxm[:, b], (dx2, dxm, du)[m][:, b], dsig[:, m], ALU.add))
                    if m == 2:
                        stats(c, lambda i: dxm[:, b, i, :], NT, 3, b)
                    c.finish()
                return body

            skewed(dve, [(dense_a1, 0), (dense_a3, 1), (dense_b(0), 2), (dense_a2, 0), (dense_b(2), 3),
                         (dense_b(1), 2)])

            def spread_rows(k):
                def body(g, b, r, first):
                    c = Chain(dve, s_sp[k])
                    start = isinstance(g, int) and g == 0
                    c.start(g, ET + 1, 0 if start else -1)
                    hold(dve, s_raw[k][b], r * 16 + 16)
                    if start:
                        hold(dve, s_ga[k][0], 80)
                    if not first:
                        hold(dve, s_tr[1] if k == 1 else s_m1, g - 1)
                    raw = gbuf[:, b, :, 0:D]
                    c.link(v.tensor_tensor(raw, raw, endm[:, bass.ds(back(g) * ET, ET)].unsqueeze(2).broadcast_to(
                        [P, ET, D]), ALU.mult))
                    for i in range(ET - 2 if start else ET - 1, -1, -1):
                        prev = bufa[:, b, ET + i + 1, :] if i < ET - 1 else bufa[:, 1 - b, ET, :]
                        c.link(v.scalar_tensor_tensor(bufa[:, b, ET + i, :], prev, cont[:, bass.ds(back(g) * ET + (i + 1), 1)],
                                                      gbuf[:, b, i, 0:D], ALU.mult, ALU.add))
                    if start:
                        c.n += 1
                    c.finish()
                return body

            def score1(g, b, r, first):
                c = Chain(dve, s_sv[1])
                c.start(g, 3)
                hold(dve, s_he[1], g * 2 + 2)
                c.link(v.tensor_tensor(bufb[:, b, 0:ET, :], bufb[:, b, 0:ET, :],
                                       PS[6 + b][:, :].rearrange("p (j f) -> p j f", f=D), ALU.max))
                c.link(v.tensor_tensor(bufb[:, b, 0:ET, :], bufb[:, b, 0:ET, :], bc(attn_bc[:], ET), ALU.mult))
                c.inc(v.tensor_reduce(S[:, :, bass.ds(back(g) * ET, ET)].rearrange("p h j -> p j h"),
                                      bufb[:, b, 0:ET, :].rearrange("p j (h f) -> p j h f", f=HD), AX.X, ALU.add))
                c.finish()

            skewed(dve, [(spread_rows(1), 0), (score1, 1)])
            scan_messages(1, softmax(1))
            slot_update(1)
            for k in (2, 3, 4):
                scan_messages(k, softmax(k))
                slot_update(k)

            def dedup(g, b, r, first):
                c = Chain(dve, s_mv)
                c.start(g, MV)
                sj = src_f[:, bass.ds(back(g) * ET, ET)]
                c.inc(v.tensor_copy(srep, sj.unsqueeze(2).broadcast_to([P, ET, P])))
                mark["srep"] = c.n
                hold(dve, s_m1, g + 1)
                if not first:
                    hold(dve, s_mp, g - 1)
                for i in range(ET):
                    c.inc(v.tensor_scalar(same[:, b, i, :], PS[3][:, i * P:(i + 1) * P],
                                          src_f[:, bass.ds(back(g) * ET + i, 1)], None, ALU.is_equal))
                mark["same"] = c.n
                c.sync()
                c.link(v.tensor_tensor(bufc[:, ET:2 * ET, :], same[:, b, :, :], bc(tri[:], ET), ALU.mult))
                c.link(v.tensor_reduce(cnt[:], bufc[:, ET:2 * ET, :], AX.X, ALU.add))
                c.link(v.tensor_scalar(cnt[:], cnt[:], 0.0, None, ALU.is_equal))
                c.link(v.tensor_tensor(cnt[:], cnt[:], real[:, bass.ds(back(g) * ET, ET)], ALU.mult))
                c.link(v.tensor_scalar(idf[:], sj, spare[:, 0:1], None, ALU.subtract))
                c.link(v.tensor_tensor(idf[:], idf[:], cnt[:], ALU.mult))
                if not first:
                    hold(dve, s_add, g * 64 - 64)
                c.link(v.tensor_scalar(idx_add[:, b, :], idf[:], spare[:, 0:1], None, ALU.add))
                c.finish()

            skewed(dve, [(spread_rows(5), 0), (dedup, 1)])
            dve.wait_ge(s_mv, EG * MV)

            def final_stats(g, b, r, first):
                c = Chain(dve, s_fv)
                c.start(g, 2 * NT)
                hold(dve, s_fl[b], r * 16 + 16)
                stats(c, lambda i: fx[:, b, i, :], NT, b, 0)
                c.finish()

            skewed(dve, [(final_stats, 0)], 4)

        @block.scalar
        def _(act):
            a = nc.scalar

            def move(to, of, sem_):
                a.activation(to, of, ACT.Copy).then_inc(sem_, 1)

            act.wait_ge(s_ld, 16 * N_LOADS)
            act.wait_ge(s_vset, 4)
            a.activation(lew[:], lew[:], ACT.Ln, bias=one[:, 0:1]).then_inc(s_aset, 1)

            def project(k):
                def body(g, b, r, first):
                    hold(act, s_tr[k], g + 1)
                    if not first:
                        hold(act, s_mm[k], g - 1)
                    move(bufT[:, b, 0:ET, :], PS[b][:, :].rearrange("p (j f) -> p j f", f=P), s_ev[k])
                    move(bufT[:, b, ET:2 * ET, :], PS[2 + b][:, :].rearrange("p (j f) -> p j f", f=P), s_ev[k])
                    hold(act, s_mm[k], g + 1)
                    move(H[:, bass.ds((back(g) if k else g) * ET, ET), 0:D], PS[4 + b][:, :].rearrange("p (j f) -> p j f", f=D), s_he[k])
                    if k == 1:
                        if not first:
                            hold(act, s_sv[1], g * 3 - 3)
                        a.activation(bufb[:, b, 0:ET, :], PS[6 + b][:, :].rearrange("p (j f) -> p j f", f=D),
                                     ACT.Copy, scale=0.2).then_inc(s_he[1], 1)
                groups(act, body)

            def exps(k):
                nh = heads[k]
                act.wait_ge(s_sm[k], mark[f"exp{k}"])
                a.activation(S[:, 0:nh, :], S[:, 0:nh, :], ACT.Exp).then_inc(s_exp, 1)
                if k >= 2:
                    a.activation(es[:], es[:], ACT.Exp).then_inc(s_exp, 1)

            def slot_update(k):
                if k == 0:
                    return
                def turn_agg(g, b, r, first):
                    hold(act, s_wt, g + 1)
                    if not first:
                        hold(act, s_wm, g)
                    move(bufT[:, 0, 0:ET, :], PS[0][:, :].rearrange("p (j f) -> p j f", f=P), s_we)

                def sigmoid(g, b, r, first):
                    hold(act, s_agg[k], g * AGG[k] + AGG[k])
                    if not first:
                        hold(act, s_y[4] if k == 4 else s_xo[k], (g - 1) * ((2 + 2 * ET) if k == 4 else 1))
                    for i in range(ET):
                        last = a.activation(bufd[:, b * ET + i, :],
                                            H[:, bass.ds(g * ET + i, 1), 0:D].rearrange("p a f -> p (a f)"),
                                            ACT.Sigmoid, scale=B[:, 0, bass.ds(g * ET + i, 1)])
                    last.then_inc(s_sg[k], 1)

                def y_scaled(g, b, r, first):
                    hold(act, s_rc[1], g * 4 + 4)
                    for i in range(ET):
                        y = bufd[:, b * ET + i, :]
                        last = a.activation(y, y, ACT.Identity, scale=rs[:, 0, b, i:i + 1], bias=nmr[:, b, i:i + 1])
                    last.then_inc(s_ys, 1)

                def out1(g, b, r, first):
                    hold(act, s_rc2, g * 4 + 4)
                    if not first:
                        hold(act, s_cs[1][b], r * 16)
                        hold(act, s_ct[1], g - 1)
                    for i in range(ET):
                        last = a.activation(bufb[:, b, i, :], bufb[:, b, ET + i, :], ACT.Identity,
                                            scale=rs[:, 1, b, i:i + 1], bias=nmr[:, 2 + b, i:i + 1])
                    last.then_inc(s_xo[1], 1)

                def keep_turned(g, b, r, first):
                    hold(act, s_ct[k], g + 1)
                    if not (isinstance(g, int) and g == 0):
                        hold(act, s_cm[k], g)
                    move(bufT[:, 1, 0:ET, :], PS[1][:, :].rearrange("p (j f) -> p j f", f=P), s_ce[k])

                def keep_rows(g, b, r, first):
                    hold(act, s_cm[k], g + 1)
                    if not first:
                        hold(act, s_ts[k][b], r * 16)
                    r3 = PS[3][:, 0:3 * EXT].rearrange("p (j e) -> p j e", e=EXT)
                    r4 = PS[4][:, 0:EXT].rearrange("p (j e) -> p j e", e=EXT)
                    move(trow[:, b, 0:3, :], r3, s_cr[k])
                    move(trow[:, b, 3:4, :], r4, s_cr[k])
                    move(sdt[:, bass.ds(g * ET, 3), :], r3[:, :, D:EXT], s_cr[k])
                    move(sdt[:, bass.ds(g * ET + 3, 1), :], r4[:, :, D:EXT], s_cr[k])

                skewed(act, {1: [(keep_turned, 5), (turn_agg, 0), (y_scaled, 1), (out1, 3), (keep_rows, 6)],
                             2: [(keep_rows, 3), (sigmoid, 0), (keep_turned, 2)],
                             3: [(keep_rows, 3), (sigmoid, 0), (keep_turned, 2)],
                             4: [(sigmoid, 0)]}[k])

            def dense_m(m):
                banks = 5 if m == 0 else 2

                def turned(g, b, r, first):
                    for q in range(2):
                        hold(act, s_dT[m], g * 2 + q + 1)
                        if q == 0 and not (isinstance(g, int) and g == 0):
                            hold(act, s_dM[m], g * 3)
                        move(dT[:, m, q * ET:(q + 1) * ET, :], PS[q][:, :].rearrange("p (j f) -> p j f", f=P), s_dE[m])

                def rows_out(g, b, r, first):
                    if not (isinstance(g, int) and g == 0):
                        hold(act, s_Bm[m], g * DB[m])
                        hold(act, s_dt2[m], g * 16)
                    for q, w in enumerate((3, 3, 2)):
                        hold(act, s_dM[m], g * 3 + q + 1)
                        a.activation(dsig[:, m, 3 * q:3 * q + w, :],
                                     PS[banks + q][:, 0:w * EXT].rearrange("p (j e) -> p j e", e=EXT)[:, :, 0:D],
                                     ACT.Sigmoid).then_inc(s_dS[m], 1)
                    for q, w in enumerate((3, 3, 2)):
                        move(trow[:, m, 3 * q:3 * q + w, :],
                             PS[banks + q][:, 0:w * EXT].rearrange("p (j e) -> p j e", e=EXT), s_dR[m])
                return turned, rows_out

            def dense_a4(g, b, r, first):
                hold(act, s_rd[2], g * 4 + 4)
                if not first:
                    hold(act, s_du, g - 1)
                    hold(act, s_dT[0], g * 2 - 2)
                for i in range(NT):
                    last = a.activation(dx2[:, b, i, :], dy[:, b, i, :], ACT.Identity, scale=rs[:, 2, b, i:i + 1],
                                        bias=nmr[:, 2 + b, i:i + 1])
                last.then_inc(s_A[3], 1)

            def dense_scale(g, b, r, first):
                hold(act, s_rd[3], g * 4 + 4)
                if not first:
                    hold(act, s_dx3[b], r * 32)
                for i in range(NT):
                    a.activation(dx3[:, b, i, :], dxm[:, b, i, :], ACT.Identity, scale=rs[:, 3, b, i:i + 1],
                                 bias=nmr[:, b, i:i + 1]).then_inc(s_dN, 1)

            project(0)
            exps(0)
            act.wait_ge(s_agg[0], EG * AGG[0])
            (turned0, rows0), (turned1, rows1), (turned2, rows2) = (dense_m(m) for m in range(3))
            skewed(act, [(turned0, 2), (turned2, 3), (rows0, 2), (rows2, 3), (turned1, 2), (dense_a4, 1), (rows1, 2),
                         (dense_scale, 3)])
            for q in range(2):
                hold(act, s_cs[0][q], (PAIRS + 1 - q) * 16)
                act.wait_ge(s_dx1[q], (PAIRS + 1 - q) * 16)
                act.wait_ge(s_dx3[q], (PAIRS + 1 - q) * 32)
            for m in range(3):
                act.wait_ge(s_dt2[m], EG * 16)
                act.wait_ge(s_Bm[m], EG * DB[m])
                act.wait_ge(s_dM[m], EG * 3)
            project(1)
            exps(1)
            slot_update(1)
            for k in (2, 3, 4):
                act.wait_ge(s_agg[k - 1], EG * AGG[k - 1])
                act.wait_ge(s_xo[k - 1], EG * XO[k - 1])

                def keep(g, b, r, first, k=k):
                    hold(act, s_ga[k][b], r * 64 + 64)
                    move(H[:, bass.ds(g * ET, ET), :], gbuf[:, b, :, :], s_he[k])
                groups(act, keep)
                exps(k)
                for q in range(2):
                    hold(act, s_ts[k - 1][q], (PAIRS + 1 - q) * 16)
                slot_update(k)
            for q in range(2):
                hold(act, s_cs[4][q], (PAIRS + 1 - q) * 16)
                act.wait_ge(s_asc[q], (PAIRS + 1 - q) * 64)

            def keep_inputs(g, b, r, first):
                hold(act, s_m1, g + 1)
                if not (isinstance(g, int) and g == 0):
                    hold(act, s_m2, g)
                for q in range(2):
                    move(bufT[:, 0, q * ET:(q + 1) * ET, :], PS[q][:, :].rearrange("p (j f) -> p j f", f=P), s_a1.sem)
                move(eaT, PS[2][0:64, :], s_a1.sem)

            def keep_hidden(g, b, r, first):
                hold(act, s_m2, g + 1)
                for q in range(2):
                    a.activation(bufT[:, 1, q * ET:(q + 1) * ET, :], PS[4 + q][:, :].rearrange("p (j f) -> p j f", f=P),
                                 ACT.Relu, bias=b31c[:, q:q + 1]).then_inc(s_a2.sem, 1)

            def keep_messages(g, b, r, first):
                hold(act, s_m3, g + 1)
                move(bufd[:, 0:ET, :], PS[6][:, :].rearrange("p (j f) -> p j f", f=D), s_a3.sem)

            def keep_sums(g, b, r, first):
                hold(act, s_mp, g + 1)
                if not first:
                    hold(act, s_add, g * 64 - 64)
                move(bufb[:, b, 0:ET, :], PS[7][:, :].rearrange("p (j f) -> p j f", f=D), s_ma)
            skewed(act, [(keep_inputs, 0), (keep_messages, 1), (keep_hidden, 0), (keep_sums, 1)])

            def final_scale(g, b, r, first):
                hold(act, s_fr, g * 4 + 4)
                if not first:
                    hold(act, s_fs[b], r * 16)
                for i in range(NT):
                    last = a.activation(fy[:, b, i, :], fx[:, b, i, :], ACT.Identity, scale=rs[:, b, 0, i:i + 1],
                                        bias=nmr[:, b, i:i + 1])
                last.then_inc(s_fv2, 1)
            skewed(act, [(final_scale, 0)], 4)

        @block.tensor
        def _(pe):
            t = nc.tensor

            def mm(to, w, m, start=True, stop=True):
                return t.matmul(to, w, m, start=start, stop=stop)

            pe.wait_ge(s_pset, 9)
            pe.wait_ge(s_vset, mark["rep"])
            t.transpose(PS[0][:, 0:P], bufc[:, 0, :], ident[:])
            t.transpose(PS[0][:, P:2 * P], bufc[:, 1, :], ident[:])
            for n in range(4):
                last = t.transpose(PS[1][0:8, n * P:(n + 1) * P], crep[:, n, :], ident[:])
            last.then_inc(s_eset, 1)
            pe.wait_ge(s_vset, mark["spread_slots"])
            pe.wait_ge(s_pset, 11)
            mm(PS[1][:, 0:1], right[:], dd[:, 0:1]).then_inc(s_eset, 1)
            pe.wait_ge(s_vset, mark["setup"])

            def project(k):
                def body(g, b, r, first):
                    if k == 0:
                        hold(pe, s_ga[0][b], r * 128 + 128)
                    else:
                        hold(pe, s_ga[1][b], r * 64 + (80 - 16 * b))
                        hold(pe, s_sp[1], g * (ET + 1) + ET)
                    for i in range(ET):
                        t.transpose(PS[b][:, i * P:(i + 1) * P], bufa[:, b, i, :], ident[:])
                    for i in range(ET):
                        last = t.transpose(PS[2 + b][:, i * P:(i + 1) * P], bufa[:, b, ET + i, :], ident[:])
                    last.then_inc(s_tr[k], 1)
                    hold(pe, s_ev[k], g * 2 + 2)
                    if not first:
                        hold(pe, s_he[k], (g - 1) * (k + 1))
                        hold(pe, s_sv[k], g - 1 if k == 0 else g * 3 - 5)
                    for i in range(ET):
                        xs, xd = bufT[:, b, i, :], bufT[:, b, ET + i, :]
                        o = PS[4 + b][:, i * D:(i + 1) * D]
                        if k == 0:
                            e = PS[6 + b][:, i * HEADS:(i + 1) * HEADS]
                            mm(o, xs, w0[:, 0:D])
                            mm(e, xs, w0[:, D:D + HEADS], stop=False)
                            last = mm(e, xd, w0[:, D:D + HEADS], start=False)
                        else:
                            e = PS[6 + b][:, i * D:(i + 1) * D]
                            mm(o, xs, wsrc[:])
                            mm(e, xs, wsrc[:], stop=False)
                            last = mm(e, xd, wdst[:], start=False)
                    last.then_inc(s_mm[k], 1)
                groups(pe, body)

            def softmax(k):
                nh = heads[k]
                if k >= 2:
                    pe.wait_ge(s_sm[k], mark[f"spread{k}"])
                    mm(PS[1][:, 0:1], right[:], dd[:, 0:1]).then_inc(s_moved, 1)
                for d in "fb":
                    pe.wait_ge(s_sm[k], mark[f"col{d}{k}"])
                    t.transpose(PS[0][0:nh, 0:P], colv[:, 0:nh], ident[:]).then_inc(s_moved, 1)
                    pe.wait_ge(s_sm[k], mark[f"row{d}{k}"])
                    t.transpose(PS[1][:, 0:nh], rowc[0:nh, :], ident[0:nh, 0:nh]).then_inc(s_moved, 1)
                pe.wait_ge(s_sm[k], mark[f"sums{k}"])
                hold(pe, s_b[k], SCAN)
                mm(PS[0][:, 0:D], left[:], H[:, J - 1, 0:D])
                mm(PS[0][:, D:D + nh], left[:], F[:, 0:nh, J - 1]).then_inc(s_moved, 1)

            def ext(m, to, xT, n):
                for i in range(n):
                    o = PS[to + i // 3][:, (i % 3) * EXT:(i % 3 + 1) * EXT]
                    mm(o, xT(i), wext[:, m, :], stop=False)
                    last = mm(o, ones3[:], b3[:, m, :], start=False)
                return last

            def slot_update(k):
                if k in (0, 4):
                    return

                def turn_agg(g, b, r, first):
                    hold(pe, s_agg[1], g * AGG[1] + AGG[1])
                    if not (isinstance(g, int) and g == 0):
                        hold(pe, s_we, g)
                    for i in range(ET):
                        last = t.transpose(PS[0][:, i * P:(i + 1) * P], bufc[:, b * ET + i, :], ident[:])
                    last.then_inc(s_wt, 1)

                def times_wout(g, b, r, first):
                    hold(pe, s_we, g + 1)
                    if not (isinstance(g, int) and g == 0):
                        hold(pe, s_y[1], g * (1 + 2 * ET))
                    for i in range(ET):
                        o = PS[2][:, i * D:(i + 1) * D]
                        mm(o, bufT[:, 0, i, :], wout[:], stop=False)
                        last = mm(o, ones3[:], b3[:, 3, 0:D], start=False)
                    last.then_inc(s_wm, 1)

                def turn_out(g, b, r, first):
                    hold(pe, s_xo[k], g * XO[k] + XO[k])
                    if not (isinstance(g, int) and g == 0):
                        hold(pe, s_ce[k], g)
                    for i in range(ET):
                        last = t.transpose(PS[1][:, i * P:(i + 1) * P], bufb[:, b, i, :], ident[:])
                    last.then_inc(s_ct[k], 1)

                def to_rows(g, b, r, first):
                    hold(pe, s_ce[k], g + 1)
                    if not (isinstance(g, int) and g == 0):
                        hold(pe, s_cr[k], g * 4)
                    ext(k - 1, 3, lambda i: bufT[:, 1, i, :], ET).then_inc(s_cm[k], 1)

                if k == 1:
                    skewed(pe, [(turn_agg, 0), (turn_out, 4), (times_wout, 0), (to_rows, 5)])
                else:
                    skewed(pe, [(turn_out, 0), (to_rows, 0)])

            def dense_m(m):
                banks = 5 if m == 0 else 2

                def turn(g, b, r, first):
                    hold(pe, s_A[3] if m == 0 else s_Bm[m - 1], g + 1)
                    start = isinstance(g, int) and g == 0
                    for q in range(2):
                        if m == 0 and not start:
                            hold(pe, s_dE[1], g * 2 + q - 1)
                        elif m == 1:
                            hold(pe, s_dE[0] if start else s_dE[2], 1 + q if start else g * 2 + q - 1)
                        elif m == 2 and isinstance(g, int) and g == EG - 1:
                            hold(pe, s_dE[1], g * 2 + q + 1)
                        elif m == 2:
                            hold(pe, s_dE[0], g * 2 + q + 3)
                        for i in range(ET):
                            xi = (dx2 if m == 0 else dxm)[:, b, q * ET + i, :]
                            last = t.transpose(PS[q][:, i * P:(i + 1) * P], xi, ident[:])
                        last.then_inc(s_dT[m], 1)

                def product(g, b, r, first):
                    if m == 0:
                        if not (isinstance(g, int) and g == 0):
                            hold(pe, s_dR[0], g * 3)
                    elif m == 1:
                        if not (isinstance(g, int) and g == 0):
                            hold(pe, s_dR[2], g * 3)
                    else:
                        hold(pe, s_dR[1], g * 3 + 3)
                    for i in range(NT):
                        if i % ET == 0:
                            hold(pe, s_dE[m], g * 2 + i // ET + 1)
                        o = PS[banks + i // 3][:, (i % 3) * EXT:(i % 3 + 1) * EXT]
                        mm(o, dT[:, m, i, :], wext[:, m, :], stop=False)
                        last = mm(o, ones3[:], b3[:, m, :], start=False)
                        if i in (2, 5, 7):
                            last.then_inc(s_dM[m], 1)
                return turn, product

            project(0)
            softmax(0)
            pe.wait_ge(s_sm[0], mark["cf0"])
            (turn0, product0), (turn1, product1), (turn2, product2) = (dense_m(m) for m in range(3))
            skewed(pe, [(turn0, 0), (turn2, 1), (product0, 0), (product2, 1), (turn1, 0), (product1, 0)])
            for m in range(3):
                pe.wait_ge(s_dR[m], EG * 3)
            project(1)
            softmax(1)
            pe.wait_ge(s_sm[1], mark["cf1"])
            slot_update(1)
            for k in (2, 3, 4):
                pe.wait_ge(s_cr[k - 1], EG * 4)
                softmax(k)
                pe.wait_ge(s_sm[k], mark[f"cf{k}"])
                slot_update(k)

            def turn_inputs(g, b, r, first):
                hold(pe, s_ga[5][b], r * 64 + (80 - 16 * b))
                hold(pe, s_sp[5], g * (ET + 1) + ET)
                hold(pe, s_el[b], r * 16 + 16)
                hold(pe, s_mv, g * MV + mark["srep"])
                if not (isinstance(g, int) and g == 0):
                    hold(pe, s_a1, g * 3)
                for i in range(ET):
                    at = slice(i * P, (i + 1) * P)
                    t.transpose(PS[0][:, at], bufa[:, b, i, :], ident[:])
                    t.transpose(PS[1][:, at], bufa[:, b, ET + i, :], ident[:])
                    t.transpose(PS[2][0:64, at], eab[:, b, i, :], ident[:])
                    last = t.transpose(PS[3][:, at], srep[:, i, :], ident[:])
                last.then_inc(s_m1.sem, 1)

            def hidden(g, b, r, first):
                hold(pe, s_a1, g * 3 + 3)
                if not (isinstance(g, int) and g == 0):
                    hold(pe, s_a2, g * 2)
                for q in range(2):
                    o = PS[4 + q][:, :]
                    at = slice(q * P, (q + 1) * P)
                    mm(o, w31a[:, at], bufT[:, 0, 0:ET, :].rearrange("p j f -> p (j f)"), stop=False)
                    mm(o, w31b[:, at], bufT[:, 0, ET:2 * ET, :].rearrange("p j f -> p (j f)"), start=False, stop=False)
                    last = mm(o, w31c[:, at], eaT, start=False)
                last.then_inc(s_m2.sem, 1)

            def messages(g, b, r, first):
                hold(pe, s_a2, g * 2 + 2)
                if not (isinstance(g, int) and g == 0):
                    hold(pe, s_a3, g)
                for i in range(ET):
                    o = PS[6][:, i * D:(i + 1) * D]
                    mm(o, bufT[:, 1, i, :], w32s[:, 0, :], stop=False)
                    mm(o, bufT[:, 1, ET + i, :], w32s[:, 1, :], start=False, stop=False)
                    last = mm(o, ones3[:], b3[:, 4, 0:D], start=False)
                last.then_inc(s_m3.sem, 1)

            def sums(g, b, r, first):
                hold(pe, s_a3, g + 1)
                hold(pe, s_mv, g * MV + mark["same"])
                if not (isinstance(g, int) and g == 0):
                    hold(pe, s_ma, g)
                for i in range(ET):
                    last = mm(PS[7][:, i * D:(i + 1) * D], same[:, b, i, :], bufd[:, i, :])
                last.then_inc(s_mp, 1)
            skewed(pe, [(turn_inputs, 0), (messages, 1), (hidden, 0), (sums, 1)])

        @block.gpsimd
        def _(pool):
            q = nc.gpsimd
            c = Chain(pool, s_pset)
            c.link(q.memset(ident[:], 0.0))
            c.inc(q.affine_select(out=ident[:], in_=ident[:], compare_op=ALU.not_equal, fill=1.0, base=0,
                                  pattern=[[-1, P]], channel_multiplier=1))
            c.link(q.memset(tri[:], 1.0))
            c.inc(q.affine_select(out=tri[:], in_=tri[:], compare_op=ALU.is_gt, fill=0.0, base=0,
                                  pattern=[[-1, P]], channel_multiplier=1))
            c.inc(q.iota(slot_i[:], pattern=[[1, J]], base=0, channel_multiplier=J))
            c.inc(q.iota(node_i[:], pattern=[[1, NPAD // P]], base=SLOTS, channel_multiplier=NPAD // P))
            c.inc(q.memset(kfn[:], -1))
            c.inc(q.memset(brow[:], 0.0))
            c.inc(q.memset(ones3[:], 1.0))
            c.sync()
            pool.wait_ge(s_vset, mark["lr"])
            c.inc(q.affine_select(out=left[:], in_=left[:], compare_op=ALU.is_gt, fill=0.0, base=0,
                                  pattern=[[1, P]], channel_multiplier=-1))
            c.inc(q.affine_select(out=right[:], in_=right[:], compare_op=ALU.is_gt, fill=0.0, base=0,
                                  pattern=[[-1, P]], channel_multiplier=1))
            c.link(q.iota(spare_i[:], pattern=[[0, 1]], base=N_NODES, channel_multiplier=1))
            pool.wait_ge(s_vset, mark["setup"])

            def fetch(table, idx, to, cur_, b, sem_):
                for i in range(ET):
                    q.indirect_dma_start(out=to(i), out_offset=None, in_=table,
                                         in_offset=bass.IndirectOffsetOnAxis(ap=cur_[:, b, i:i + 1], axis=0)
                                         ).then_inc(sem_, 16)

            def gather2(k, table, isrc, idst, free):
                def body(g, b, r, first):
                    c = Chain(pool, s_gi[k])
                    c.start(g, 2)
                    if not first:
                        hold(pool, s_ga[k][b], r * 128)
                        free(g, b, r)
                    c.inc(q.tensor_copy(cur[:, b, :], isrc[:, bass.ds(g * ET, ET)]))
                    c.inc(q.tensor_copy(cur2[:, b, :], idst[:, bass.ds(g * ET, ET)]))
                    c.sync()
                    fetch(table, None, lambda i: bufa[:, b, i, :], cur, b, s_ga[k][b])
                    fetch(table, None, lambda i: bufa[:, b, ET + i, :], cur2, b, s_ga[k][b])
                return body

            def free0(g, b, r):
                hold(pool, s_tr[0], g - 1)
                hold(pool, s_xst[b], r * 16)
            groups(pool, gather2(0, x[:, :], src_i, dstc, free0))

            pool.wait_ge(s_slots, 16)
            for b in range(2):
                pool.wait_ge(s_ga[0][b], (PAIRS + 1 - b) * 128)

            def scatter_slots(g, b, r, first):
                c = Chain(pool, s_scq)
                c.start(g, 2)
                if not first:
                    hold(pool, s_scat[b], r * 64)
                c.inc(q.tensor_copy(cur[:, b, :], dscat[:, bass.ds(g * ET, ET)]))
                c.inc(q.tensor_copy(cur2[:, b, :], slot_i[:, bass.ds(g * ET, ET)]))
                c.sync()
                for i in range(ET):
                    q.indirect_dma_start(out=slot_of_node[:, :], out_offset=bass.IndirectOffsetOnAxis(ap=cur[:, b, i:i + 1], axis=0),
                                         in_=cur2[:, b, i:i + 1], in_offset=None, bounds_check=N_NODES - 1,
                                         oob_is_err=False).then_inc(s_scat[b], 16)

            def look_up(g, b, r, first):
                c = Chain(pool, s_mapq)
                c.start(g, 2, -g if first else -2)
                if not first:
                    hold(pool, s_gmap[b], r * 64)
                    c.inc(q.tensor_copy(gsrc[:, bass.ds(g * ET - 2 * ET, ET)], cur2[:, b, :]))
                c.inc(q.tensor_copy(cur[:, b, :], src_i[:, bass.ds(g * ET, ET)]))
                c.sync()
                fetch(slot_of_node[:, :], None, lambda i: cur2[:, b, i:i + 1], cur, b, s_gmap[b])

            def root(ready, count, out_sem, which, n, with_mean=False, nmr_second=False):
                per = 4 if with_mean else 2

                def body(g, b, r, first):
                    c = Chain(pool, out_sem)
                    c.start(g, per)
                    w, u = (b, 0) if which is None else (which, b)
                    at_ = 2 + b if nmr_second else b
                    hold(pool, ready, g * count + count)
                    c.link(q.tensor_scalar(rs[:, w, u, 0:n], mvs[:, w, u, 0:n, 1], LN_EPS, None, ALU.add))
                    c.inc(q.tensor_tensor(rs[:, w, u, 0:n], rs[:, w, u, 0:n], half[:, 0:n], ALU.pow))
                    if with_mean:
                        c.inc(q.tensor_scalar(nmr[:, at_, 0:n], mvs[:, w, u, 0:n, 0], -1.0, None, ALU.mult))
                        c.sync()
                        c.inc(q.tensor_tensor(nmr[:, at_, 0:n], nmr[:, at_, 0:n], rs[:, w, u, 0:n], ALU.mult))
                    c.finish()
                return body

            skewed(pool, [(root(s_agg[0], AGG[0], s_rc[0], 0, ET), 0), (scatter_slots, 0)])
            for b in range(2):
                pool.wait_ge(s_scat[b], (PAIRS + 1 - b) * 64)

            def dense_a(g, b, r, first):
                hold(pool, s_dl[b], r * 16 + 16)
                if not first:
                    hold(pool, s_A[1], g * DA2 - DA2)
                q.tensor_tensor(da[:, b], dx[:, b], bc(bias_bc[:], NT), ALU.add).then_inc(s_da_, 1)

            def dense_t(g, b, r, first):
                hold(pool, s_A[1], g * DA2 + DA2)
                if not first:
                    hold(pool, s_A[2], g * DA3 - DA3)
                q.tensor_tensor(dt_[:, b], dx1[:, b], bc(bet_bc[:], NT), ALU.add).then_inc(s_dtt, 1)

            pool.wait_ge(s_agg[0], EG * AGG[0])
            def dense_u(g, b, r, first):
                hold(pool, s_Bm[1], g + 1)
                if not first:
                    hold(pool, s_Bm[2], g * DB[2] - DB[2])
                q.tensor_tensor(du[:, b], dxm[:, b], dx2[:, b], ALU.add).then_inc(s_du, 1)

            skewed(pool, [(dense_u, 4), (root(s_A[0], DA1, s_rd[0], 0, NT), 1), (look_up, 0),
                          (root(s_A[2], DA3, s_rd[2], 2, NT, True, True), 2), (dense_a, 0),
                          (root(s_A[1], DA2, s_rd[1], 1, NT), 1), (dense_t, 1),
                          (root(s_Bm[2], DB[2], s_rd[3], 3, NT, True), 4)])
            for g in (EG - 2, EG - 1):
                b = g % 2
                pool.wait_ge(s_gmap[b], (PAIRS + 1 - b) * 64)
                q.tensor_copy(gsrc[:, g * ET:(g + 1) * ET], cur2[:, b, :]).then_inc(s_idx, 1)
            hold(pool, s_mapq, 2 * EG)

            def stored(k):
                for b in range(2):
                    hold(pool, s_cs[k][b], (PAIRS + 1 - b) * 16)
                    if k in s_ts:
                        hold(pool, s_ts[k][b], (PAIRS + 1 - b) * 16)

            stored(0)
            for b in range(2):
                pool.wait_ge(s_dx1[b], (PAIRS + 1 - b) * 16)
                pool.wait_ge(s_dx3[b], (PAIRS + 1 - b) * 32)
            for m in range(3):
                pool.wait_ge(s_dt2[m], EG * 16)
            def gather_src(k, table):
                def body(g, b, r, first):
                    c = Chain(pool, s_gi[k])
                    c.start(g, 1)
                    if not first:
                        hold(pool, s_ga[k][b], r * 64 + (16 - 16 * b))
                        hold(pool, s_tr[1] if k == 1 else s_m1, g - 1)
                    c.link(q.tensor_copy(cur[:, b, :], gsrc[:, bass.ds(back(g) * ET, ET)]))
                    if isinstance(g, int) and g == 0:
                        q.indirect_dma_start(out=bufa[:, 0, 2 * ET - 1, :], out_offset=None, in_=table,
                                             in_offset=bass.IndirectOffsetOnAxis(ap=gdst[:, J - 1:J], axis=0)
                                             ).then_inc(s_ga[k][0], 16)
                    fetch(table, None, lambda i: bufa[:, b, i, :], cur, b, s_ga[k][b])
                return body
            groups(pool, gather_src(1, t1[:, :]))
            for b in range(2):
                pool.wait_ge(s_ga[1][b], (PAIRS + 1 - b) * 64 + 16 - 16 * b)

            def x_beta(g, b, r, first):
                hold(pool, s_cl[1][b], r * CLD[1] + CLD[1])
                if not first:
                    hold(pool, s_z, g * Z1 - Z1)
                q.tensor_tensor(bufa[:, b, ET:2 * ET, :], bufa[:, b, 0:ET, :], bc(bet_bc[:], ET), ALU.add).then_inc(s_xb, 1)
            skewed(pool, [(root(s_y[1], 1 + 2 * ET, s_rc[1], 0, ET, True), 1),
                          (root(s_z, Z1, s_rc2, 1, ET, True, True), 2), (x_beta, 0)])
            for k in (2, 3, 4):
                stored(k - 1)

                def gather1(g, b, r, first, k=k):
                    c = Chain(pool, s_gi[k])
                    c.start(g, 1)
                    if not first:
                        hold(pool, s_ga[k][b], r * 64)
                        hold(pool, s_he[k], g - 1)
                    c.link(q.tensor_copy(cur[:, b, :], gsrc[:, bass.ds(g * ET, ET)]))
                    fetch(t2[k - 2][:, :], None, lambda i: gbuf[:, b, i, :], cur, b, s_ga[k][b])
                groups(pool, gather1)
                for b in range(2):
                    pool.wait_ge(s_ga[k][b], (PAIRS + 1 - b) * 64)
                if k == 4:
                    break

            pool.wait_ge(s_accp, 16)

            def scatter_acc(g, b, r, first):
                c = Chain(pool, s_asq)
                c.start(g, 1)
                if not first:
                    hold(pool, s_asc[b], r * 64)
                c.link(q.tensor_copy(cur[:, b, :], dscat[:, bass.ds(g * ET, ET)]))
                hold(pool, s_xo[4], g * ET + ET)
                for i in range(ET):
                    q.indirect_dma_start(out=acc[:, :], out_offset=bass.IndirectOffsetOnAxis(ap=cur[:, b, i:i + 1], axis=0),
                                         in_=bufb[:, b, i, :], in_offset=None, bounds_check=N_NODES - 1,
                                         oob_is_err=False).then_inc(s_asc[b], 16)
            skewed(pool, [(root(s_y[4], 2 + 2 * ET, s_rc[4], 0, ET), 0), (scatter_acc, 1)])
            for b in range(2):
                pool.wait_ge(s_asc[b], (PAIRS + 1 - b) * 64)
            stored(4)

            def add(g, b, r, more=True):
                c = Chain(pool, s_gi[5])
                if more:
                    c.start(g, 1, 3)
                    n = 1 - b
                    hold(pool, s_ga[5][n], (r + b) * 64 + (80 - 16 * n))
                    hold(pool, s_m1, g + 2)
                    c.link(q.tensor_copy(cur[:, n, :], gsrc[:, bass.ds(back(g) * ET - 3 * ET, ET)]))
                hold(pool, s_ma, g + 1)
                hold(pool, s_mv, g * MV + MV)
                for i in range(ET):
                    if not (isinstance(g, int) and g == 0 and i == 0):
                        hold(pool, s_add, g * 64 + i * 16)
                    q.indirect_dma_start(out=acc[:, :], out_offset=bass.IndirectOffsetOnAxis(ap=idx_add[:, b, i:i + 1], axis=0),
                                         in_=bufb[:, b, i, :], in_offset=None, compute_op=ALU.add).then_inc(s_add, 16)
                    if more:
                        q.indirect_dma_start(out=bufa[:, n, i, :], out_offset=None, in_=t3[:, :],
                                             in_offset=bass.IndirectOffsetOnAxis(ap=cur[:, n, i:i + 1], axis=0)
                                             ).then_inc(s_ga[5][n], 16)
            first_gathers = gather_src(5, t3[:, :])
            for g in range(3):
                first_gathers(g, g % 2, g // 2, g < 2)
            add(0, 0, 0)
            add(1, 1, 0)
            with pool.Fori(1, PAIRS - 1) as t:
                add(t * 2, 0, t)
                add(t * 2 + 1, 1, t)
            add(EG - 3, 0, PAIRS - 1, False)
            add(EG - 2, 1, PAIRS - 1, False)
            add(EG - 1, 0, PAIRS, False)
            skewed(pool, [(root(s_fv, 2 * NT, s_fr, None, NT, True), 0)], 4)

        @block.sync
        def _(sp):
            n_loads = [0]

            def load(to, of, slow=False):
                n_loads[0] += 1
                sp.dma_start(to, of, allow_slow_non_contiguous=slow).then_inc(s_ld, 16)
            load(src_i[:], src)
            load(dst_i[:], dst)
            load(lew[:], ew)
            load(w0[:, 0:D], w0t)
            load(wa_bc[:], w_attn.unsqueeze(0).broadcast_to([P, HD]))
            load(bias_bc[:], bias0.unsqueeze(0).broadcast_to([P, D]))
            load(wsrc[:], w_src)
            load(wdst[:], w_dst)
            load(attn_bc[:], attn.unsqueeze(0).broadcast_to([P, D]))
            load(wout[:], w_out)
            load(bo_bc[:], b_out.unsqueeze(0).broadcast_to([P, D]))
            load(gam_bc[:], gamma.unsqueeze(0).broadcast_to([P, D]))
            load(bet_bc[:], beta.unsqueeze(0).broadcast_to([P, D]))
            load(wext[:, :, 0:D], w2.rearrange("m k n -> k m n"))
            load(av[:, :, 0, :], a_src.unsqueeze(0).broadcast_to([P, 3, D]))
            load(av[:, :, 1, :], a_dst.unsqueeze(0).broadcast_to([P, 3, D]))
            load(w31a[:], w31[0:D, :])
            load(w31b[:], w31[D:2 * D, :])
            load(w31c[:], w31[2 * D:2 * D + 64, :])
            load(b31c[:], b31)
            load(w32s[:], w32.rearrange("(t p) n -> p t n", p=P))
            sp.wait_ge(s_pset, 9)
            load(brow[:, 0:3, 0:D], b2.unsqueeze(0).broadcast_to([3, 3, D]))
            load(brow[:, 3, 0:D], b_out.unsqueeze(0).broadcast_to([3, D]))
            load(brow[:, 4, 0:D], b32.unsqueeze(0).broadcast_to([3, D]))
            load(kfn[0:P - 1, 0:1], dst[1:P, 0:1], slow=True)
            load(kfn[1:P, 1:2], dst[0:P - 1, J - 1:J], slow=True)
            assert n_loads[0] == N_LOADS
            sp.dma_start(slot_of_node.rearrange("(p c) w -> p (c w)", p=P), node_i[:]).then_inc(s_slots, 16)
            sp.dma_start(acc[N_NODES:N_NODES + P, :], ident[:]).then_inc(s_accp, 16)

            def keep_dst(g, b, r, first):
                hold(sp, s_ga[0][b], r * 128 + 128)
                sp.dma_start(rows4(x0_dst, g), bufa[:, b, ET:2 * ET, :]).then_inc(s_xst[b], 16)
            groups(sp, keep_dst)

            def all_of(pair, per):
                for b in range(2):
                    hold(sp, pair[b], (PAIRS + 1 - b) * per)

            def slots(k):
                def load_(g, b, r, first):
                    if not first:
                        if k == 1:
                            hold(sp, s_xb, g - 1)
                            hold(sp, s_y[1], (g - 1) * (1 + 2 * ET))
                        else:
                            hold(sp, s_agg[k], (g - 1) * AGG[k])
                    if k < 2:
                        sp.dma_start(bufa[:, b, 0:ET, :], rows4([x0_dst, t1][k], g)).then_inc(s_slots_in[b], 16)
                    else:
                        sp.dma_start(gbuf[:, b, :, :], rows4(t2[k - 2], g)).then_inc(s_slots_in[b], 16)

                def load_state(g, b, r, first):
                    if not first:
                        hold(sp, *((s_y[4], (g - 1) * (2 + 2 * ET)) if k == 4 else (s_xo[k], g - 1)))
                    sp.dma_start(bufa[:, b, 0:ET, :], rows4(x2s[k - 2], g)).then_inc(s_states_in[b], 16)
                    if k == 4:
                        sp.dma_start(bufa[:, b, ET:2 * ET, :], rows4(x2s[0], g)).then_inc(s_states_in[b], 16)

                def store(g, b, r, first):
                    hold(sp, s_xo[k], g * XO[k] + XO[k])
                    sp.dma_start(rows4([t1, x2s[0], x2s[1], x2s[2], t3][k], g), bufb[:, b, 0:ET, :]).then_inc(
                        s_slots_out[b], 16)

                def store_rows(g, b, r, first):
                    hold(sp, s_cr[k], g * 4 + 4)
                    sp.dma_start(rows4(t2[k - 1], g), trow[:, b, 0:ET, :]).then_inc(s_rows_out[b], 16)
                skewed(sp, {0: [(load_, 0), (store, 2)],
                            1: [(load_, 0), (store, 4), (store_rows, 7)],
                            2: [(load_, 0), (load_state, 0), (store, 2), (store_rows, 4)],
                            3: [(load_, 0), (load_state, 0), (store, 2), (store_rows, 4)],
                            4: [(load_, 0), (load_state, 0), (store, 3)]}[k])

            sp.wait_ge(s_tr[0], EG)
            all_of(s_xst, 16)
            slots(0)
            all_of(s_cs[0], 16)
            sp.wait_ge(s_agg[0], EG * AGG[0])

            def dense_load(g, b, r, first):
                parts = TAIL if isinstance(g, int) and g == EG - 1 else P
                if not first:
                    hold(sp, s_da_, g - 1)
                sp.dma_start(dx[0:parts, b, :, :], node_rows(x, g, 0, parts)).then_inc(s_dl[b], 16)

            def parts_of(g):
                return TAIL if isinstance(g, int) and g == EG - 1 else P

            def store_x1(g, b, r, first):
                n = parts_of(g)
                hold(sp, s_A[1], g * DA2 + DA2)
                sp.dma_start(node_rows(t1, g, SLOTS, n), dx1[0:n, b, :, :]).then_inc(s_dx1[b], 16)

            def store_rows(m):
                def body(g, b, r, first):
                    n = parts_of(g)
                    hold(sp, s_dR[m], g * 3 + 3)
                    sp.dma_start(node_rows(t2[m], g, SLOTS, n), trow[0:n, m, :, :]).then_inc(s_dt2[m], 16)
                return body

            def store_x3(g, b, r, first):
                n = parts_of(g)
                hold(sp, s_dN, g * NT + NT)
                sp.dma_start(node_rows(t3, g, SLOTS, n), dx3[0:n, b, :, :]).then_inc(s_dx3[b], 16)
                sp.dma_start(node_rows(acc, g, 0, n), dx3[0:n, b, :, :]).then_inc(s_dx3[b], 16)

            skewed(sp, [(dense_load, 0), (store_rows(2), 4), (store_rows(0), 3), (store_x1, 1), (store_rows(1), 3),
                        (store_x3, 4)])

            def load_raw(k, table):
                def body(g, b, r, first):
                    if not first:
                        hold(sp, s_sp[k], g * (ET + 1) - (ET + 2))
                    sp.dma_start(gbuf[:, b, :, 0:D], rows4(table, back(g))).then_inc(s_slots_in[b], 16)
                return body
            groups(sp, load_raw(1, t1))
            sp.wait_ge(s_tr[1], EG)
            slots(1)
            for k in (2, 3, 4):
                all_of(s_cs[k - 1], 16)
                all_of(s_ts[k - 1], 16)
                sp.wait_ge(s_xo[k - 1], EG * XO[k - 1])
                sp.wait_ge(s_he[k], EG)
                slots(k)

            def edge_attr(g, b, r, first):
                if not first:
                    hold(sp, s_m1, g - 1)
                sp.dma_start(eab[:, b, :, :], rows4(ea, back(g))).then_inc(s_el[b], 16)
            all_of(s_cs[4], 16)
            skewed(sp, [(load_raw(5, t3), 0), (edge_attr, 0)])

            sp.wait_ge(s_add, EG * 64)
            sp.wait_ge(s_mp, EG)

            def final_load(g, b, r, first):
                n = parts_of(g)
                if not first:
                    hold(sp, s_fv2, g - 3)
                sp.dma_start(fx[0:n, b, :, :], node_rows(acc, g, 0, n)).then_inc(s_fl[b], 16)

            def final_store(g, b, r, first):
                n = parts_of(g)
                hold(sp, s_fv2, g + 1)
                sp.dma_start(node_rows(out, g, 0, n), fy[0:n, b, :, :]).then_inc(s_fs[b], 16)
            skewed(sp, [(final_load, 0), (final_store, 2)], 4)
            for b in range(4):
                sp.wait_ge(s_fs[b], (EG // 4 + (b == 0)) * 16)
            all_of(s_el, 16)


def kernel(**inputs):
    import numpy as np
    import concourse.bacc as bacc
    from concourse.bass_utils import run_bass_kernel_spmd

    def slots(name, fill):
        a = np.asarray(inputs[name])
        pad = np.full((SLOTS - N_EDGES,) + a.shape[1:], fill, a.dtype)
        return np.concatenate([a, pad])

    arrays = {
        "x": inputs["x"],
        "src": slots("src", 0).reshape(P, J),
        "dst": slots("dst", N_NODES).reshape(P, J),
        "ew": slots("edge_weight", 0).reshape(P, J),
        "ea": slots("edge_attr_64", 0),
        "w0t": np.asarray(inputs["L0_gnn_W_fc"]).T,
        "w_attn": inputs["L0_gnn_w_attn"],
        "bias0": inputs["L0_gnn_bias"],
        "w_src": inputs["L1_gnn_W_src"],
        "w_dst": inputs["L1_gnn_W_dst"],
        "attn": np.asarray(inputs["L1_gnn_attn"]).reshape(-1),
        "w_out": inputs["L1_gnn_W_out"],
        "b_out": inputs["L1_gnn_b_out"],
        "gamma": inputs["L1_gnn_gamma"],
        "beta": inputs["L1_gnn_beta"],
        "w2": inputs["L2_gnn_Ws"],
        "a_src": inputs["L2_gnn_att_src"],
        "a_dst": inputs["L2_gnn_att_dst"],
        "b2": inputs["L2_gnn_bias"],
        "w31": inputs["L3_gnn_W1"],
        "b31": np.asarray(inputs["L3_gnn_b1"]).reshape(2, P).T,
        "w32": inputs["L3_gnn_W2"],
        "b32": inputs["L3_gnn_b2"],
    }
    nc = bacc.Bacc("TRN2", target_bir_lowering=False, num_devices=1)
    fed, aps = {}, {}
    for name, a in arrays.items():
        a = np.ascontiguousarray(a)
        fed[f"in_{name}"] = a
        aps[name] = nc.dram_tensor(f"in_{name}", a.shape, mybir.dt.from_np(a.dtype), kind="ExternalInput").ap()
    aps["out"] = nc.dram_tensor("out_0", (N_NODES, D), fp32, kind="ExternalOutput").ap()
    build(nc, **aps)
    r = run_bass_kernel_spmd(nc, [fed], core_ids=[0])
    return r.results[0]["out_0"]
```
